# Optimizing a Trainium2 kernel written in Bass

```python
import numpy as np
import jax
import jax.numpy as jnp

def _softmax(x, axis=-1):
    return jax.nn.softmax(x, axis=axis)
def _gelu(x):
    return jax.nn.gelu(x, approximate=True)
def _silu(x):
    return jax.nn.silu(x)
def _sigmoid(x):
    return jax.nn.sigmoid(x)
def _layernorm(x, axis=-1, eps=1e-5):
    m = jnp.mean(x, axis=axis, keepdims=True)
    v = jnp.var(x, axis=axis, keepdims=True)
    return (x - m) / jnp.sqrt(v + eps)
def _scatter_add(tgt, idx, src, axis=0):
    return tgt.at[idx].add(src)
def _segment_sum(src, seg, n):
    return jax.ops.segment_sum(src, seg, n)

kernel_name = 'mk_conv_attn_hybrid_d2_conv_nchw256_237bdb'

def setup_inputs(seed: int = 0):
    np.random.seed(seed)
    _w = jnp.asarray
    def _rec_inputs():
        import jax
        import jax.numpy as jnp
        _gk = jax.random.key(seed)
        x = -0.0006537 + 1.001 * jax.random.normal(jax.random.fold_in(_gk, 1), (4, 256, 48, 48), jnp.float32)
        return x
    x = _rec_inputs()
    def _L0_conv_setup():
        import jax, jax.numpy as jnp
        import numpy as np
        DIM = 256
        NUM_HEADS = 8
        HEAD_DIM = DIM // NUM_HEADS
        SCALE = HEAD_DIM ** (-0.5)

        def _conv1x1(x, w, b):
            return jnp.einsum('bchw,oc->bohw', x, w[:, :, 0, 0]) + b[None, :, None, None]

        def _dwconv3x3(x, w, b):
            y = jax.lax.conv_general_dilated(x, w, window_strides=(1, 1), padding='SAME', feature_group_count=x.shape[1], dimension_numbers=('NCHW', 'OIHW', 'NCHW'))
            return y + b[None, :, None, None]
        key = jax.random.key(seed)
        ks = jax.random.split(key, 9)
        s = 0.05
        return {'x': jax.random.normal(ks[0], (4, DIM, 48, 48), jnp.float32), 'w_qk': jax.random.normal(ks[1], (2 * DIM, DIM, 1, 1), jnp.float32) * s, 'b_qk': jax.random.normal(ks[2], (2 * DIM,), jnp.float32) * s, 'w_v': jax.random.normal(ks[3], (DIM, DIM, 1, 1), jnp.float32) * s, 'b_v': jax.random.normal(ks[4], (DIM,), jnp.float32) * s, 'w_pe': jax.random.normal(ks[5], (DIM, 1, 3, 3), jnp.float32) * s, 'b_pe': jax.random.normal(ks[6], (DIM,), jnp.float32) * s, 'w_proj': jax.random.normal(ks[7], (DIM, DIM, 1, 1), jnp.float32) * s, 'b_proj': jax.random.normal(ks[8], (DIM,), jnp.float32) * s}
    _L0_conv_all = _L0_conv_setup()
    _L0_conv_in = {k: v for k, v in _L0_conv_all.items() if k in ('w_qk', 'b_qk', 'w_v', 'b_v', 'w_pe', 'b_pe', 'w_proj', 'b_proj', )}
    del _L0_conv_all

    def _L1_attn_setup():
        import jax, jax.numpy as jnp
        import numpy as np
        ATT_WIDTH = 24
        key = jax.random.key(seed)
        k1, k2 = jax.random.split(key)
        B, T, D = (4, 4096, 256)
        x = jax.random.normal(k1, (B, T, D), dtype=jnp.float32)
        K = jax.random.normal(k2, (D, D), dtype=jnp.float32) * (1.0 / np.sqrt(D))
        temperature = jnp.ones((1,), dtype=jnp.float32)
        bias = jnp.zeros((1,), dtype=jnp.float32)
        return {'x': x, 'K': K, 'temperature': temperature, 'bias': bias}
    _L1_attn_all = _L1_attn_setup()
    _L1_attn_in = {k: v for k, v in _L1_attn_all.items() if k in ('K', 'temperature', 'bias', )}
    del _L1_attn_all

    def _L1_ffn_setup():
        import math
        import jax, jax.numpy as jnp
        import numpy as np
        CAPACITY_FACTOR = 1.25
        key = jax.random.key(seed)
        ks = jax.random.split(key, 5)
        B, L, D, F, E = (8, 8192, 256, 1024, 8)
        h = jax.random.normal(ks[0], (B, L, D), dtype=jnp.float32)
        gate_w = jax.random.normal(ks[1], (D, E), dtype=jnp.float32) * 0.02
        gate_b = jnp.zeros((E,), dtype=jnp.float32)
        w1 = jax.random.normal(ks[2], (E, D, F), dtype=jnp.float32) * (1.0 / math.sqrt(D))
        b1 = jnp.zeros((E, F), dtype=jnp.float32)
        w2 = jax.random.normal(ks[3], (E, F, D), dtype=jnp.float32) * (1.0 / math.sqrt(F))
        b2 = jnp.zeros((E, D), dtype=jnp.float32)
        return {'h': h, 'gate_w': gate_w, 'gate_b': gate_b, 'w1': w1, 'b1': b1, 'w2': w2, 'b2': b2}
    _L1_ffn_all = _L1_ffn_setup()
    _L1_ffn_in = {k: v for k, v in _L1_ffn_all.items() if k in ('gate_w', 'gate_b', 'w1', 'b1', 'w2', 'b2', )}
    del _L1_ffn_all

    return {
        "x": x,
        "L0_conv_w_qk": _L0_conv_in["w_qk"],
        "L0_conv_b_qk": _L0_conv_in["b_qk"],
        "L0_conv_w_v": _L0_conv_in["w_v"],
        "L0_conv_b_v": _L0_conv_in["b_v"],
        "L0_conv_w_pe": _L0_conv_in["w_pe"],
        "L0_conv_b_pe": _L0_conv_in["b_pe"],
        "L0_conv_w_proj": _L0_conv_in["w_proj"],
        "L0_conv_b_proj": _L0_conv_in["b_proj"],
        "L1_attn_K": _L1_attn_in["K"],
        "L1_attn_temperature": _L1_attn_in["temperature"],
        "L1_attn_bias": _L1_attn_in["bias"],
        "L1_ffn_gate_w": _L1_ffn_in["gate_w"],
        "L1_ffn_gate_b": _L1_ffn_in["gate_b"],
        "L1_ffn_w1": _L1_ffn_in["w1"],
        "L1_ffn_b1": _L1_ffn_in["b1"],
        "L1_ffn_w2": _L1_ffn_in["w2"],
        "L1_ffn_b2": _L1_ffn_in["b2"],
    }

def reference(x, L0_conv_w_qk, L0_conv_b_qk, L0_conv_w_v, L0_conv_b_v, L0_conv_w_pe, L0_conv_b_pe, L0_conv_w_proj, L0_conv_b_proj, L1_attn_K, L1_attn_temperature, L1_attn_bias, L1_ffn_gate_w, L1_ffn_gate_b, L1_ffn_w1, L1_ffn_b1, L1_ffn_w2, L1_ffn_b2):
    import jax
    import jax.numpy as jnp
    def _L0_conv_ref(x, w_qk, b_qk, w_v, b_v, w_pe, b_pe, w_proj, b_proj):
        import jax, jax.numpy as jnp
        import numpy as np
        DIM = 256
        NUM_HEADS = 8
        HEAD_DIM = DIM // NUM_HEADS
        SCALE = HEAD_DIM ** (-0.5)

        def _conv1x1(x, w, b):
            return jnp.einsum('bchw,oc->bohw', x, w[:, :, 0, 0]) + b[None, :, None, None]

        def _dwconv3x3(x, w, b):
            y = jax.lax.conv_general_dilated(x, w, window_strides=(1, 1), padding='SAME', feature_group_count=x.shape[1], dimension_numbers=('NCHW', 'OIHW', 'NCHW'))
            return y + b[None, :, None, None]
        B, C, H, W = x.shape
        N = H * W
        h, d = (NUM_HEADS, HEAD_DIM)
        qk = _conv1x1(x, w_qk, b_qk).reshape(B, h, 2 * d, N)
        v4 = _conv1x1(x, w_v, b_v)
        pe = _dwconv3x3(v4, w_pe, b_pe)
        v = v4.reshape(B, h, d, N)
        q, k = (qk[:, :, :d, :], qk[:, :, d:, :])
        attn = jnp.einsum('bhdi,bhdj->bhij', q, k) * SCALE
        attn = jax.nn.softmax(attn, axis=-1)
        out = jnp.einsum('bhdj,bhij->bhdi', v, attn)
        out = out.reshape(B, C, H, W)
        return _conv1x1(out + pe, w_proj, b_proj)

    def _L1_attn_ref(x, K, temperature, bias):
        import jax, jax.numpy as jnp
        import numpy as np
        ATT_WIDTH = 24
        B, T, D = x.shape
        key = jnp.einsum('btd,de->bte', x, K)
        logits = jnp.einsum('btd,bsd->bts', key, x)
        logits = jax.nn.relu(logits + bias[0])
        i = jnp.arange(T)[:, None]
        j = jnp.arange(T)[None, :]
        lower = i - ATT_WIDTH // 2
        window = (lower <= j) & (j < lower + ATT_WIDTH)
        logits = logits - 10000.0 * (1.0 - window.astype(jnp.float32))
        logits = logits * temperature[0]
        scores = jax.nn.softmax(logits, axis=-1)
        return jnp.einsum('bts,bsd->btd', scores, x)

    def _L1_ffn_ref(h, gate_w, gate_b, w1, b1, w2, b2):
        import math
        import jax, jax.numpy as jnp
        import numpy as np
        CAPACITY_FACTOR = 1.25
        B, L, D = h.shape
        E = gate_w.shape[1]
        T = B * L
        C = max(1, math.ceil(CAPACITY_FACTOR * T / E))
        x = h.reshape(T, D)
        logits = x @ gate_w + gate_b
        probs = jax.nn.softmax(logits, axis=-1)
        idx = jnp.argmax(probs, axis=-1)
        prb = jnp.take_along_axis(probs, idx[:, None], axis=1)[:, 0]
        one_hot = jax.nn.one_hot(idx, E, dtype=jnp.float32)
        pos = (jnp.cumsum(one_hot, axis=0) * one_hot).sum(-1).astype(jnp.int32) - 1
        kept = pos < C
        pos_safe = jnp.where(kept, pos, C)
        buf = jnp.zeros((E, C, D), dtype=h.dtype).at[idx, pos_safe].set(x, mode='drop')
        hmid = jax.nn.relu(jnp.einsum('ecd,edf->ecf', buf, w1) + b1[:, None, :])
        ybuf = jnp.einsum('ecf,efd->ecd', hmid, w2) + b2[:, None, :]
        pos_g = jnp.minimum(pos, C - 1)
        y_tok = ybuf[idx, pos_g] * (prb * kept)[:, None]
        y = y_tok.reshape(B, L, D)
        y = jnp.nan_to_num(y, nan=0.0, posinf=10000.0, neginf=-10000.0)
        return y

    def _gn(v, G=32, eps=1e-5):
        B_, C_, H_, W_ = v.shape
        g = v.reshape(B_, G, C_ // G, H_, W_)
        m = jnp.mean(g, axis=(2, 3, 4), keepdims=True)
        s = jnp.var(g, axis=(2, 3, 4), keepdims=True)
        return ((g - m) / jnp.sqrt(s + eps)).reshape(v.shape)

    def _ln_c(v, eps=1e-6):
        m = jnp.mean(v, axis=1, keepdims=True)
        s = jnp.var(v, axis=1, keepdims=True)
        return (v - m) / jnp.sqrt(s + eps)

    def _ln_t(v, eps=1e-5):
        m = jnp.mean(v, axis=-1, keepdims=True)
        s = jnp.var(v, axis=-1, keepdims=True)
        return (v - m) / jnp.sqrt(s + eps)

    def _to_tokens(v):
        B_, C_, H_, W_ = v.shape
        return v.reshape(B_, C_, H_ * W_).transpose(0, 2, 1)
    def _from_tokens(t, like):
        B_, C_, H_, W_ = like.shape
        return t.transpose(0, 2, 1).reshape(B_, C_, H_, W_)

    x = x + _L0_conv_ref(_gn(x), L0_conv_w_qk, L0_conv_b_qk, L0_conv_w_v, L0_conv_b_v, L0_conv_w_pe, L0_conv_b_pe, L0_conv_w_proj, L0_conv_b_proj)
    t = _to_tokens(x)
    t = t + _L1_attn_ref(_ln_t(t), L1_attn_K, L1_attn_temperature, L1_attn_bias)
    t = t + _L1_ffn_ref(_ln_t(t), L1_ffn_gate_w, L1_ffn_gate_b, L1_ffn_w1, L1_ffn_b1, L1_ffn_w2, L1_ffn_b2)
    x = _from_tokens(t, x)
    return x


_drawn_inputs = setup_inputs


def setup_inputs(seed=0):
    import zlib

    import numpy as np

    out = dict(_drawn_inputs(seed))
    spreads = {'L1_ffn_gate_b': (0.0, 0.1), 'L1_ffn_b1': (0.0, 0.8), 'L1_ffn_b2': (0.0, 0.574)}
    factors = {'L0_conv_b_qk': 6.974}
    for name, (base, spread) in spreads.items():
        noise = np.random.default_rng([zlib.crc32(name.encode()), seed]).standard_normal(out[name].shape)
        drawn = base * np.exp(spread * noise) if base else spread * noise
        out[name] = jnp.asarray(drawn.astype(out[name].dtype))
    for name, factor in factors.items():
        out[name] = (out[name] * factor).astype(out[name].dtype)
    return out
```

```python
from contextlib import ExitStack

import concourse.bass as bass
from concourse import mybir

F32 = mybir.dt.float32
F32R = mybir.dt.float32r
BF16 = mybir.dt.bfloat16
I32 = mybir.dt.int32
U32 = mybir.dt.uint32
ALU = mybir.AluOpType
ACT = mybir.ActivationFunctionType
AX = mybir.AxisListType

P = 128
B, CH, IMG = 4, 256, 48
N = IMG * IMG
T = B * N
KT = CH // P
NT = N // P
TT = T // P
W = 384
NC = N // W
SUB = W // P
HEADS, HD = 8, 32
EXPERTS = 8
HG = P // HD
SCALE = HD ** -0.5
MAX_SCORE = 30.0
GN_GROUP = 8
GN_EPS, LN_EPS = 1e-5, 1e-5
WINDOW = 24
OUTSIDE = 10000.0
UNDERFLOW = 110.0
GONE = -1e30
BG = B * KT
BN6, BN2 = 6, 2


class Steps:

    def __init__(self, engine, sem, base=0):
        self.engine, self.sem, self.base, self.n = engine, sem, base, 0

    def then(self, instruction):
        self.n += 1
        instruction.then_inc(self.sem, 1)
        self.engine.wait_ge(self.sem, self.base + self.n)


def conv_inputs(nc, x, w_qkv, b_qkv, bv_row, group_mean, head_sum, eye, qh, ql, kh, kl, v_img, v_tok, small_scores):
    with ExitStack() as ctx:
        def sb(name, shape, dt=F32):
            return ctx.enter_context(nc.sbuf_tensor(name, shape, dt))

        def sem(name):
            return ctx.enter_context(nc.semaphore(name))

        x_sb = sb("cx", [P, KT, N])
        xn = sb("cxn", [P, KT, N])
        wq = sb("cw", [P, KT, 3 * CH])
        bq = sb("cb", [P, 3 * KT])
        bv = sb("cbv", [P, CH])
        gm = sb("cgm", [P, P])
        stats = sb("cstats", [P, KT, NC, BN6])
        mv = sb("cmv", [P, KT, BN2])
        dev = sb("cdev", [P, KT])
        dev2 = sb("cdev2", [P, KT])
        mean = sb("cmean", [P, KT])
        mhalf = sb("cmhalf", [P, KT])
        rstd = sb("crstd", [P, KT])
        veps = sb("cveps", [P, KT])
        qkf = sb("cqkf", [P, 2, 2 * KT, W])
        hi = sb("chi", [P, 2, 2 * KT, W], F32R)
        lo = sb("clo", [P, 2, 2 * KT, W], F32R)
        vi = sb("cvi", [P, 2, KT, W])
        vt = sb("cvt", [P, 2, SUB, CH])
        heads = sb("cheads", [P, P])
        heads16 = sb("cheads16", [P, P], BF16)
        ident = sb("cident", [P, P])
        squares = sb("csquares", [P, 2, 2 * KT, W], BF16)
        norms = sb("cnorms", [P, 2 * KT, B * NC])
        peaks = sb("cpeaks", [P, 2 * KT, B])
        bound = sb("cbound", [P, KT, B])
        worst = sb("cworst", [P, 1])
        worst_all = sb("cworst_all", [1, 1])
        NB_IMG, NB_TOK, NB_NORM = 3, 2, 2
        ps_img = [ctx.enter_context(nc.psum_tensor(f"cpi{i}", [P, 512], F32)) for i in range(NB_IMG)]
        ps_tok = [ctx.enter_context(nc.psum_tensor(f"cpt{i}", [P, 512], F32)) for i in range(NB_TOK)]
        ps_norm = [ctx.enter_context(nc.psum_tensor(f"cpn{i}", [P, 512], F32)) for i in range(NB_NORM)]
        ps_st = ctx.enter_context(nc.psum_tensor("cps", [P, 512], F32))

        consts_in = sem("c_consts_in")
        x_in = sem("c_x_in")
        xn_done = sem("c_xn_done")
        aggr_done = sem("c_aggr_done")
        mean_mm = sem("c_mean_mm")
        dev_done = sem("c_dev_done")
        var_mm = sem("c_var_mm")
        veps_done = sem("c_veps_done")
        rstd_done = sem("c_rstd_done")
        mhalf_done = sem("c_mhalf_done")
        dve_step = sem("c_dve_step")
        img_mm = sem("c_img_mm")
        img_out = sem("c_img_out")
        tok_mm = sem("c_tok_mm")
        tok_out = sem("c_tok_out")
        split_done = sem("c_split_done")
        heads_done = sem("c_heads_done")
        squares_done = sem("c_squares_done")
        norm_mm = sem("c_norm_mm")
        norm_done = sem("c_norm_done")
        worst_done = sem("c_worst_done")
        worst_mm = sem("c_worst_mm")
        stored = [sem(f"c_stored{i}") for i in range(2)]
        block = ctx.enter_context(nc.Block())
        MI, MQK = 3 * KT, 2 * KT
        SLOT_STORES = 6 * 16
        STEPS = 4 + NC

        @block.sync
        def _(sp):
            sp.dma_start(wq[:], w_qkv.rearrange("(k p) n -> p k n", p=P)).then_inc(consts_in, 16)
            sp.dma_start(bq[:], b_qkv[:]).then_inc(consts_in, 16)
            sp.dma_start(bv[:], bv_row.partition_broadcast(P)).then_inc(consts_in, 16)
            sp.dma_start(gm[:], group_mean[:]).then_inc(consts_in, 16)
            sp.dma_start(heads[:], head_sum[:]).then_inc(consts_in, 16)
            sp.dma_start(ident[:], eye[:]).then_inc(consts_in, 16)

            def load_x(b):
                sp.dma_start(x_sb[:], x[bass.ds(b, 1)].rearrange("a (k p) n -> p (a k) n", p=P)).then_inc(x_in, 16)

            def store_chunks(b):
                for c in range(NC):
                    s = c % 2
                    cols = slice(c * W, (c + 1) * W)
                    sp.wait_ge(tok_out, 1 + (b * NC + c) * SUB + SUB)
                    sp.dma_start(v_tok[bass.ds(b, 1), c * W:(c + 1) * W, :].rearrange("a (j p) n -> p (a j) n", p=P),
                                 vt[:, s]).then_inc(stored[s], 16)
                    sp.wait_ge(split_done, 1 + b * NC + c + 1)
                    for dram, part, m in ((qh, hi, 0), (kh, hi, KT), (ql, lo, 0), (kl, lo, KT)):
                        if m == 0:
                            to = dram.rearrange("(g c) p n -> g c p n", c=NC)[bass.ds(b * KT, KT), c]
                        else:
                            to = dram[bass.ds(b * KT, KT), :, cols]
                        sp.dma_start(to.rearrange("k p n -> p k n"),
                                     part[:, s, m:m + KT, :].bitcast(F32)).then_inc(stored[s], 16)
                    sp.wait_ge(img_out, 1 + (b * NC + c) * MI + MI)
                    sp.dma_start(v_img[bass.ds(b * KT, KT), :, cols].rearrange("k p n -> p k n"),
                                 vi[:, s]).then_inc(stored[s], 16)

            for counter in stored:
                sp.sem_inc(counter, 1)
            load_x(0)
            with sp.Fori(0, B - 1) as b:
                sp.wait_ge(xn_done, b + 1)
                load_x(b + 1)
                store_chunks(b)
            store_chunks(B - 1)
            for s in range(2):
                sp.wait_ge(stored[s], 1 + B * (NC // 2) * SLOT_STORES)

        @block.vector
        def _(dve):
            for counter in (veps_done, tok_out, split_done, norm_done):
                dve.sem_inc(counter, 1)
            dve.sem_inc(norm_done, NB_NORM - 1)
            dve.wait_ge(consts_in, 6 * 16)
            nc.vector.tensor_copy(heads16[:], heads[:]).then_inc(heads_done, 1)
            with dve.Fori(0, B) as b:
                st = Steps(dve, dve_step, b * STEPS)
                dve.wait_ge(x_in, b * 16 + 16)
                for k in range(KT):
                    for c in range(NC):
                        i = nc.vector.bn_stats(stats[:, k, c, :], x_sb[:, k, c * W:(c + 1) * W])
                st.then(i)
                nc.vector.memset(dev[:], 0.0)
                for k in range(KT):
                    i = nc.vector.bn_aggr(mv[:, k, :], stats[:, k].rearrange("p c s -> p (c s)"))
                i.then_inc(aggr_done, 1)
                dve.wait_ge(mean_mm, b + 1)
                dve.wait_ge(aggr_done, b + 1)
                st.then(nc.vector.tensor_copy(mean[:], ps_st[:, 0:KT]))
                st.then(nc.vector.tensor_tensor(dev[:], mv[:, :, 0], mean[:], ALU.subtract))
                st.then(nc.vector.tensor_tensor(dev2[:], dev[:], dev[:], ALU.mult))
                nc.vector.tensor_tensor(dev2[:], dev2[:], mv[:, :, 1], ALU.add).then_inc(dev_done, 1)
                dve.wait_ge(var_mm, b + 1)
                nc.vector.tensor_scalar(veps[:], ps_st[:, 8:8 + KT], GN_EPS, None, ALU.add).then_inc(veps_done, 1)
                dve.wait_ge(rstd_done, b + 1)
                dve.wait_ge(img_mm, 1 + b * MI * NC)
                dve.wait_ge(tok_mm, 1 + b * NC * SUB)
                for k in range(KT):
                    i = nc.vector.tensor_scalar(xn[:, k, :], x_sb[:, k, :], mean[:, k:k + 1], rstd[:, k:k + 1],
                                                ALU.subtract, ALU.mult)
                i.then_inc(xn_done, 1)
                for c in range(NC):
                    s = c % 2
                    if c < 2:
                        dve.wait_ge(stored[s], 1 + b * (NC // 2) * SLOT_STORES)
                    else:
                        dve.wait_ge(stored[s], 1 + (b * (NC // 2) + c // 2) * SLOT_STORES)
                    for j in range(SUB):
                        dve.wait_ge(tok_mm, 1 + (b * NC + c) * SUB + j + 1)
                        nc.vector.tensor_tensor(vt[:, s, j, :], ps_tok[(c * SUB + j) % NB_TOK][:, 0:CH], bv[:],
                                                ALU.add).then_inc(tok_out, 1)
                    dve.wait_ge(img_out, 1 + (b * NC + c) * MI + MQK)
                    st.then(nc.vector.tensor_copy(hi[:, s], qkf[:, s]))
                    nc.vector.tensor_tensor(lo[:, s], qkf[:, s], hi[:, s].bitcast(F32), ALU.subtract).then_inc(split_done, 1)
                    for m in range(MQK):
                        dve.wait_ge(norm_mm, 1 + MQK + (b * NC + c) * MQK + m + 1)
                        nc.vector.reduce_max(norms[:, m, bass.ds(b * NC + c, 1)], ps_norm[m % NB_NORM][:, 0:W],
                                             AX.X).then_inc(norm_done, 1)
                assert st.n == STEPS, st.n
            st = Steps(dve, dve_step, B * STEPS)
            dve.wait_ge(norm_done, NB_NORM + B * NC * MQK)
            st.then(nc.vector.reduce_max(peaks[:], norms[:].rearrange("p m (b c) -> p m b c", b=B), AX.X))
            st.then(nc.vector.tensor_tensor(bound[:], peaks[:, 0:KT], peaks[:, KT:MQK], ALU.mult))
            nc.vector.reduce_max(worst[:], bound[:], AX.XY).then_inc(worst_done, 1)
            dve.wait_ge(worst_mm, 1)
            st.then(nc.vector.reduce_max(worst_all[:], ps_st[0:1, 128:256], AX.X))
            st.then(nc.vector.tensor_scalar(small_scores[:], worst_all[:], 0.98 * (MAX_SCORE / SCALE) ** 2, None, ALU.is_lt))

        @block.gpsimd
        def _(pool):
            nc.gpsimd.memset(mhalf[:], -0.5).then_inc(mhalf_done, 1)
            pool.wait_ge(mhalf_done, 1)
            with pool.Fori(0, B) as b:
                pool.wait_ge(veps_done, 1 + b + 1)
                nc.gpsimd.tensor_tensor(rstd[:], veps[:], mhalf[:], ALU.pow).then_inc(rstd_done, 1)

        @block.scalar
        def _(act):
            act.sem_inc(img_out, 1)
            with act.Fori(0, B) as b:
                for c in range(NC):
                    s = c % 2
                    act.wait_ge(stored[s], 1 + (b * (NC // 2) + c // 2) * SLOT_STORES)
                    act.wait_ge(split_done, 1 + b * NC + c - 1) if c else act.wait_ge(split_done, 1 + b * NC)
                    for m in range(MI):
                        act.wait_ge(img_mm, 1 + (b * NC + c) * MI + m + 1)
                        dst = qkf[:, s, m, :] if m < MQK else vi[:, s, m - MQK, :]
                        src = ps_img[(c * MI + m) % NB_IMG][:, 0:W]
                        if m == 0:
                            act.wait_ge(norm_mm, 1 + (b * NC + c) * MQK)
                        if m < MQK:
                            nc.scalar.activation(squares[:, s, m, :], src, ACT.Square, bias=bq[:, m:m + 1]
                                                 ).then_inc(squares_done, 1)
                        nc.scalar.activation(dst, src, ACT.Identity, bias=bq[:, m:m + 1]).then_inc(img_out, 1)

        @block.tensor
        def _(pe):
            for counter in (img_mm, tok_mm, norm_mm):
                pe.sem_inc(counter, 1)
            pe.sem_inc(norm_mm, MQK)
            pe.wait_ge(consts_in, 6 * 16)
            pe.wait_ge(heads_done, 1)
            with pe.Fori(0, B) as b:
                pe.wait_ge(aggr_done, b + 1)
                pe.wait_ge(veps_done, 1 + b)
                nc.tensor.matmul(ps_st[:, 0:KT], gm[:], mv[:, :, 0], start=True, stop=True).then_inc(mean_mm, 1)
                pe.wait_ge(dev_done, b + 1)
                nc.tensor.matmul(ps_st[:, 8:8 + KT], gm[:], dev2[:], start=True, stop=True).then_inc(var_mm, 1)
                pe.wait_ge(xn_done, b + 1)
                for c in range(NC):
                    cols = slice(c * W, (c + 1) * W)
                    for m in range(MI):
                        u = c * MI + m
                        if u >= NB_IMG:
                            pe.wait_ge(img_out, 1 + b * NC * MI + u - NB_IMG + 1)
                        else:
                            pe.wait_ge(img_out, 1 + b * NC * MI)
                        for k in range(KT):
                            i = nc.tensor.matmul(ps_img[u % NB_IMG][:, 0:W], wq[:, k, m * P:(m + 1) * P], xn[:, k, cols],
                                                 start=(k == 0), stop=(k == KT - 1))
                        i.then_inc(img_mm, 1)
                        if m % 2:
                            j = m // 2
                            u = c * SUB + j
                            if u >= NB_TOK:
                                pe.wait_ge(tok_out, 1 + b * NC * SUB + u - NB_TOK + 1)
                            else:
                                pe.wait_ge(tok_out, 1 + b * NC * SUB)
                            for k in range(KT):
                                i = nc.tensor.matmul(ps_tok[u % NB_TOK][:, 0:CH], xn[:, k, c * W + j * P:c * W + (j + 1) * P],
                                                     wq[:, k, 2 * CH:3 * CH], start=(k == 0), stop=(k == KT - 1))
                            i.then_inc(tok_mm, 1)
                    for m in range(MQK):
                        u = (b * NC + c) * MQK + m
                        pe.wait_ge(squares_done, u + 1)
                        pe.wait_ge(norm_done, 1 + u)
                        nc.tensor.matmul(ps_norm[m % NB_NORM][:, 0:W], heads16[:], squares[:, c % 2, m, :],
                                         start=True, stop=True).then_inc(norm_mm, 1)
            pe.wait_ge(worst_done, 1)
            nc.tensor.transpose(ps_st[0:1, 128:256], worst[:], ident[:]).then_inc(worst_mm, 1)


def conv_attention(nc, qh, ql, kh, kl, v_img, v_tok, w_pe, b_pe, eye, small_scores, attn, pe_img):
    with ExitStack() as ctx:
        def sb(name, shape, dt=F32):
            return ctx.enter_context(nc.sbuf_tensor(name, shape, dt))

        def sem(name):
            return ctx.enter_context(nc.semaphore(name))

        G3 = NT // SUB
        NP_SLOTS = 2 * HG
        MAXES = HG * SUB * 2
        UNITS = G3 * HG
        ADDS = (G3 - 1) * HG
        CHUNKS = BG * NC
        k_sb = sb("ak", [P, KT, HG, N], F32R)
        v_sb = sb("av", [P, KT, NT, P])
        q_sb = sb("aq", [P, 2, HG, W], F32R)
        probs = sb("aprobs", [P, NP_SLOTS, SUB, W])
        sums = sb("asums", [P, HG, SUB, W])
        mx = sb("amx", [P, 2, HG * SUB])
        top = sb("atop", [P, HG * SUB])
        diag = sb("adiag", [P, HG, W])
        ident = sb("aident", [P, P])
        minus = sb("aminus", [P, P])
        ones = sb("aones", [P, HD])
        rden = sb("arden", [P, W])
        o_sb = sb("ao", [P, 2, W])
        vc = sb("avc", [P, IMG, IMG])
        tap = sb("atap", [P, IMG, IMG])
        conv = sb("aconv", [P, IMG, IMG])
        wpe = sb("awpe", [P, KT, 9])
        bpe = sb("abpe", [P, KT])
        ps_s = [ctx.enter_context(nc.psum_tensor(f"ass{i}", [P, SUB, 512], F32)) for i in range(2)]
        ps_o = ctx.enter_context(nc.psum_tensor("aso", [P, 512], F32))
        ps_d = ctx.enter_context(nc.psum_tensor("asd", [P, 512], F32))

        consts_in = sem("a_consts_in")
        taps_in = sem("a_taps_in")
        consts_set = sem("a_consts_set")
        kv_in = [sem(f"a_kv_in{g}") for g in range(KT)]
        q_in = [sem(f"a_q_in{i}") for i in range(2)]
        max_mm = sem("a_max_mm")
        max_done = sem("a_max_done")
        diag_done = sem("a_diag_done")
        dve_step = sem("a_dve_step")
        score_mm = sem("a_score_mm")
        exp_done = sem("a_exp_done")
        add_done = sem("a_add_done")
        pv_done = sem("a_pv_done")
        den_mm = sem("a_den_mm")
        out_done = sem("a_out_done")
        o_stored = [sem(f"a_o_stored{i}") for i in range(2)]
        img_in = sem("a_img_in")
        pool_step = sem("a_pool_step")
        conv_stored = sem("a_conv_stored")
        block = ctx.enter_context(nc.Block())

        @block.sync
        def _(sp):
            for counter in o_stored:
                sp.sem_inc(counter, 1)
            sp.dma_start(ident[:], eye[:]).then_inc(consts_in, 16)

            def load_kv(b, g):
                for r, part in enumerate((kh, kl, kh, kl)):
                    sp.dma_start(k_sb[r * HD:(r + 1) * HD, g].bitcast(F32),
                                 part[bass.ds(b * KT + g, 1)].rearrange("a (h d) n -> d (a h) n", d=HD)).then_inc(kv_in[g], 16)
                sp.dma_start(v_sb[:, g], v_tok[bass.ds(b, 1), :, g * P:(g + 1) * P].rearrange("a (t p) c -> p (a t) c", p=P)
                             ).then_inc(kv_in[g], 16)

            def load_q(n, i):
                for r, part in enumerate((qh, qh, ql, ql)):
                    sp.dma_start(q_sb[r * HD:(r + 1) * HD, i].bitcast(F32),
                                 part[bass.ds(n, 1)].rearrange("a (h d) n -> d (a h) n", d=HD)).then_inc(q_in[i], 16)

            def store_out(n, i):
                sp.wait_ge(out_done, 1 + n + 1)
                sp.dma_start(attn[bass.ds(n, 1)].rearrange("a p n -> p (a n)"), o_sb[:, i]).then_inc(o_stored[i], 16)

            def one_batch(b, last):
                for c in range(KT * NC):
                    n = b * KT * NC + c
                    if not (last and c == KT * NC - 1):
                        load_q(n + 1, (c + 1) % 2)
                    store_out(n, c % 2)
                    if c % NC == NC - 1 and not last:
                        load_kv(b + 1, c // NC)

            load_kv(0, 0)
            load_q(0, 0)
            load_kv(0, 1)
            with sp.Fori(0, B - 1) as b:
                one_batch(b, False)
            one_batch(B - 1, True)
            for i in range(2):
                sp.wait_ge(o_stored[i], 1 + CHUNKS // 2 * 16)

        @block.gpsimd
        def _(pool):
            pool.dma_start(wpe[:], w_pe.rearrange("(k p) t -> p k t", p=P)).then_inc(taps_in, 16)
            pool.dma_start(bpe[:], b_pe[:]).then_inc(taps_in, 16)
            pool.wait_ge(taps_in, 32)
            nc.gpsimd.memset(minus[:], -1.0).then_inc(consts_set, 1)
            nc.gpsimd.memset(ones[:], 1.0).then_inc(consts_set, 1)
            with pool.Fori(0, B) as b:
                for g in range(KT):
                    st = Steps(pool, pool_step, (b * KT + g) * 18)
                    pool.wait_ge(img_in, (b * KT + g + 1) * 16)
                    order = [4, 0, 1, 2, 3, 5, 6, 7, 8]
                    for t in order:
                        dy, dx = t // 3 - 1, t % 3 - 1
                        y0, y1 = max(0, -dy), IMG - max(0, dy)
                        x0, x1 = max(0, -dx), IMG - max(0, dx)
                        tap_w = wpe[:, g, t:t + 1].to_broadcast([P, N])
                        if t == 4:
                            pool.wait_ge(conv_stored, 1 + (b * KT + g) * 16)
                            st.then(nc.gpsimd.tensor_tensor(conv[:].rearrange("p y x -> p (y x)"), vc[:].rearrange("p y x -> p (y x)"),
                                                            tap_w, ALU.mult))
                            st.then(nc.gpsimd.tensor_tensor(conv[:].rearrange("p y x -> p (y x)"), conv[:].rearrange("p y x -> p (y x)"),
                                                            bpe[:, g:g + 1].to_broadcast([P, N]), ALU.add))
                        else:
                            st.then(nc.gpsimd.tensor_tensor(tap[:].rearrange("p y x -> p (y x)"), vc[:].rearrange("p y x -> p (y x)"),
                                                            tap_w, ALU.mult))
                            st.then(nc.gpsimd.tensor_tensor(conv[:, y0:y1, x0:x1], conv[:, y0:y1, x0:x1],
                                                            tap[:, y0 + dy:y1 + dy, x0 + dx:x1 + dx], ALU.add))
                    assert st.n == 18

        @block.vector
        def _(dve):
            for counter in (max_done, add_done, out_done):
                dve.sem_inc(counter, 1)
            dve.sem_inc(add_done, HG)
            dve.wait_ge(consts_in, 16)
            STEPS = {True: 2, False: 1}

            def attend(shifted):
                with dve.Fori(0, BG * NC // 2) as pair:
                    for i in range(2):
                        n = pair * 2 + i
                        st = Steps(dve, dve_step, n * STEPS[shifted])
                        if shifted:
                            for u in range(MAXES):
                                dve.wait_ge(max_mm, 1 + n * MAXES + u + 1)
                                nc.vector.reduce_max(mx[:, u % 2, u // 2:u // 2 + 1], ps_s[u % 2][:, :, 0:W], AX.XY).then_inc(max_done, 1)
                            dve.wait_ge(max_done, 1 + n * MAXES + MAXES)
                            st.then(nc.vector.tensor_tensor(top[:], mx[:, 0], mx[:, 1], ALU.max))
                            for h in range(HG):
                                for j in range(SUB):
                                    last = nc.vector.tensor_scalar(diag[:, h, j * P:(j + 1) * P], ident[:], top[:, h * SUB + j:h * SUB + j + 1],
                                                                   None, ALU.mult)
                            last.then_inc(diag_done, 1)
                        for g3 in range(1, G3):
                            for h in range(HG):
                                u = g3 * HG + h
                                dve.wait_ge(exp_done, 3 + n * UNITS + u + 1)
                                if g3 == 1:
                                    first = probs[:, h]
                                    dve.wait_ge(den_mm, 1 + n)
                                else:
                                    first = sums[:, h]
                                    dve.wait_ge(add_done, 1 + HG + n * ADDS + (g3 - 2) * HG + h + 1)
                                nc.vector.tensor_tensor(sums[:, h], first, probs[:, u % NP_SLOTS], ALU.add).then_inc(add_done, 1)
                        dve.wait_ge(den_mm, 1 + n + 1)
                        st.then(nc.vector.reciprocal(rden[:], ps_d[:, 0:W]))
                        dve.wait_ge(pv_done, 3 + n * G3 + G3)
                        dve.wait_ge(o_stored[i], 1 + pair * 16)
                        nc.vector.tensor_tensor(o_sb[:, i], ps_o[:, 0:W], rden[:], ALU.mult).then_inc(out_done, 1)
                        assert st.n == STEPS[shifted]

            small = dve.value_load(small_scores[0:1, 0:1], min_val=0, max_val=1)
            with dve.If(small):
                attend(False)
            with dve.Else():
                attend(True)

        @block.scalar
        def _(act):
            act.sem_inc(exp_done, 3)
            act.sem_inc(conv_stored, 1)
            FREED = {0: 0, 1: 4, 2: 8, 3: 8, 4: 12, 5: 16}
            with act.Fori(0, B) as b:
                for g in range(KT):
                    act.dma_start(vc[:].rearrange("p y x -> p (y x)"),
                                  v_img[bass.ds(b * KT + g, 1)].rearrange("a p n -> p (a n)")).then_inc(img_in, 16)
                    with act.Fori(0, NC // 2) as cp:
                        for i in range(2):
                            n = (b * KT + g) * NC + cp * 2 + i
                            for u in range(UNITS):
                                if u % HG == 0:
                                    act.wait_ge(pv_done, 1 + n * G3 + u // HG + 1)
                                    act.wait_ge(add_done, 1 + n * ADDS + FREED[u // HG])
                                act.wait_ge(score_mm, 1 + n * UNITS + u + 1)
                                nc.scalar.activation(probs[:, u % NP_SLOTS], ps_s[u % 2][:, :, 0:W], ACT.Exp, scale=SCALE
                                                     ).then_inc(exp_done, 1)
                    act.wait_ge(pool_step, (b * KT + g + 1) * 18)
                    act.dma_start(pe_img[bass.ds(b * KT + g, 1)].rearrange("a p n -> p (a n)"),
                                  conv[:].rearrange("p y x -> p (y x)")).then_inc(conv_stored, 16)
            act.wait_ge(conv_stored, 1 + BG * 16)

        @block.tensor
        def _(pe):
            for counter in (max_mm, score_mm, pv_done, den_mm):
                pe.sem_inc(counter, 1)
            pe.sem_inc(pv_done, 2)
            pe.wait_ge(consts_set, 2)
            def attend(shifted):
                with pe.Fori(0, B) as b:
                    for g in range(KT):
                        with pe.Fori(0, NC // 2) as cp:
                            for i in range(2):
                                n = (b * KT + g) * NC + cp * 2 + i
                                pe.wait_ge(kv_in[g], (b + 1) * 5 * 16)
                                pe.wait_ge(q_in[i], ((b * KT + g) * (NC // 2) + cp + 1) * 4 * 16)
                                if shifted:
                                    for u in range(MAXES):
                                        h, j, half = u // (2 * SUB), u // 2 % SUB, u % 2
                                        if u < 2:
                                            pe.wait_ge(exp_done, 3 + n * UNITS)
                                        else:
                                            pe.wait_ge(max_done, 1 + n * MAXES + u - 1)
                                        for a in range(SUB):
                                            key = (half * SUB + a) * W
                                            last = nc.tensor.matmul(ps_s[u % 2][:, a, 0:W], q_sb[:, i, h, j * P:(j + 1) * P],
                                                                    k_sb[:, g, h, key:key + W], start=True, stop=True)
                                        last.then_inc(max_mm, 1)
                                    pe.wait_ge(max_done, 1 + n * MAXES + MAXES)
                                    pe.wait_ge(diag_done, n + 1)

                                def scores(u):
                                    g3, h = u // HG, u % HG
                                    if u >= 2 or not shifted:
                                        pe.wait_ge(exp_done, 1 + n * UNITS + u + 1)
                                    for a in range(SUB):
                                        key = (g3 * SUB + a) * P
                                        last = nc.tensor.matmul(ps_s[u % 2][:, a, 0:W], k_sb[:, g, h, key:key + P], q_sb[:, i, h, :],
                                                         start=True, stop=not shifted)
                                        if shifted:
                                            last = nc.tensor.matmul(ps_s[u % 2][:, a, 0:W], minus[:], diag[:, h, :],
                                                                    start=False, stop=True)
                                    last.then_inc(score_mm, 1)

                                def values(g3, a):
                                    kt = g3 * SUB + a
                                    for h in range(HG):
                                        u = g3 * HG + h
                                        if a == 0:
                                            pe.wait_ge(exp_done, 3 + n * UNITS + u + 1)
                                        if kt == 0 and h == 0:
                                            pe.wait_ge(out_done, 1 + n)
                                        last = nc.tensor.matmul(ps_o[h * HD:(h + 1) * HD, 0:W], v_sb[:, g, kt, h * HD:(h + 1) * HD],
                                                                probs[:, u % NP_SLOTS, a, :], start=(kt == 0), stop=(kt == NT - 1))
                                    if a == SUB - 1:
                                        last.then_inc(pv_done, 1)

                                for h in range(HG):
                                    scores(h)
                                for g3 in range(1, G3):
                                    for h in range(HG):
                                        scores(g3 * HG + h)
                                        if h < SUB:
                                            values(g3 - 1, h)
                                for a in range(SUB):
                                    values(G3 - 1, a)
                                pe.wait_ge(add_done, 1 + HG + n * ADDS + ADDS)
                                for a in range(SUB):
                                    for h in range(HG):
                                        last = nc.tensor.matmul(ps_d[h * HD:(h + 1) * HD, 0:W], ones[:], sums[:, h, a, :],
                                                                start=(a == 0), stop=(a == SUB - 1))
                                last.then_inc(den_mm, 1)

            small = pe.value_load(small_scores[0:1, 0:1], min_val=0, max_val=1)
            with pe.If(small):
                attend(False)
            with pe.Else():
                attend(True)


def project_and_norm(nc, attn, pe_img, x, w_proj, bp_row, eye, w_key, temperature, bias, near_only, t1, xn_tok, xn_ch, key_ch):
    with ExitStack() as ctx:
        def sb(name, shape, dt=F32):
            return ctx.enter_context(nc.sbuf_tensor(name, shape, dt))

        def sem(name):
            return ctx.enter_context(nc.semaphore(name))

        CHUNKS = B * NC
        a_in = sb("pa", [P, 2, KT, W])
        c_in = sb("pc", [P, 2, KT, W])
        x_in = sb("px", [P, 2, KT, W])
        both = sb("pboth", [P, 2, KT, W])
        wp = sb("pwp", [P, KT, CH])
        wk = sb("pwk", [P, KT, CH])
        bp = sb("pbp", [P, CH])
        ident = sb("pident", [P, P])
        tok = sb("ptok", [P, 2, SUB, CH])
        xn = sb("pxn", [P, 2, SUB, CH])
        xt = sb("pxt", [P, 2, KT, W])
        key = sb("pkey", [P, 2, KT, W])
        stats = sb("pstats", [P, SUB, BN6])
        mv = sb("pmv", [P, SUB, BN2])
        veps = sb("pveps", [P, SUB])
        rstd = sb("prstd", [P, SUB])
        mhalf = sb("pmhalf", [P, SUB])
        squares = sb("psquares", [P, KT, W], BF16)
        ones16 = sb("pones16", [P, P], BF16)
        norms = sb("pnorms", [P, CHUNKS])
        temp = sb("ptemp", [P, 1])
        bcol = sb("pbcol", [P, 1])
        test = sb("ptest", [P, 6])
        ps_t = [ctx.enter_context(nc.psum_tensor(f"ppt{i}", [P, 512], F32)) for i in range(SUB)]
        ps_x = [ctx.enter_context(nc.psum_tensor(f"ppx{i}", [P, 512], F32)) for i in range(KT)]
        ps_k = [ctx.enter_context(nc.psum_tensor(f"ppk{i}", [P, 512], F32)) for i in range(KT)]

        ps_n = ctx.enter_context(nc.psum_tensor("ppn", [P, 512], F32))
        ones_done = sem("p_ones_done")
        squares_done = sem("p_squares_done")
        norm_mm = sem("p_norm_mm")
        norm_done = sem("p_norm_done")
        consts_in = sem("p_consts_in")
        mhalf_done = sem("p_mhalf_done")
        chunk_in = [sem(f"p_chunk_in{i}") for i in range(2)]
        both_done = sem("p_both_done")
        tok_mm = sem("p_tok_mm")
        tok_done = sem("p_tok_done")
        dve_step = sem("p_dve_step")
        veps_done = sem("p_veps_done")
        rstd_done = sem("p_rstd_done")
        xn_done = sem("p_xn_done")
        xt_mm = sem("p_xt_mm")
        xt_done = sem("p_xt_done")
        key_mm = sem("p_key_mm")
        key_done = sem("p_key_done")
        stored = [sem(f"p_stored{i}") for i in range(2)]
        block = ctx.enter_context(nc.Block())
        STEPS = 3

        @block.sync
        def _(sp):
            sp.dma_start(wp[:], w_proj.rearrange("(k p) n -> p k n", p=P)).then_inc(consts_in, 16)
            sp.dma_start(wk[:], w_key.rearrange("(k p) n -> p k n", p=P)).then_inc(consts_in, 16)
            sp.dma_start(bp[:], bp_row.partition_broadcast(P)).then_inc(consts_in, 16)
            sp.dma_start(ident[:], eye[:]).then_inc(consts_in, 16)
            sp.dma_start(temp[:], temperature.partition_broadcast(P)).then_inc(consts_in, 16)
            sp.dma_start(bcol[:], bias.partition_broadcast(P)).then_inc(consts_in, 16)
            for counter in stored:
                sp.sem_inc(counter, 1)
            by_chunk = attn.rearrange("(g c) p n -> g c p n", c=NC)
            with sp.Fori(0, B) as b:
                for c in range(NC):
                    i = c % 2
                    cols = slice(c * W, (c + 1) * W)
                    sp.wait_ge(tok_mm, 1 + SUB + (b * NC + c - 2) * SUB + SUB)
                    for dst, src in ((a_in, by_chunk[bass.ds(b * KT, KT), c]),
                                     (c_in, pe_img[bass.ds(b * KT, KT), :, cols]),
                                     (x_in, x[bass.ds(b, 1), :, cols].rearrange("a (k p) n -> (a k) p n", p=P))):
                        sp.dma_start(dst[:, i], src.rearrange("k p n -> p k n")).then_inc(chunk_in[i], 16)

        @block.gpsimd
        def _(pool):
            nc.gpsimd.memset(ones16[:], 1.0).then_inc(ones_done, 1)
            nc.gpsimd.memset(mhalf[:], -0.5).then_inc(mhalf_done, 1)
            pool.wait_ge(mhalf_done, 1)
            with pool.Fori(0, CHUNKS) as n:
                pool.wait_ge(veps_done, n + 1)
                nc.gpsimd.tensor_tensor(rstd[:], veps[:], mhalf[:], ALU.pow).then_inc(rstd_done, 1)

        @block.vector
        def _(dve):
            dve.sem_inc(tok_done, 1)
            dve.sem_inc(xn_done, 1)
            dve.sem_inc(norm_done, 1)
            dve.wait_ge(consts_in, 6 * 16)
            with dve.Fori(0, CHUNKS // 2) as pair:
                for i in range(2):
                    n = pair * 2 + i
                    st = Steps(dve, dve_step, n * STEPS)
                    dve.wait_ge(chunk_in[i], (pair + 1) * 3 * 16)
                    nc.vector.tensor_tensor(both[:, i], a_in[:, i], c_in[:, i], ALU.add).then_inc(both_done, 1)
                    dve.wait_ge(stored[i], 1 + pair * 4 * 16)
                    for j in range(SUB):
                        dve.wait_ge(tok_mm, 1 + SUB + n * SUB + j + 1)
                        last = nc.vector.tensor_tensor(tok[:, i, j], ps_t[j][:, 0:CH], bp[:], ALU.add)
                        last.then_inc(tok_done, 1)
                    dve.wait_ge(tok_done, 1 + (n + 1) * SUB)
                    for j in range(SUB):
                        last = nc.vector.bn_stats(stats[:, j], tok[:, i, j])
                    st.then(last)
                    nc.vector.memset(veps[:], 0.0)
                    for j in range(SUB):
                        last = nc.vector.bn_aggr(mv[:, j], stats[:, j])
                    st.then(last)
                    nc.vector.tensor_scalar(veps[:], mv[:, :, 1], LN_EPS, None, ALU.add).then_inc(veps_done, 1)
                    dve.wait_ge(rstd_done, n + 1)
                    dve.wait_ge(xt_mm, 1 + n * KT)
                    for j in range(SUB):
                        last = nc.vector.tensor_scalar(xn[:, i, j], tok[:, i, j], mv[:, j, 0:1], rstd[:, j:j + 1],
                                                       ALU.subtract, ALU.mult)
                    st.then(last)
                    dve.sem_inc(xn_done, 1)
                    assert st.n == STEPS
                    dve.wait_ge(norm_mm, 1 + n + 1)
                    nc.vector.reduce_max(norms[:, bass.ds(n, 1)], ps_n[:, 0:W], AX.X).then_inc(norm_done, 1)
            st = Steps(dve, dve_step, CHUNKS * STEPS)
            dve.wait_ge(norm_done, 1 + CHUNKS)
            st.then(nc.vector.reduce_max(test[:, 0:1], norms[:], AX.X))
            st.then(nc.vector.tensor_scalar(test[:, 1:2], temp[:], 1e-6, None, ALU.max))
            st.then(nc.vector.reciprocal(test[:, 2:3], test[:, 1:2]))
            st.then(nc.vector.tensor_scalar(test[:, 1:2], test[:, 2:3], -UNDERFLOW, OUTSIDE, ALU.mult, ALU.add))
            st.then(nc.vector.tensor_scalar(test[:, 2:3], bcol[:], -1.0, None, ALU.mult))
            st.then(nc.vector.tensor_tensor(test[:, 3:4], bcol[:], test[:, 2:3], ALU.max))
            st.then(nc.vector.tensor_tensor(test[:, 4:5], test[:, 1:2], test[:, 3:4], ALU.subtract))
            st.then(nc.vector.tensor_scalar(test[:, 4:5], test[:, 4:5], 0.0, None, ALU.max))
            st.then(nc.vector.tensor_tensor(test[:, 5:6], test[:, 4:5], test[:, 4:5], ALU.mult))
            st.then(nc.vector.tensor_scalar(test[:, 0:1], test[:, 0:1], 1.04 * CH, None, ALU.mult))
            st.then(nc.vector.tensor_tensor(near_only[:], test[0:1, 0:1], test[0:1, 5:6], ALU.is_lt))

        @block.scalar
        def _(act):
            act.sem_inc(xt_done, 1)
            act.sem_inc(key_done, 1)
            act.wait_ge(mhalf_done, 1)
            with act.Fori(0, B) as b:
                for c in range(NC):
                    i = c % 2
                    n = b * NC + c
                    cols = slice(c * W, (c + 1) * W)
                    rows = slice(c * W, (c + 1) * W)
                    act.wait_ge(stored[i], 1 + (b * (NC // 2) + c // 2) * 4 * 16)
                    for k in range(KT):
                        act.wait_ge(xt_mm, 1 + n * KT + k + 1)
                        nc.scalar.activation(xt[:, i, k], ps_x[k][:, 0:W], ACT.Identity).then_inc(xt_done, 1)
                    for k in range(KT):
                        act.wait_ge(key_mm, 1 + n * KT + k + 1)
                        if k == 0:
                            act.wait_ge(norm_mm, 1 + n)
                        nc.scalar.activation(squares[:, k], ps_k[k][:, 0:W], ACT.Square).then_inc(squares_done, 1)
                        nc.scalar.activation(key[:, i, k], ps_k[k][:, 0:W], ACT.Identity).then_inc(key_done, 1)
                    act.wait_ge(xn_done, 1 + n + 1)
                    for dram, src in ((t1, tok), (xn_tok, xn)):
                        act.dma_start(dram[bass.ds(b, 1), rows].rearrange("a (j p) n -> p (a j) n", p=P), src[:, i]
                                      ).then_inc(stored[i], 16)
                    act.wait_ge(key_done, 1 + (n + 1) * KT)
                    act.wait_ge(xt_done, 1 + (n + 1) * KT)
                    for dram, src in ((xn_ch, xt), (key_ch, key)):
                        act.dma_start(dram[bass.ds(b * KT, KT), :, cols].rearrange("k p n -> p k n"), src[:, i]
                                      ).then_inc(stored[i], 16)
            for i in range(2):
                act.wait_ge(stored[i], 1 + CHUNKS // 2 * 4 * 16)

        @block.tensor
        def _(pe):
            for counter in (tok_mm, xt_mm, key_mm, norm_mm):
                pe.sem_inc(counter, 1)
            pe.sem_inc(tok_mm, SUB)
            pe.wait_ge(consts_in, 6 * 16)
            pe.wait_ge(ones_done, 1)

            def project(n, pair, i):
                pe.wait_ge(both_done, n + 1)
                pe.wait_ge(chunk_in[i], (pair + 1) * 3 * 16)
                for j in range(SUB):
                    pe.wait_ge(tok_done, 1 + n * SUB)
                    part = slice(j * P, (j + 1) * P)
                    for k in range(KT):
                        nc.tensor.matmul(ps_t[j][:, k * P:(k + 1) * P], x_in[:, i, k, part], ident[:],
                                         start=(k == 0), stop=False, skip_group_check=True)
                    for k in range(KT):
                        last = nc.tensor.matmul(ps_t[j][:, 0:CH], both[:, i, k, part], wp[:, k, :],
                                                start=False, stop=(k == KT - 1), skip_group_check=True)
                    last.then_inc(tok_mm, 1)

            def norm_products(n, i):
                pe.wait_ge(xn_done, 1 + n + 1)
                for k in range(KT):
                    pe.wait_ge(xt_done, 1 + n * KT)
                    for j in range(SUB):
                        last = nc.tensor.transpose(ps_x[k][:, j * P:(j + 1) * P], xn[:, i, j, k * P:(k + 1) * P], ident[:])
                    last.then_inc(xt_mm, 1)
                pe.wait_ge(xt_done, 1 + (n + 1) * KT)
                for m in range(KT):
                    pe.wait_ge(key_done, 1 + n * KT)
                    for k in range(KT):
                        last = nc.tensor.matmul(ps_k[m][:, 0:W], wk[:, k, m * P:(m + 1) * P], xt[:, i, k, :],
                                                start=(k == 0), stop=(k == KT - 1))
                    last.then_inc(key_mm, 1)
                pe.wait_ge(squares_done, (n + 1) * KT)
                pe.wait_ge(norm_done, 1 + n)
                for k in range(KT):
                    last = nc.tensor.matmul(ps_n[:, 0:W], ones16[:], squares[:, k], start=(k == 0), stop=(k == KT - 1))
                last.then_inc(norm_mm, 1)

            with pe.Fori(0, CHUNKS // 2) as pair:
                for i in range(2):
                    project(pair * 2 + i, pair, i)
                    norm_products(pair * 2 + i, i)


def near_attention(nc, t1, xn_tok, xn_ch, key_ch, near_masks, temperature, bias, eye, near_only, t2):
    with ExitStack() as ctx:
        def sb(name, shape, dt=F32):
            return ctx.enter_context(nc.sbuf_tensor(name, shape, dt))

        def sem(name):
            return ctx.enter_context(nc.semaphore(name))

        WT = SUB + 2
        near = sb("nnear", [P, 3, W])
        temp = sb("ntemp", [P, 1])
        bcol = sb("nbcol", [P, 1])
        ident = sb("nident", [P, P])
        keys = sb("nkeys", [P, 2, KT, W])
        xw = sb("nxw", [P, 2, KT, WT * P])
        vw = sb("nvw", [P, 2, WT, CH])
        t1_sb = sb("nt1", [P, 2, SUB, CH])
        logit = sb("nlogit", [P, SUB, W])
        prob = sb("nprob", [P, 2, SUB, W])
        probt = sb("nprobt", [P, SUB, W])
        mx = sb("nmx", [P, SUB])
        nmx = sb("nnmx", [P, SUB])
        rs = sb("nrs", [P, 2, SUB])
        rrs = sb("nrrs", [P, SUB])
        ps_l = [ctx.enter_context(nc.psum_tensor(f"npl{i}", [P, 512], F32)) for i in range(SUB)]
        ps_p = [ctx.enter_context(nc.psum_tensor(f"npp{i}", [P, 512], F32)) for i in range(2)]
        ps_o = [ctx.enter_context(nc.psum_tensor(f"npo{i}", [P, 512], F32)) for i in range(SUB)]

        consts_in = sem("n_consts_in")
        masks_done = sem("n_masks_done")
        chunk_in = [sem(f"n_chunk_in{i}") for i in range(2)]
        logit_mm = sem("n_logit_mm")
        relu_done = sem("n_relu_done")
        nmx_done = sem("n_nmx_done")
        exp_done = sem("n_exp_done")
        probt_mm = sem("n_probt_mm")
        probt_done = sem("n_probt_done")
        out_mm = sem("n_out_mm")
        t2_done = sem("n_t2_done")
        dve_step = sem("n_dve_step")
        block = ctx.enter_context(nc.Block())
        LOADS = [0, 0]
        upto = []
        for c in range(NC):
            LOADS[c % 2] += 4 + 2 * (c in (0, NC - 1))
            upto.append(LOADS[c % 2])

        def kind(c, j):
            return 0 if (c, j) == (0, 0) else 2 if (c, j) == (NC - 1, SUB - 1) else 1

        @block.sync
        def _(sp):
            for dst, src in ((near[:], near_masks.rearrange("k p n -> p k n")),
                             (temp[:], temperature.partition_broadcast(P)), (bcol[:], bias.partition_broadcast(P)),
                             (ident[:], eye[:])):
                sp.dma_start(dst, src).then_inc(consts_in, 16)
            fast = sp.value_load(near_only[0:1, 0:1], min_val=0, max_val=1)
            with sp.If(fast):
                with sp.Fori(0, B) as b:
                    for c in range(NC):
                        i = c % 2
                        first, end = max(0, c * SUB - 1), min(NT, (c + 1) * SUB + 1)
                        cols = slice(c * W, (c + 1) * W)
                        parts = [(first, end, first - (c * SUB - 1))]
                        parts += [(0, 1, 0)] * (c == 0) + [(NT - 1, NT, WT - 1)] * (c == NC - 1)
                        sp.wait_ge(t2_done, 1 + (b * NC + c) * SUB)
                        for a, z, to in parts:
                            sp.dma_start(xw[:, i, :, to * P:(to + z - a) * P],
                                         xn_ch[bass.ds(b * KT, KT), :, a * P:z * P].rearrange("k p n -> p k n")
                                         ).then_inc(chunk_in[i], 16)
                            sp.dma_start(vw[:, i, to:to + z - a],
                                         xn_tok[bass.ds(b, 1), a * P:z * P].rearrange("a (t p) n -> p (a t) n", p=P)
                                         ).then_inc(chunk_in[i], 16)
                        sp.dma_start(keys[:, i], key_ch[bass.ds(b * KT, KT), :, cols].rearrange("k p n -> p k n")
                                     ).then_inc(chunk_in[i], 16)
                        sp.dma_start(t1_sb[:, i], t1[bass.ds(b, 1), cols].rearrange("a (j p) n -> p (a j) n", p=P)
                                     ).then_inc(chunk_in[i], 16)

        @block.scalar
        def _(act):
            for counter in (relu_done, exp_done, probt_done):
                act.sem_inc(counter, 1)
            act.wait_ge(consts_in, 4 * 16)
            fast = act.value_load(near_only[0:1, 0:1], min_val=0, max_val=1)
            with act.If(fast):
                with act.Fori(0, B) as b:
                    for s in range(NC + 1):
                        if s < NC:
                            n = b * NC + s
                            act.wait_ge(exp_done, 1 + n * SUB)
                            for j in range(SUB):
                                act.wait_ge(logit_mm, 1 + n * SUB + j + 1)
                                nc.scalar.activation(logit[:, j], ps_l[j][:, 0:W], ACT.Relu, bias=bcol[:]).then_inc(relu_done, 1)
                        if s > 0:
                            n = b * NC + s - 1
                            for j in range(SUB):
                                act.wait_ge(probt_mm, 1 + n * SUB + j + 1)
                                act.wait_ge(out_mm, 1 + n * SUB)
                                nc.scalar.activation(probt[:, j], ps_p[j % 2][:, 0:W], ACT.Identity).then_inc(probt_done, 1)
                        if s < NC:
                            n = b * NC + s
                            act.wait_ge(nmx_done, n + 1)
                            act.wait_ge(probt_mm, 1 + n * SUB)
                            for j in range(SUB):
                                nc.scalar.activation(prob[:, s % 2, j], logit[:, j], ACT.Exp, bias=nmx[:, j:j + 1],
                                                     accum_out=rs[:, s % 2, j:j + 1]).then_inc(exp_done, 1)

        @block.vector
        def _(dve):
            dve.sem_inc(t2_done, 1 + SUB)
            dve.wait_ge(consts_in, 4 * 16)
            nc.vector.tensor_scalar(near[:], near[:], temp[:], None, ALU.mult).then_inc(masks_done, 1)
            dve.wait_ge(masks_done, 1)
            fast = dve.value_load(near_only[0:1, 0:1], min_val=0, max_val=1)
            STEPS = 3 * NC
            with dve.If(fast):
                with dve.Fori(0, B) as b:
                    st = Steps(dve, dve_step, b * STEPS)
                    for s in range(NC + 1):
                        if s < NC:
                            n = b * NC + s
                            for j in range(SUB):
                                dve.wait_ge(relu_done, 1 + n * SUB + j + 1)
                                last = nc.vector.scalar_tensor_tensor(out=logit[:, j], in0=logit[:, j], scalar=temp[:],
                                                                      in1=near[:, kind(s, j)], op0=ALU.mult, op1=ALU.add)
                            st.then(last)
                            st.then(nc.vector.reduce_max(mx[:], logit[:], AX.X))
                            nc.vector.tensor_scalar(nmx[:], mx[:], -1.0, None, ALU.mult).then_inc(nmx_done, 1)
                        if s > 0:
                            n = b * NC + s - 1
                            i = (s - 1) % 2
                            dve.wait_ge(exp_done, 1 + (n + 1) * SUB)
                            dve.wait_ge(chunk_in[i], (b * LOADS[i] + upto[s - 1]) * 16)
                            dve.wait_ge(t2_done, 1 + SUB + n * SUB)
                            st.then(nc.vector.reciprocal(rrs[:], rs[:, i]))
                            for j in range(SUB):
                                dve.wait_ge(out_mm, 1 + n * SUB + j + 1)
                                nc.vector.scalar_tensor_tensor(out=t2[:, bass.ds(n * SUB + j, 1)].rearrange("p a n -> p (a n)"),
                                                               in0=ps_o[j][:, 0:CH], scalar=rrs[:, j:j + 1], in1=t1_sb[:, i, j],
                                                               op0=ALU.mult, op1=ALU.add).then_inc(t2_done, 1)
                    assert st.n == STEPS

        @block.tensor
        def _(pe):
            for counter in (logit_mm, probt_mm, out_mm):
                pe.sem_inc(counter, 1)
            pe.wait_ge(consts_in, 4 * 16)
            fast = pe.value_load(near_only[0:1, 0:1], min_val=0, max_val=1)
            with pe.If(fast):
                with pe.Fori(0, B) as b:
                    for s in range(NC + 1):
                        if s < NC:
                            n, i = b * NC + s, s % 2
                            pe.wait_ge(chunk_in[i], (b * LOADS[i] + upto[s]) * 16)
                            for j in range(SUB):
                                pe.wait_ge(relu_done, 1 + n * SUB)
                                for k in range(KT):
                                    last = nc.tensor.matmul(ps_l[j][:, 0:W], keys[:, i, k, j * P:(j + 1) * P],
                                                            xw[:, i, k, j * P:j * P + W], start=(k == 0), stop=(k == KT - 1))
                                last.then_inc(logit_mm, 1)
                        if s > 0:
                            n, i = b * NC + s - 1, (s - 1) % 2

                            def transpose_probs(j):
                                pe.wait_ge(exp_done, 1 + n * SUB + j + 1)
                                pe.wait_ge(probt_done, 1 + n * SUB + max(0, j - 1))
                                for a in range(SUB):
                                    last = nc.tensor.transpose(ps_p[j % 2][:, a * P:(a + 1) * P],
                                                               prob[:, i, j, a * P:(a + 1) * P], ident[:])
                                last.then_inc(probt_mm, 1)

                            def values(j):
                                pe.wait_ge(probt_done, 1 + n * SUB + j + 1)
                                pe.wait_ge(t2_done, 1 + SUB + n * SUB)
                                for a in range(SUB):
                                    last = nc.tensor.matmul(ps_o[j][:, 0:CH], probt[:, j, a * P:(a + 1) * P], vw[:, i, j + a],
                                                            start=(a == 0), stop=(a == SUB - 1))
                                last.then_inc(out_mm, 1)

                            transpose_probs(0)
                            transpose_probs(1)
                            values(0)
                            transpose_probs(2)
                            values(1)
                            values(2)


def dense_attention(nc, t1, xn_tok, xn_ch, key_ch, wide_mask, temperature, bias, eye, near_only, t2):
    with ExitStack() as ctx:
        def sb(name, shape, dt=F32):
            return ctx.enter_context(nc.sbuf_tensor(name, shape, dt))

        def sem(name):
            return ctx.enter_context(nc.semaphore(name))

        wide = sb("dwide", [P, (2 * NT - 1) * P])
        temp = sb("dtemp", [P, 1])
        bcol = sb("dbcol", [P, 1])
        ident = sb("dident", [P, P])
        keys = sb("dkeys", [P, KT, P])
        xw = sb("dxw", [P, KT, N])
        vw = sb("dvw", [P, NT, CH])
        t1_sb = sb("dt1", [P, CH])
        logit = sb("dlogit", [P, NC, W])
        probt = sb("dprobt", [P, NC, W])
        mx = sb("dmx", [P, 1])
        nmx = sb("dnmx", [P, 1])
        rs = sb("drs", [P, 1])
        rrs = sb("drrs", [P, 1])
        ps_l = [ctx.enter_context(nc.psum_tensor(f"dpl{i}", [P, 512], F32)) for i in range(NC)]
        ps_p = ctx.enter_context(nc.psum_tensor("dpp", [P, 512], F32))
        ps_o = ctx.enter_context(nc.psum_tensor("dpo", [P, 512], F32))

        consts_in = sem("d_consts_in")
        masks_done = sem("d_masks_done")
        batch_in = sem("d_batch_in")
        tile_in = sem("d_tile_in")
        logit_mm = sem("d_logit_mm")
        relu_done = sem("d_relu_done")
        nmx_done = sem("d_nmx_done")
        exp_done = sem("d_exp_done")
        probt_mm = sem("d_probt_mm")
        probt_done = sem("d_probt_done")
        out_mm = sem("d_out_mm")
        t2_done = sem("d_t2_done")
        dve_step = sem("d_dve_step")
        block = ctx.enter_context(nc.Block())

        @block.sync
        def _(sp):
            for dst, src in ((wide[:], wide_mask[:]), (temp[:], temperature.partition_broadcast(P)),
                             (bcol[:], bias.partition_broadcast(P)), (ident[:], eye[:])):
                sp.dma_start(dst, src).then_inc(consts_in, 16)
            near = sp.value_load(near_only[0:1, 0:1], min_val=0, max_val=1)
            with sp.If(1 - near):
                with sp.Fori(0, B) as b:
                    sp.wait_ge(t2_done, 1 + b * NT)
                    sp.dma_start(xw[:], xn_ch[bass.ds(b * KT, KT)].rearrange("k p n -> p k n")).then_inc(batch_in, 16)
                    sp.dma_start(vw[:], xn_tok[bass.ds(b, 1)].rearrange("a (t p) n -> p (a t) n", p=P)).then_inc(batch_in, 16)
                    with sp.Fori(0, NT) as t:
                        sp.wait_ge(t2_done, 1 + b * NT + t)
                        sp.dma_start(keys[:], key_ch[bass.ds(b * KT, KT), :, bass.ds(t * P, P)].rearrange("k p n -> p k n")
                                     ).then_inc(tile_in, 16)
                        sp.dma_start(t1_sb[:], t1[bass.ds(b, 1), bass.ds(t * P, P)].rearrange("a p n -> p (a n)")
                                     ).then_inc(tile_in, 16)

        @block.scalar
        def _(act):
            act.wait_ge(consts_in, 4 * 16)
            near = act.value_load(near_only[0:1, 0:1], min_val=0, max_val=1)
            with act.If(1 - near):
                with act.Fori(0, TT) as n:
                    for c in range(NC):
                        act.wait_ge(logit_mm, n * NC + c + 1)
                        nc.scalar.activation(logit[:, c], ps_l[c][:, 0:W], ACT.Relu, bias=bcol[:]).then_inc(relu_done, 1)
                    act.wait_ge(nmx_done, n + 1)
                    nc.scalar.activation(logit[:], logit[:], ACT.Exp, bias=nmx[:], accum_out=rs[:]).then_inc(exp_done, 1)
                    for c in range(NC):
                        act.wait_ge(probt_mm, n * NC + c + 1)
                        nc.scalar.activation(probt[:, c], ps_p[:, 0:W], ACT.Identity).then_inc(probt_done, 1)

        @block.vector
        def _(dve):
            dve.sem_inc(t2_done, 1)
            dve.wait_ge(consts_in, 4 * 16)
            nc.vector.tensor_scalar(wide[:], wide[:], temp[:], None, ALU.mult).then_inc(masks_done, 1)
            dve.wait_ge(masks_done, 1)
            near = dve.value_load(near_only[0:1, 0:1], min_val=0, max_val=1)
            STEPS = 3
            with dve.If(1 - near):
                with dve.Fori(0, B) as b:
                    with dve.Fori(0, NT) as t:
                        n = b * NT + t
                        st = Steps(dve, dve_step, n * STEPS)
                        dve.wait_ge(relu_done, (n + 1) * NC)
                        flat = logit[:].rearrange("p c n -> p (c n)")
                        st.then(nc.vector.scalar_tensor_tensor(out=flat, in0=flat, scalar=temp[:],
                                                               in1=wide[:, bass.ds((NT - 1) * P - t * P, N)],
                                                               op0=ALU.mult, op1=ALU.add))
                        st.then(nc.vector.reduce_max(mx[:], flat, AX.X))
                        nc.vector.tensor_scalar(nmx[:], mx[:], -1.0, None, ALU.mult).then_inc(nmx_done, 1)
                        dve.wait_ge(exp_done, n + 1)
                        dve.wait_ge(t2_done, 1 + n)
                        st.then(nc.vector.reciprocal(rrs[:], rs[:]))
                        dve.wait_ge(tile_in, (n + 1) * 2 * 16)
                        dve.wait_ge(out_mm, n + 1)
                        nc.vector.scalar_tensor_tensor(out=t2[:, bass.ds(n, 1)].rearrange("p a n -> p (a n)"), in0=ps_o[:, 0:CH],
                                                       scalar=rrs[:], in1=t1_sb[:], op0=ALU.mult, op1=ALU.add).then_inc(t2_done, 1)

        @block.tensor
        def _(pe):
            pe.wait_ge(consts_in, 4 * 16)
            near = pe.value_load(near_only[0:1, 0:1], min_val=0, max_val=1)
            with pe.If(1 - near):
                with pe.Fori(0, B) as b:
                    with pe.Fori(0, NT) as t:
                        n = b * NT + t
                        pe.wait_ge(batch_in, (b + 1) * 2 * 16)
                        pe.wait_ge(tile_in, (n + 1) * 2 * 16)
                        for c in range(NC):
                            for k in range(KT):
                                last = nc.tensor.matmul(ps_l[c][:, 0:W], keys[:, k], xw[:, k, c * W:(c + 1) * W],
                                                        start=(k == 0), stop=(k == KT - 1))
                            last.then_inc(logit_mm, 1)
                        pe.wait_ge(exp_done, n + 1)
                        for c in range(NC):
                            if c:
                                pe.wait_ge(probt_done, n * NC + c)
                            for a in range(SUB):
                                last = nc.tensor.transpose(ps_p[:, a * P:(a + 1) * P], logit[:, c, a * P:(a + 1) * P], ident[:])
                            last.then_inc(probt_mm, 1)
                        pe.wait_ge(probt_done, (n + 1) * NC)
                        for c in range(NC):
                            for a in range(SUB):
                                last = nc.tensor.matmul(ps_o[:, 0:CH], probt[:, c, a * P:(a + 1) * P], vw[:, c * SUB + a],
                                                        start=(c + a == 0), stop=(c * SUB + a == NT - 1))
                        last.then_inc(out_mm, 1)


def norm_and_gate(nc, t2, gate_w, gate_b_row, eye, xn2, gate_logits):
    with ExitStack() as ctx:
        def sb(name, shape, dt=F32):
            return ctx.enter_context(nc.sbuf_tensor(name, shape, dt))

        def sem(name):
            return ctx.enter_context(nc.semaphore(name))

        E = gate_w.shape[1]
        CHUNKS = TT // SUB
        ident = sb("gident", [P, P])
        gw = sb("ggw", [P, KT, E])
        gb = sb("ggb", [P, E])
        stats = sb("gstats", [P, SUB, BN6])
        mv = sb("gmv", [P, SUB, BN2])
        veps = sb("gveps", [P, SUB])
        rstd = sb("grstd", [P, SUB])
        mhalf = sb("gmhalf", [P, SUB])
        xn = sb("gxn", [P, 2, SUB, CH])
        xt = sb("gxt", [P, 2, KT, W])
        ps_x = [[ctx.enter_context(nc.psum_tensor(f"gpx{i}{k}", [P, 512], F32)) for k in range(KT)] for i in range(2)]
        ps_g = [ctx.enter_context(nc.psum_tensor(f"gpg{i}", [P, 512], F32)) for i in range(2)]

        consts_in = sem("g_consts_in")
        mhalf_done = sem("g_mhalf_done")
        veps_done = sem("g_veps_done")
        rstd_done = sem("g_rstd_done")
        dve_step = sem("g_dve_step")
        xn_done = sem("g_xn_done")
        xt_mm = sem("g_xt_mm")
        xt_done = sem("g_xt_done")
        gate_mm = sem("g_gate_mm")
        gate_done = sem("g_gate_done")
        block = ctx.enter_context(nc.Block())

        @block.sync
        def _(sp):
            for dst, src in ((ident[:], eye[:]), (gw[:], gate_w.rearrange("(k p) e -> p k e", p=P)),
                             (gb[:], gate_b_row.partition_broadcast(P))):
                sp.dma_start(dst, src).then_inc(consts_in, 16)

        @block.gpsimd
        def _(pool):
            nc.gpsimd.memset(mhalf[:], -0.5).then_inc(mhalf_done, 1)
            pool.wait_ge(mhalf_done, 1)
            with pool.Fori(0, CHUNKS) as n:
                pool.wait_ge(veps_done, n + 1)
                nc.gpsimd.tensor_tensor(rstd[:], veps[:], mhalf[:], ALU.pow).then_inc(rstd_done, 1)

        @block.vector
        def _(dve):
            dve.sem_inc(xn_done, 1)
            dve.sem_inc(gate_done, 1 + SUB)
            dve.wait_ge(consts_in, 3 * 16)
            STEPS = 2
            with dve.Fori(0, CHUNKS // 2) as pair:
                for i in range(2):
                    n = pair * 2 + i
                    st = Steps(dve, dve_step, n * STEPS)
                    nc.vector.memset(veps[:, 0:1], 0.0)
                    for j in range(SUB):
                        last = nc.vector.bn_stats(stats[:, j], t2[:, bass.ds(n * SUB + j, 1)].rearrange("p a n -> p (a n)"))
                    st.then(last)
                    dve.wait_ge(xn_done, 1 + n * SUB)
                    nc.vector.memset(veps[:, 0:1], 0.0)
                    for j in range(SUB):
                        last = nc.vector.bn_aggr(mv[:, j], stats[:, j])
                    st.then(last)
                    nc.vector.tensor_scalar(veps[:], mv[:, :, 1], LN_EPS, None, ALU.add).then_inc(veps_done, 1)
                    dve.wait_ge(rstd_done, n + 1)
                    dve.wait_ge(xt_mm, 1 + n * KT)
                    for j in range(SUB):
                        token_tile = t2[:, bass.ds(n * SUB + j, 1)].rearrange("p a n -> p (a n)")
                        nc.vector.tensor_scalar(xn2[:, bass.ds(n * SUB + j, 1)].rearrange("p a n -> p (a n)"), token_tile,
                                                mv[:, j, 0:1], rstd[:, j:j + 1], ALU.subtract, ALU.mult)
                        nc.vector.tensor_scalar(xn[:, i, j], token_tile, mv[:, j, 0:1], rstd[:, j:j + 1],
                                                ALU.subtract, ALU.mult).then_inc(xn_done, 1)
                    dve.wait_ge(gate_mm, (n + 1) * SUB)
                    for j in range(SUB):
                        nc.vector.tensor_tensor(gate_logits[:, :, bass.ds(n * SUB + j, 1)].rearrange("p e a -> p (e a)"),
                                                ps_g[i][:, j * E:(j + 1) * E], gb[:], ALU.add).then_inc(gate_done, 1)

        @block.scalar
        def _(act):
            act.sem_inc(xt_done, 1)
            with act.Fori(0, CHUNKS // 2) as pair:
                for i in range(2):
                    n = pair * 2 + i
                    for k in range(KT):
                        act.wait_ge(xt_mm, 1 + KT + n * KT + k + 1)
                        nc.scalar.activation(xt[:, i, k], ps_x[i][k][:, 0:W], ACT.Identity).then_inc(xt_done, 1)

        @block.tensor
        def _(pe):
            pe.sem_inc(xt_mm, 1 + KT)
            pe.wait_ge(consts_in, 3 * 16)
            with pe.Fori(0, CHUNKS // 2) as pair:
                for i in range(2):
                    n = pair * 2 + i
                    pe.wait_ge(xn_done, 1 + (n + 1) * SUB)
                    for k in range(KT):
                        pe.wait_ge(xt_done, 1 + n * KT)
                        for j in range(SUB):
                            last = nc.tensor.transpose(ps_x[i][k][:, j * P:(j + 1) * P], xn[:, i, j, k * P:(k + 1) * P], ident[:])
                        last.then_inc(xt_mm, 1)
                    pe.wait_ge(xt_done, 1 + (n + 1) * KT)
                    pe.wait_ge(gate_done, 1 + n * SUB)
                    for j in range(SUB):
                        for k in range(KT):
                            last = nc.tensor.matmul(ps_g[i][:, j * E:(j + 1) * E], xt[:, i, k, j * P:(j + 1) * P], gw[:, k],
                                                    start=(k == 0), stop=(k == KT - 1))
                        last.then_inc(gate_mm, 1)


def route(nc, gate_logits, capacity, rank, base, trash_place, prefix, to_slot, from_slot, weight):
    with ExitStack() as ctx:
        E = gate_logits.shape[1]

        def sb(name, shape, dt=F32):
            return ctx.enter_context(nc.sbuf_tensor(name, shape, dt))

        def sem(name):
            return ctx.enter_context(nc.semaphore(name))

        HALF = E // 2
        rk = sb("rrank", [P, E, TT])
        bs = sb("rbase", [P, E, TT])
        trash = sb("rtrash", [P, TT])
        tri = sb("rtri", [P, P])
        ones = sb("rones", [P, P])
        zeros = sb("rzeros", [P, TT])
        best = sb("rbest", [P, TT])
        prob = sb("rprob", [P, E, TT])
        total = sb("rtotal", [P, TT])
        inv = sb("rinv", [P, TT])
        top = sb("rtop", [P, TT])
        hot = sb("rhot", [P, E, TT])
        pick = sb("rpick", [P, TT])
        count = sb("rcount", [P, E, TT])
        scan = sb("rscan", [P, E, TT])
        place = sb("rplace", [P, E, TT])
        pos = sb("rpos", [P, TT])
        off = sb("roff", [P, TT])
        kept = sb("rkept", [P, TT])
        tmp = sb("rtmp", [P, TT])
        ps_c = [ctx.enter_context(nc.psum_tensor(f"rpc{i}", [P, 512], F32)) for i in range(2)]
        ps_t = [ctx.enter_context(nc.psum_tensor(f"rpt{i}", [P, 512], F32)) for i in range(2)]

        consts_in = sem("r_consts_in")
        ones_done = sem("r_ones_done")
        dve_step = sem("r_dve_step")
        exp_done = sem("r_exp_done")
        hot_done = sem("r_hot_done")
        counts_mm = sem("r_counts_mm")
        block = ctx.enter_context(nc.Block())

        def over_experts(t):
            return t[:].rearrange("p e t -> p t e")

        def to_experts(t):
            return t[:].rearrange("p (a t) -> p a t", a=1).to_broadcast([P, E, TT])

        @block.sync
        def _(sp):
            for dst, src in ((rk[:], rank[:]), (bs[:], base[:]), (trash[:], trash_place[:]), (tri[:], prefix[:])):
                sp.dma_start(dst, src).then_inc(consts_in, 16)

        @block.gpsimd
        def _(pool):
            nc.gpsimd.memset(zeros[:], 0.0).then_inc(ones_done, 1)
            nc.gpsimd.memset(ones[:], 1.0).then_inc(ones_done, 1)

        @block.scalar
        def _(act):
            act.wait_ge(dve_step, 2)
            nc.scalar.activation(prob[:], gate_logits[:], ACT.Exp).then_inc(exp_done, 1)

        @block.tensor
        def _(pe):
            pe.wait_ge(consts_in, 4 * 16)
            pe.wait_ge(ones_done, 2)
            pe.wait_ge(hot_done, 1)
            for i in range(2):
                half = hot[:, i * HALF:(i + 1) * HALF].rearrange("p e t -> p (e t)")
                nc.tensor.matmul(ps_c[i][:, 0:HALF * TT], tri[:], half, start=True, stop=True)
                last = nc.tensor.matmul(ps_t[i][:, 0:HALF * TT], ones[:], half, start=True, stop=True)
            last.then_inc(counts_mm, 1)

        @block.vector
        def _(dve):
            st = Steps(dve, dve_step)
            tt, ts = nc.vector.tensor_tensor, nc.vector.tensor_scalar
            st.then(nc.vector.reduce_max(best[:], over_experts(gate_logits), AX.X))
            st.then(tt(gate_logits[:], gate_logits[:], to_experts(best), ALU.subtract))
            dve.wait_ge(exp_done, 1)
            st.then(nc.vector.reduce_sum(total[:], over_experts(prob), AX.X))
            st.then(nc.vector.reciprocal(inv[:], total[:]))
            st.then(tt(prob[:], prob[:], to_experts(inv), ALU.mult))
            st.then(nc.vector.reduce_max(top[:], over_experts(prob), AX.X))
            st.then(tt(hot[:], prob[:], to_experts(top), ALU.is_equal))
            dve.wait_ge(consts_in, 4 * 16)
            st.then(tt(hot[:], hot[:], rk[:], ALU.mult))
            st.then(nc.vector.reduce_max(pick[:], over_experts(hot), AX.X))
            st.then(tt(count[:], rk[:], to_experts(pick), ALU.is_equal))
            nc.vector.tensor_copy(hot[:], count[:]).then_inc(hot_done, 1)
            dve.wait_ge(counts_mm, 1)
            dve.wait_ge(ones_done, 2)
            for i in range(2):
                es = slice(i * HALF, (i + 1) * HALF)
                last = nc.vector.tensor_copy(count[:, es].rearrange("p e t -> p (e t)"), ps_t[i][:, 0:HALF * TT])
            st.then(last)
            for e in range(E):
                last = nc.vector.tensor_tensor_scan(scan[:, e], count[:, e], zeros[:], initial=0.0, op0=ALU.add, op1=ALU.add)
            st.then(last)
            st.then(tt(scan[:], scan[:], count[:], ALU.subtract))
            for i in range(2):
                es = slice(i * HALF, (i + 1) * HALF)
                last = tt(place[:, es].rearrange("p e t -> p (e t)"), ps_c[i][:, 0:HALF * TT],
                          scan[:, es].rearrange("p e t -> p (e t)"), ALU.add)
            st.then(last)
            st.then(tt(place[:], place[:], hot[:], ALU.mult))
            st.then(nc.vector.reduce_sum(pos[:], over_experts(place), AX.X))
            st.then(ts(pos[:], pos[:], -1.0, None, ALU.add))
            st.then(tt(hot[:], hot[:], bs[:], ALU.mult))
            st.then(nc.vector.reduce_sum(off[:], over_experts(hot), AX.X))
            st.then(ts(kept[:], pos[:], float(capacity), None, ALU.is_lt))
            st.then(tt(weight[:], top[:], kept[:], ALU.mult))
            st.then(ts(tmp[:], pos[:], float(capacity - 1), None, ALU.min))
            st.then(tt(tmp[:], tmp[:], off[:], ALU.add))
            st.then(nc.vector.tensor_copy(from_slot[:], tmp[:]))
            st.then(tt(pos[:], pos[:], off[:], ALU.add))
            st.then(tt(pos[:], pos[:], trash[:], ALU.subtract))
            st.then(tt(pos[:], pos[:], kept[:], ALU.mult))
            st.then(tt(pos[:], pos[:], trash[:], ALU.add))
            st.then(nc.vector.tensor_copy(to_slot[:], pos[:]))


def scatter_tokens(nc, xn2, to_slot, slots_used, slots):
    with ExitStack() as ctx:
        zeros = ctx.enter_context(nc.sbuf_tensor("szeros", [P, slots_used // P * CH // 9], F32))
        zeros_set = ctx.enter_context(nc.semaphore("s_zeros_set"))
        zeroed = ctx.enter_context(nc.semaphore("s_zeroed"))
        scattered = ctx.enter_context(nc.semaphore("s_scattered"))
        block = ctx.enter_context(nc.Block())

        @block.vector
        def _(dve):
            nc.vector.memset(zeros[:], 0.0).then_inc(zeros_set, 1)

        @block.sync
        def _(sp):
            sp.wait_ge(zeros_set, 1)
            rows = slots_used // 9
            for a in range(9):
                sp.dma_start(slots[a * rows:(a + 1) * rows].rearrange("(p r) n -> p (r n)", p=P), zeros[:]).then_inc(zeroed, 16)

        @block.gpsimd
        def _(pool):
            pool.wait_ge(zeroed, 9 * 16)
            for n in range(TT):
                pool.indirect_dma_start(slots[:], bass.IndirectOffsetOnAxis(ap=to_slot[:, n:n + 1], axis=0), xn2[:, n], None
                                        ).then_inc(scattered, 16)
            pool.wait_ge(scattered, TT * 16)


def experts(nc, slots, w1, b1_cols, w2, b2, eye, capacity, results):
    with ExitStack() as ctx:
        def sb(name, shape, dt=F32):
            return ctx.enter_context(nc.sbuf_tensor(name, shape, dt))

        def sem(name):
            return ctx.enter_context(nc.semaphore(name))

        E, _, F = w1.shape
        FT = F // P
        RT = 3
        S = 4
        R = capacity // (RT * S)
        RW = S * R
        w1_sb = sb("ew1", [P, 2, KT, F])
        w2_sb = sb("ew2", [P, 2, FT, CH])
        b1_sb = sb("eb1", [P, 2, FT])
        b2_sb = sb("eb2", [P, 2, CH])
        ident = sb("eident", [P, P])
        x = sb("ex", [R, 2, S, CH])
        xt = sb("ext", [P, KT, RW])
        hid = sb("ehid", [P, FT, RW])
        y = sb("ey", [R, 2, S, CH])
        ps_x = [ctx.enter_context(nc.psum_tensor(f"epx{i}", [P, 512], F32)) for i in range(KT)]
        ps_h = [ctx.enter_context(nc.psum_tensor(f"eph{i}", [P, 512], F32)) for i in range(4)]
        ps_y = [ctx.enter_context(nc.psum_tensor(f"epy{i}", [P, 512], F32)) for i in range(2)]

        consts_in = sem("e_consts_in")
        w_in = [sem(f"e_w_in{i}") for i in range(2)]
        x_in = [sem(f"e_x_in{i}") for i in range(2)]
        xt_mm = sem("e_xt_mm")
        xt_done = sem("e_xt_done")
        hid_mm = sem("e_hid_mm")
        hid_done = sem("e_hid_done")
        y_mm = sem("e_y_mm")
        y_done = sem("e_y_done")
        stored = [sem(f"e_stored{i}") for i in range(2)]
        block = ctx.enter_context(nc.Block())
        rows = slots[0:E * capacity].rearrange("(n s r) c -> n r s c", s=S, r=R)
        rows_out = results.rearrange("(n s r) c -> n r s c", s=S, r=R)
        TILES = E * RT

        def tiles(it):
            for j in range(2 * RT):
                yield j, it * 2 * RT + j, j // RT, j % 2

        @block.sync
        def _(sp):
            sp.dma_start(ident[:], eye[:]).then_inc(consts_in, 16)

            def load_rows(n, i):
                sp.dma_start(x[:, i], rows[bass.ds(n, 1)].rearrange("a r s c -> r (a s) c")).then_inc(x_in[i], 16)

            def load_weights(expert, e):
                one = bass.ds(expert, 1)
                for dst, src in ((w1_sb[:, e], w1[one].rearrange("a (k p) f -> p (a k) f", p=P)),
                                 (w2_sb[:, e], w2[one].rearrange("a (f p) c -> p (a f) c", p=P)),
                                 (b1_sb[:, e], b1_cols[one].rearrange("a p f -> p (a f)")),
                                 (b2_sb[:, e], b2[one].rearrange("a c -> (a c)").partition_broadcast(P))):
                    sp.dma_start(dst, src).then_inc(w_in[e], 16)

            def two_experts(it, last):
                for j, n, e, i in tiles(it):
                    if not (last and j == 2 * RT - 1):
                        load_rows(n + 1, 1 - i)
                    sp.wait_ge(y_done, 3 + (n + 1) * S)
                    sp.dma_start(rows_out[bass.ds(n, 1)].rearrange("a r s c -> r (a s) c"), y[:, i]).then_inc(stored[i], 16)
                    if j % RT == RT - 1 and not last:
                        load_weights(it * 2 + 2 + e, e)

            load_rows(0, 0)
            load_weights(0, 0)
            load_weights(1, 1)
            with sp.Fori(0, E // 2 - 1) as it:
                two_experts(it, False)
            two_experts(E // 2 - 1, True)
            for i in range(2):
                sp.wait_ge(stored[i], 1 + TILES // 2 * 16)

        @block.scalar
        def _(act):
            act.sem_inc(xt_done, 1)
            act.sem_inc(hid_done, 1 + FT)
            with act.Fori(0, E // 2) as it:
                for j, n, e, i in tiles(it):
                    for k in range(KT):
                        act.wait_ge(xt_mm, 2 + n)
                        nc.scalar.activation(xt[:, k], ps_x[k][:, 0:RW], ACT.Identity).then_inc(xt_done, 1)
                    act.wait_ge(w_in[e], (it + 1) * 4 * 16)
                    for f in range(FT):
                        act.wait_ge(hid_mm, 1 + n * FT + f + 1)
                        act.wait_ge(y_mm, 1 + n * S)
                        nc.scalar.activation(hid[:, f], ps_h[f % 4][:, 0:RW], ACT.Relu,
                                             bias=b1_sb[:, e, f:f + 1]).then_inc(hid_done, 1)

        @block.vector
        def _(dve):
            dve.sem_inc(y_done, 1 + 2)
            for counter in stored:
                dve.sem_inc(counter, 1)
            with dve.Fori(0, E // 2) as it:
                for j, n, e, i in tiles(it):
                    dve.wait_ge(w_in[e], (it + 1) * 4 * 16)
                    dve.wait_ge(stored[i], 1 + (it * RT + j // 2) * 16)
                    for s in range(S):
                        dve.wait_ge(y_mm, 1 + n * S + s + 1)
                        nc.vector.tensor_tensor(y[:, i, s], ps_y[s % 2][0:R, 0:CH], b2_sb[0:R, e], ALU.add).then_inc(y_done, 1)

        @block.tensor
        def _(pe):
            for counter in (xt_mm, hid_mm, y_mm):
                pe.sem_inc(counter, 1)
            pe.wait_ge(consts_in, 16)
            with pe.Fori(0, E // 2) as it:
                for j, n, e, i in tiles(it):
                    pe.wait_ge(x_in[i], (it * RT + j // 2 + 1) * 16)
                    pe.wait_ge(xt_done, 1 + n * KT)
                    for k in range(KT):
                        for s in range(S):
                            last = nc.tensor.transpose(ps_x[k][:, s * R:(s + 1) * R], x[:, i, s, k * P:(k + 1) * P], ident[0:R, 0:R])
                    last.then_inc(xt_mm, 1)
                    pe.wait_ge(xt_done, 1 + (n + 1) * KT)
                    pe.wait_ge(w_in[e], (it + 1) * 4 * 16)
                    for f in range(FT):
                        pe.wait_ge(hid_done, 1 + FT + n * FT + f - 3)
                        for k in range(KT):
                            last = nc.tensor.matmul(ps_h[f % 4][:, 0:RW], w1_sb[:, e, k, f * P:(f + 1) * P], xt[:, k],
                                                    start=(k == 0), stop=(k == KT - 1))
                        last.then_inc(hid_mm, 1)
                    for s in range(S):
                        pe.wait_ge(y_done, 3 + n * S + s - 1)
                        for f in range(FT):
                            if s == 0:
                                pe.wait_ge(hid_done, 1 + FT + n * FT + f + 1)
                            last = nc.tensor.matmul(ps_y[s % 2][0:R, 0:CH], hid[:, f, s * R:(s + 1) * R], w2_sb[:, e, f],
                                                    start=(f == 0), stop=(f == FT - 1))
                        last.then_inc(y_mm, 1)


def combine(nc, results, from_slot, weight, t2, eye, out):
    with ExitStack() as ctx:
        def sb(name, shape, dt=F32):
            return ctx.enter_context(nc.sbuf_tensor(name, shape, dt))

        def sem(name):
            return ctx.enter_context(nc.semaphore(name))

        FLT_MAX = 3.4028234e38
        NAN_TO_NUM = 10000.0
        SLOTS = 2
        rows = sb("orows", [P, SLOTS, SUB, CH])
        pos = sb("opos", [P, SUB, CH])
        neg = sb("oneg", [P, SUB, CH])
        cap = sb("ocap", [P, 2, SUB, CH])
        tok = sb("otok", [P, SUB, CH])
        img = sb("oimg", [P, 2, KT, W])
        ident = sb("oident", [P, P])
        ps = [[ctx.enter_context(nc.psum_tensor(f"op{i}{k}", [P, 512], F32)) for k in range(KT)] for i in range(2)]
        CHUNKS = B * NC

        consts_in = sem("o_consts_in")
        rows_in = [sem(f"o_rows_in{i}") for i in range(2)]
        rows_used = sem("o_rows_used")
        dve_step = sem("o_dve_step")
        tok_done = sem("o_tok_done")
        tok_mm = sem("o_tok_mm")
        img_done = sem("o_img_done")
        stored = [sem(f"o_stored{i}") for i in range(2)]
        block = ctx.enter_context(nc.Block())

        @block.sync
        def _(sp):
            sp.dma_start(ident[:], eye[:]).then_inc(consts_in, 16)
            for counter in stored:
                sp.sem_inc(counter, 1)
            with sp.Fori(0, B) as b:
                for c in range(NC):
                    sp.wait_ge(img_done, 1 + (b * NC + c + 1) * KT)
                    sp.dma_start(out[bass.ds(b, 1), :, c * W:(c + 1) * W].rearrange("a (k p) n -> p (a k) n", p=P), img[:, c % 2]
                                 ).then_inc(stored[c % 2], 16)
            for i in range(2):
                sp.wait_ge(stored[i], 1 + CHUNKS // 2 * 16)

        @block.gpsimd
        def _(pool):
            for n in range(CHUNKS):
                if n >= 2:
                    pool.wait_ge(rows_used, n - 1)
                for j in range(SUB):
                    at = n * SUB + j
                    pool.indirect_dma_start(rows[:, n % 2, j], None, results[:],
                                            bass.IndirectOffsetOnAxis(ap=from_slot[:, at:at + 1], axis=0)
                                            ).then_inc(rows_in[n % 2], 16)

        @block.vector
        def _(dve):
            dve.wait_ge(consts_in, 16)
            STEPS = 4
            with dve.Fori(0, CHUNKS // 2) as pair:
                for i in range(2):
                    n = pair * 2 + i
                    st = Steps(dve, dve_step, n * STEPS)
                    dve.wait_ge(rows_in[i], (pair + 1) * SUB * 16)
                    for j in range(SUB):
                        w = weight[:, bass.ds(n * SUB + j, 1)]
                        nc.vector.tensor_scalar(pos[:, j], rows[:, i, j], w, 0.0, ALU.mult, ALU.max)
                        last = nc.vector.tensor_scalar(neg[:, j], rows[:, i, j], w, 0.0, ALU.mult, ALU.min)
                    st.then(last)
                    dve.sem_inc(rows_used, 1)
                    nc.vector.tensor_scalar(cap[:, 0], pos[:], FLT_MAX, FLT_MAX, ALU.is_le, ALU.mult)
                    st.then(nc.vector.tensor_scalar(cap[:, 1], neg[:], -FLT_MAX, -FLT_MAX, ALU.is_ge, ALU.mult))
                    nc.vector.scalar_tensor_tensor(out=pos[:], in0=cap[:, 0], scalar=NAN_TO_NUM, in1=pos[:],
                                                   op0=ALU.max, op1=ALU.min)
                    st.then(nc.vector.scalar_tensor_tensor(out=neg[:], in0=cap[:, 1], scalar=-NAN_TO_NUM, in1=neg[:],
                                                           op0=ALU.min, op1=ALU.max))
                    st.then(nc.vector.tensor_tensor(pos[:], pos[:], neg[:], ALU.add))
                    dve.wait_ge(tok_mm, 1 + n * KT)
                    nc.vector.tensor_tensor(tok[:], pos[:], t2[:, bass.ds(n * SUB, SUB)], ALU.add).then_inc(tok_done, 1)
                    dve.wait_ge(tok_done, n + 1)

        @block.scalar
        def _(act):
            act.sem_inc(img_done, 1)
            with act.Fori(0, CHUNKS // 2) as pair:
                for i in range(2):
                    n = pair * 2 + i
                    act.wait_ge(stored[i], 1 + pair * 16)
                    for k in range(KT):
                        act.wait_ge(tok_mm, 1 + n * KT + k + 1)
                        nc.scalar.activation(img[:, i, k], ps[i][k][:, 0:W], ACT.Identity).then_inc(img_done, 1)

        @block.tensor
        def _(pe):
            pe.sem_inc(tok_mm, 1)
            pe.wait_ge(consts_in, 16)
            with pe.Fori(0, CHUNKS // 2) as pair:
                for i in range(2):
                    n = pair * 2 + i
                    pe.wait_ge(tok_done, n + 1)
                    for k in range(KT):
                        pe.wait_ge(img_done, 1 + n * KT)
                        for j in range(SUB):
                            last = nc.tensor.transpose(ps[i][k][:, j * P:(j + 1) * P], tok[:, j, k * P:(k + 1) * P], ident[:])
                        last.then_inc(tok_mm, 1)


_INS = []


def kernel(**inputs):
    import numpy as _np
    import concourse.bacc as _bacc
    from concourse.bass_utils import run_bass_kernel_spmd as _run

    g = inputs
    w_qk = _np.asarray(g["L0_conv_w_qk"]).reshape(HEADS, 2, HD, CH)
    w_q, w_k = w_qk[:, 0].reshape(CH, CH), w_qk[:, 1].reshape(CH, CH)
    b_qk = _np.asarray(g["L0_conv_b_qk"]).reshape(HEADS, 2, HD)
    b_all = _np.stack([b_qk[:, 0].reshape(CH), b_qk[:, 1].reshape(CH), _np.asarray(g["L0_conv_b_v"])])
    eye = _np.eye(P, dtype=_np.float32)
    arrays = {
        "x": _np.asarray(g["x"]).reshape(B, CH, N),
        "w_qkv": _np.concatenate([w_q.T, w_k.T, _np.asarray(g["L0_conv_w_v"])[:, :, 0, 0].T], axis=1),
        "b_qkv": b_all.reshape(3 * KT, P).T,
        "bv_row": _np.asarray(g["L0_conv_b_v"]),
        "group_mean": _np.kron(_np.eye(P // GN_GROUP, dtype=_np.float32), _np.full((GN_GROUP, GN_GROUP), 1 / GN_GROUP, _np.float32)),
    }
    arrays["w_pe"] = _np.asarray(g["L0_conv_w_pe"]).reshape(CH, 9)
    arrays["b_pe"] = _np.asarray(g["L0_conv_b_pe"]).reshape(KT, P).T
    arrays["w_proj"] = _np.asarray(g["L0_conv_w_proj"])[:, :, 0, 0].T
    arrays["bp_row"] = _np.asarray(g["L0_conv_b_proj"])
    arrays["eye"] = eye
    arrays["head_sum"] = _np.kron(_np.eye(HG, dtype=_np.float32), _np.ones((HD, HD), _np.float32))
    arrays["w_key"] = _np.asarray(g["L1_attn_K"])
    arrays["temperature"] = _np.asarray(g["L1_attn_temperature"])
    arrays["bias"] = _np.asarray(g["L1_attn_bias"])
    ahead = _np.arange(-(NT - 1) * P, NT * P)[None, :] - _np.arange(P)[:, None]
    outside = (ahead < -(WINDOW // 2)) | (ahead >= WINDOW - WINDOW // 2)
    arrays["wide_mask"] = _np.where(outside, _np.float32(-OUTSIDE), _np.float32(0))
    inner = arrays["wide_mask"][:, (NT - 2) * P:(NT + 1) * P]
    near_masks = _np.stack([inner, inner, inner])
    near_masks[0, :, :P] = near_masks[2, :, 2 * P:] = GONE
    arrays["near_masks"] = near_masks
    capacity = -(-T * 5 // (4 * EXPERTS))
    arrays["gate_w"] = _np.asarray(g["L1_ffn_gate_w"])
    arrays["gate_b"] = _np.asarray(g["L1_ffn_gate_b"])
    arrays["w1"] = _np.asarray(g["L1_ffn_w1"])
    arrays["w2"] = _np.asarray(g["L1_ffn_w2"])
    arrays["b1_cols"] = _np.asarray(g["L1_ffn_b1"]).reshape(EXPERTS, -1, P).transpose(0, 2, 1)
    arrays["b2"] = _np.asarray(g["L1_ffn_b2"])
    table = _np.zeros((P, EXPERTS, TT), _np.float32)
    expert = _np.arange(EXPERTS, dtype=_np.float32)[None, :, None]
    arrays["rank"] = table + (EXPERTS - expert)
    arrays["base"] = table + expert * capacity
    arrays["trash_place"] = _np.float32(EXPERTS * capacity) + _np.arange(T, dtype=_np.float32).reshape(TT, P).T
    arrays["prefix"] = _np.triu(_np.ones((P, P), _np.float32))
    nc = _bacc.Bacc("TRN2", target_bir_lowering=False, num_devices=1)
    arrays = {k: _np.ascontiguousarray(v) for k, v in arrays.items()}
    ap = {k: nc.dram_tensor(k, v.shape, mybir.dt.from_np(v.dtype), kind="ExternalInput").ap() for k, v in arrays.items()}
    def scratch(name, shape, dt=F32):
        return nc.dram_tensor(name, shape, dt).ap()
    small_scores = nc.alloc_sbuf_tensor("small_scores", [1, 1], I32)
    qh, ql = (scratch(n, (BG * NC, P, W)) for n in ("qh", "ql"))
    kh, kl, v_img, pe_img, xn_ch, key_ch = (scratch(n, (BG, P, N)) for n in ("kh", "kl", "v_img", "pe_img", "xn_ch", "key_ch"))
    v_tok, xn_tok = (scratch(n, (B, N, CH)) for n in ("v_tok", "xn_tok"))
    attn = scratch("attn", (BG * NC, P, W))
    conv_inputs(nc, ap["x"], ap["w_qkv"], ap["b_qkv"], ap["bv_row"], ap["group_mean"], ap["head_sum"], ap["eye"], qh, ql, kh, kl, v_img, v_tok, small_scores)
    conv_attention(nc, qh, ql, kh, kl, v_img, v_tok, ap["w_pe"], ap["b_pe"], ap["eye"], small_scores, attn, pe_img)
    out = nc.dram_tensor("out_0", (B, CH, N), F32, kind="ExternalOutput").ap()
    t1 = scratch("t1", (B, N, CH))
    near_only = nc.alloc_sbuf_tensor("near_only", [1, 1], I32)
    t2 = nc.alloc_sbuf_tensor("t2", [P, TT, CH], F32)
    project_and_norm(nc, attn, pe_img, ap["x"], ap["w_proj"], ap["bp_row"], ap["eye"], ap["w_key"], ap["temperature"],
                     ap["bias"], near_only, t1, xn_tok, xn_ch, key_ch)
    near_attention(nc, t1, xn_tok, xn_ch, key_ch, ap["near_masks"], ap["temperature"], ap["bias"], ap["eye"], near_only, t2)
    dense_attention(nc, t1, xn_tok, xn_ch, key_ch, ap["wide_mask"], ap["temperature"], ap["bias"], ap["eye"], near_only, t2)
    gate_logits = nc.alloc_sbuf_tensor("gate_logits", [P, EXPERTS, TT], F32)
    to_slot = nc.alloc_sbuf_tensor("to_slot", [P, TT], U32)
    from_slot = nc.alloc_sbuf_tensor("from_slot", [P, TT], U32)
    weight = nc.alloc_sbuf_tensor("weight", [P, TT], F32)
    slots = scratch("slots", (EXPERTS * capacity + T, CH))
    results = scratch("results", (EXPERTS * capacity, CH))
    with nc.sbuf_tensor("xn2", [P, TT, CH], F32) as xn2:
        norm_and_gate(nc, t2, ap["gate_w"], ap["gate_b"], ap["eye"], xn2, gate_logits)
        route(nc, gate_logits, capacity, ap["rank"], ap["base"], ap["trash_place"], ap["prefix"], to_slot, from_slot, weight)
        scatter_tokens(nc, xn2, to_slot, EXPERTS * capacity, slots)
    experts(nc, slots, ap["w1"], ap["b1_cols"], ap["w2"], ap["b2"], ap["eye"], capacity, results)
    combine(nc, results, from_slot, weight, t2, ap["eye"], out)
    r = _run(nc, [arrays], core_ids=[0])
    return r.results[0]["out_0"].reshape(B, CH, IMG, IMG)
```

```python
from contextlib import ExitStack

import concourse.bass as bass
from concourse import mybir

F32 = mybir.dt.float32
F32R = mybir.dt.float32r
BF16 = mybir.dt.bfloat16
I32 = mybir.dt.int32
U32 = mybir.dt.uint32
ALU = mybir.AluOpType
ACT = mybir.ActivationFunctionType
AX = mybir.AxisListType

P = 128
B, CH, IMG = 4, 256, 48
N = IMG * IMG
T = B * N
KT = CH // P
NT = N // P
TT = T // P
W = 384
NC = N // W
SUB = W // P
HEADS, HD = 8, 32
EXPERTS = 8
HG = P // HD
SCALE = HD ** -0.5
MAX_SCORE = 30.0
GN_GROUP = 8
GN_EPS, LN_EPS = 1e-5, 1e-5
WINDOW = 24
OUTSIDE = 10000.0
UNDERFLOW = 110.0
GONE = -1e30
BG = B * KT
BN6, BN2 = 6, 2


class Steps:

    def __init__(self, engine, sem, base=0):
        self.engine, self.sem, self.base, self.n = engine, sem, base, 0

    def then(self, instruction):
        self.n += 1
        instruction.then_inc(self.sem, 1)
        self.engine.wait_ge(self.sem, self.base + self.n)


def conv_inputs(nc, x, w_qkv, b_qkv, bv_row, group_mean, head_sum, eye, qh, ql, kh, kl, v_img, v_tok, small_scores):
    with ExitStack() as ctx:
        def sb(name, shape, dt=F32):
            return ctx.enter_context(nc.sbuf_tensor(name, shape, dt))

        def sem(name):
            return ctx.enter_context(nc.semaphore(name))

        x_sb = sb("cx", [P, KT, N])
        xn = sb("cxn", [P, KT, N])
        wq = sb("cw", [P, KT, 3 * CH])
        bq = sb("cb", [P, 3 * KT])
        bv = sb("cbv", [P, CH])
        gm = sb("cgm", [P, P])
        stats = sb("cstats", [P, KT, NC, BN6])
        mv = sb("cmv", [P, KT, BN2])
        dev = sb("cdev", [P, KT])
        dev2 = sb("cdev2", [P, KT])
        mean = sb("cmean", [P, KT])
        mhalf = sb("cmhalf", [P, KT])
        rstd = sb("crstd", [P, KT])
        veps = sb("cveps", [P, KT])
        qkf = sb("cqkf", [P, 2, 2 * KT, W])
        hi = sb("chi", [P, 2, 2 * KT, W], F32R)
        lo = sb("clo", [P, 2, 2 * KT, W], F32R)
        vi = sb("cvi", [P, 2, KT, W])
        vt = sb("cvt", [P, 2, SUB, CH])
        heads = sb("cheads", [P, P])
        heads16 = sb("cheads16", [P, P], BF16)
        ident = sb("cident", [P, P])
        squares = sb("csquares", [P, 2, 2 * KT, W], BF16)
        norms = sb("cnorms", [P, 2 * KT, B * NC])
        peaks = sb("cpeaks", [P, 2 * KT, B])
        bound = sb("cbound", [P, KT, B])
        worst = sb("cworst", [P, 1])
        worst_all = sb("cworst_all", [1, 1])
        NB_IMG, NB_TOK, NB_NORM = 3, 2, 2
        ps_img = [ctx.enter_context(nc.psum_tensor(f"cpi{i}", [P, 512], F32)) for i in range(NB_IMG)]
        ps_tok = [ctx.enter_context(nc.psum_tensor(f"cpt{i}", [P, 512], F32)) for i in range(NB_TOK)]
        ps_norm = [ctx.enter_context(nc.psum_tensor(f"cpn{i}", [P, 512], F32)) for i in range(NB_NORM)]
        ps_st = ctx.enter_context(nc.psum_tensor("cps", [P, 512], F32))

        consts_in = sem("c_consts_in")
        x_in = sem("c_x_in")
        xn_done = sem("c_xn_done")
        aggr_done = sem("c_aggr_done")
        mean_mm = sem("c_mean_mm")
        dev_done = sem("c_dev_done")
        var_mm = sem("c_var_mm")
        veps_done = sem("c_veps_done")
        rstd_done = sem("c_rstd_done")
        mhalf_done = sem("c_mhalf_done")
        dve_step = sem("c_dve_step")
        img_mm = sem("c_img_mm")
        img_out = sem("c_img_out")
        tok_mm = sem("c_tok_mm")
        tok_out = sem("c_tok_out")
        split_done = sem("c_split_done")
        heads_done = sem("c_heads_done")
        squares_done = sem("c_squares_done")
        norm_mm = sem("c_norm_mm")
        norm_done = sem("c_norm_done")
        worst_done = sem("c_worst_done")
        worst_mm = sem("c_worst_mm")
        stored = [sem(f"c_stored{i}") for i in range(2)]
        block = ctx.enter_context(nc.Block())
        MEAN_AT, VAR_AT = 2, 3
        MI, MQK = 3 * KT, 2 * KT
        SLOT_STORES = 6 * 16
        PREPARE = 4
        STEPS = PREPARE + NC

        @block.sync
        def _(sp):
            def load_x(b):
                sp.dma_start(x_sb[:], x[bass.ds(b, 1)].rearrange("a (k p) n -> p (a k) n", p=P)).then_inc(x_in, 16)

            load_x(0)
            sp.dma_start(wq[:], w_qkv.rearrange("(k p) n -> p k n", p=P)).then_inc(consts_in, 16)
            sp.dma_start(bq[:], b_qkv[:]).then_inc(consts_in, 16)
            sp.dma_start(bv[:], bv_row.partition_broadcast(P)).then_inc(consts_in, 16)
            sp.dma_start(gm[:], group_mean[:]).then_inc(consts_in, 16)
            sp.dma_start(heads[:], head_sum[:]).then_inc(consts_in, 16)
            sp.dma_start(ident[:], eye[:]).then_inc(consts_in, 16)

            def store_chunks(b):
                for c in range(NC):
                    s = c % 2
                    cols = slice(c * W, (c + 1) * W)
                    sp.wait_ge(tok_out, 1 + (b * NC + c) * SUB + SUB)
                    sp.dma_start(v_tok[bass.ds(b, 1), c * W:(c + 1) * W, :].rearrange("a (j p) n -> p (a j) n", p=P),
                                 vt[:, s]).then_inc(stored[s], 16)
                    sp.wait_ge(split_done, 1 + b * NC + c + 1)
                    for dram, part, m in ((qh, hi, 0), (kh, hi, KT), (ql, lo, 0), (kl, lo, KT)):
                        if m == 0:
                            to = dram.rearrange("(g c) p n -> g c p n", c=NC)[bass.ds(b * KT, KT), c]
                        else:
                            to = dram[bass.ds(b * KT, KT), :, cols]
                        sp.dma_start(to.rearrange("k p n -> p k n"),
                                     part[:, s, m:m + KT, :].bitcast(F32)).then_inc(stored[s], 16)
                    sp.wait_ge(img_out, 1 + (b * NC + c) * MI + MI)
                    sp.dma_start(v_img[bass.ds(b * KT, KT), :, cols].rearrange("k p n -> p k n"),
                                 vi[:, s]).then_inc(stored[s], 16)

            for counter in stored:
                sp.sem_inc(counter, 1)
            with sp.Fori(0, B - 1) as b:
                sp.wait_ge(xn_done, (b + 1) * NC)
                load_x(b + 1)
                store_chunks(b)
            store_chunks(B - 1)
            for s in range(2):
                sp.wait_ge(stored[s], 1 + B * (NC // 2) * SLOT_STORES)

        @block.vector
        def _(dve):
            for counter in (veps_done, tok_out, split_done, norm_done):
                dve.sem_inc(counter, 1)
            dve.sem_inc(norm_done, NB_NORM - 1)
            dve.wait_ge(consts_in, 6 * 16)
            nc.vector.tensor_copy(heads16[:], heads[:]).then_inc(heads_done, 1)

            def statistics(b, st):
                dve.wait_ge(x_in, b * 16 + 16)
                for k in range(KT):
                    for c in range(NC):
                        i = nc.vector.bn_stats(stats[:, k, c, :], x_sb[:, k, c * W:(c + 1) * W])
                st.then(i)
                nc.vector.memset(dev[:], 0.0)
                for k in range(KT):
                    i = nc.vector.bn_aggr(mv[:, k, :], stats[:, k].rearrange("p c s -> p (c s)"))
                i.then_inc(aggr_done, 1)

            def deviations(b, st):
                dve.wait_ge(mean_mm, b + 1)
                dve.wait_ge(aggr_done, b + 1)
                st.then(nc.vector.tensor_copy(mean[:], ps_st[:, 0:KT]))
                st.then(nc.vector.tensor_tensor(dev[:], mv[:, :, 0], mean[:], ALU.subtract))
                st.then(nc.vector.tensor_tensor(dev2[:], dev[:], dev[:], ALU.mult))
                nc.vector.tensor_tensor(dev2[:], dev2[:], mv[:, :, 1], ALU.add).then_inc(dev_done, 1)

            def variances(b):
                dve.wait_ge(var_mm, b + 1)
                nc.vector.tensor_scalar(veps[:], ps_st[:, 8:8 + KT], GN_EPS, None, ALU.add).then_inc(veps_done, 1)

            def normalise(b, chunks, last_used):
                dve.wait_ge(rstd_done, b + 1)
                for c in chunks:
                    if last_used:
                        dve.wait_ge(img_mm, 1 + ((b - 1) * NC + c + 1) * MI)
                        dve.wait_ge(tok_mm, 1 + ((b - 1) * NC + c + 1) * SUB)
                    for k in range(KT):
                        cols = slice(c * W, (c + 1) * W)
                        i = nc.vector.tensor_scalar(xn[:, k, cols], x_sb[:, k, cols], mean[:, k:k + 1], rstd[:, k:k + 1],
                                                    ALU.subtract, ALU.mult)
                    i.then_inc(xn_done, 1)

            def finish_chunk(b, c, st):
                s = c % 2
                if c < 2:
                    dve.wait_ge(stored[s], 1 + b * (NC // 2) * SLOT_STORES)
                else:
                    dve.wait_ge(stored[s], 1 + (b * (NC // 2) + c // 2) * SLOT_STORES)
                for j in range(SUB):
                    dve.wait_ge(tok_mm, 1 + (b * NC + c) * SUB + j + 1)
                    nc.vector.tensor_tensor(vt[:, s, j, :], ps_tok[(c * SUB + j) % NB_TOK][:, 0:CH], bv[:],
                                            ALU.add).then_inc(tok_out, 1)
                dve.wait_ge(img_out, 1 + (b * NC + c) * MI + MQK)
                st.then(nc.vector.tensor_copy(hi[:, s], qkf[:, s]))
                nc.vector.tensor_tensor(lo[:, s], qkf[:, s], hi[:, s].bitcast(F32), ALU.subtract).then_inc(split_done, 1)
                for m in range(MQK):
                    dve.wait_ge(norm_mm, 1 + MQK + (b * NC + c) * MQK + m + 1)
                    nc.vector.reduce_max(norms[:, m, bass.ds(b * NC + c, 1)], ps_norm[m % NB_NORM][:, 0:W],
                                         AX.X).then_inc(norm_done, 1)

            def one_batch(b, more):
                st = Steps(dve, dve_step, PREPARE + b * STEPS)
                for c in range(NC):
                    finish_chunk(b, c, st)
                    if more and c == 1:
                        statistics(b + 1, st)
                    if more and c == MEAN_AT:
                        deviations(b + 1, st)
                    if more and c == VAR_AT:
                        variances(b + 1)
                    if more and c == NC - 2:
                        normalise(b + 1, range(NC - 2), True)
                if more:
                    normalise(b + 1, range(NC - 2, NC), True)

            first = Steps(dve, dve_step)
            statistics(0, first)
            deviations(0, first)
            variances(0)
            normalise(0, range(NC), False)
            with dve.Fori(0, B - 1) as b:
                one_batch(b, True)
            one_batch(B - 1, False)
            st = Steps(dve, dve_step, PREPARE + (B - 1) * STEPS + NC)
            dve.wait_ge(norm_done, NB_NORM + B * NC * MQK)
            st.then(nc.vector.reduce_max(peaks[:], norms[:].rearrange("p m (b c) -> p m b c", b=B), AX.X))
            st.then(nc.vector.tensor_tensor(bound[:], peaks[:, 0:KT], peaks[:, KT:MQK], ALU.mult))
            nc.vector.reduce_max(worst[:], bound[:], AX.XY).then_inc(worst_done, 1)
            dve.wait_ge(worst_mm, 1)
            st.then(nc.vector.reduce_max(worst_all[:], ps_st[0:1, 128:256], AX.X))
            st.then(nc.vector.tensor_scalar(small_scores[:], worst_all[:], 0.98 * (MAX_SCORE / SCALE) ** 2, None, ALU.is_lt))

        @block.gpsimd
        def _(pool):
            nc.gpsimd.memset(mhalf[:], -0.5).then_inc(mhalf_done, 1)
            pool.wait_ge(mhalf_done, 1)
            with pool.Fori(0, B) as b:
                pool.wait_ge(veps_done, 1 + b + 1)
                nc.gpsimd.tensor_tensor(rstd[:], veps[:], mhalf[:], ALU.pow).then_inc(rstd_done, 1)

        @block.scalar
        def _(act):
            act.sem_inc(img_out, 1)
            with act.Fori(0, B) as b:
                for c in range(NC):
                    s = c % 2
                    act.wait_ge(stored[s], 1 + (b * (NC // 2) + c // 2) * SLOT_STORES)
                    act.wait_ge(split_done, 1 + b * NC + c - 1) if c else act.wait_ge(split_done, 1 + b * NC)
                    for m in range(MI):
                        act.wait_ge(img_mm, 1 + (b * NC + c) * MI + m + 1)
                        dst = qkf[:, s, m, :] if m < MQK else vi[:, s, m - MQK, :]
                        src = ps_img[(c * MI + m) % NB_IMG][:, 0:W]
                        if m == 0:
                            act.wait_ge(norm_mm, 1 + (b * NC + c) * MQK)
                        if m < MQK:
                            nc.scalar.activation(squares[:, s, m, :], src, ACT.Square, bias=bq[:, m:m + 1]
                                                 ).then_inc(squares_done, 1)
                        nc.scalar.activation(dst, src, ACT.Identity, bias=bq[:, m:m + 1]).then_inc(img_out, 1)

        @block.tensor
        def _(pe):
            for counter in (img_mm, tok_mm, norm_mm):
                pe.sem_inc(counter, 1)
            pe.sem_inc(norm_mm, MQK)
            pe.wait_ge(consts_in, 6 * 16)
            pe.wait_ge(heads_done, 1)

            def group_means(b):
                pe.wait_ge(aggr_done, b + 1)
                pe.wait_ge(veps_done, 1 + b)
                nc.tensor.matmul(ps_st[:, 0:KT], gm[:], mv[:, :, 0], start=True, stop=True).then_inc(mean_mm, 1)

            def group_variances(b):
                pe.wait_ge(dev_done, b + 1)
                nc.tensor.matmul(ps_st[:, 8:8 + KT], gm[:], dev2[:], start=True, stop=True).then_inc(var_mm, 1)

            def norm_products(b, c):
                for m in range(MQK):
                    u = (b * NC + c) * MQK + m
                    pe.wait_ge(squares_done, u + 1)
                    pe.wait_ge(norm_done, 1 + u)
                    nc.tensor.matmul(ps_norm[m % NB_NORM][:, 0:W], heads16[:], squares[:, c % 2, m, :],
                                     start=True, stop=True).then_inc(norm_mm, 1)

            def one_batch(b, more):
                for c in range(NC):
                    pe.wait_ge(xn_done, b * NC + c + 1)
                    cols = slice(c * W, (c + 1) * W)
                    for m in range(MI):
                        u = c * MI + m
                        if u >= NB_IMG:
                            pe.wait_ge(img_out, 1 + b * NC * MI + u - NB_IMG + 1)
                        else:
                            pe.wait_ge(img_out, 1 + b * NC * MI)
                        for k in range(KT):
                            i = nc.tensor.matmul(ps_img[u % NB_IMG][:, 0:W], wq[:, k, m * P:(m + 1) * P], xn[:, k, cols],
                                                 start=(k == 0), stop=(k == KT - 1))
                        i.then_inc(img_mm, 1)
                        if m == 1 and c > 0:
                            norm_products(b, c - 1)
                        if m % 2:
                            j = m // 2
                            u = c * SUB + j
                            if u >= NB_TOK:
                                pe.wait_ge(tok_out, 1 + b * NC * SUB + u - NB_TOK + 1)
                            else:
                                pe.wait_ge(tok_out, 1 + b * NC * SUB)
                            for k in range(KT):
                                i = nc.tensor.matmul(ps_tok[u % NB_TOK][:, 0:CH], xn[:, k, c * W + j * P:c * W + (j + 1) * P],
                                                     wq[:, k, 2 * CH:3 * CH], start=(k == 0), stop=(k == KT - 1))
                            i.then_inc(tok_mm, 1)
                    if c == NC - 1:
                        norm_products(b, c)
                    if more and c == MEAN_AT:
                        group_means(b + 1)
                    if more and c == VAR_AT:
                        group_variances(b + 1)

            group_means(0)
            group_variances(0)
            with pe.Fori(0, B - 1) as b:
                one_batch(b, True)
            one_batch(B - 1, False)
            pe.wait_ge(worst_done, 1)
            nc.tensor.transpose(ps_st[0:1, 128:256], worst[:], ident[:]).then_inc(worst_mm, 1)


def conv_attention(nc, qh, ql, kh, kl, v_img, v_tok, w_pe, b_pe, eye, small_scores, attn, pe_img):
    with ExitStack() as ctx:
        def sb(name, shape, dt=F32):
            return ctx.enter_context(nc.sbuf_tensor(name, shape, dt))

        def sem(name):
            return ctx.enter_context(nc.semaphore(name))

        G3 = NT // SUB
        NP_SLOTS = 2 * HG
        MAXES = HG * SUB * 2
        UNITS = G3 * HG
        ADDS = (G3 - 1) * HG
        EARLY = HG + 1
        CHUNKS = BG * NC
        k_sb = sb("ak", [P, KT, HG, N], F32R)
        v_sb = sb("av", [P, KT, NT, P])
        q_sb = sb("aq", [P, 2, HG, W], F32R)
        probs = sb("aprobs", [P, NP_SLOTS, SUB, W])
        sums = sb("asums", [P, HG, SUB, W])
        mx = sb("amx", [P, 2, HG * SUB])
        top = sb("atop", [P, HG * SUB])
        diag = sb("adiag", [P, HG, W])
        ident = sb("aident", [P, P])
        minus = sb("aminus", [P, P])
        ones = sb("aones", [P, HD])
        rden = sb("arden", [P, W])
        o_sb = sb("ao", [P, 2, W])
        vc = sb("avc", [P, IMG, IMG])
        tap = sb("atap", [P, IMG, IMG])
        conv = sb("aconv", [P, IMG, IMG])
        wpe = sb("awpe", [P, KT, 9])
        bpe = sb("abpe", [P, KT])
        ps_s = [ctx.enter_context(nc.psum_tensor(f"ass{i}", [P, SUB, 512], F32)) for i in range(2)]
        ps_o = ctx.enter_context(nc.psum_tensor("aso", [P, 512], F32))
        ps_d = ctx.enter_context(nc.psum_tensor("asd", [P, 512], F32))

        consts_in = sem("a_consts_in")
        taps_in = sem("a_taps_in")
        consts_set = sem("a_consts_set")
        kv_in = [sem(f"a_kv_in{g}") for g in range(KT)]
        q_in = [sem(f"a_q_in{i}") for i in range(2)]
        max_mm = sem("a_max_mm")
        max_done = sem("a_max_done")
        diag_done = sem("a_diag_done")
        top_done = sem("a_top_done")
        score_mm = sem("a_score_mm")
        exp_done = sem("a_exp_done")
        add_done = sem("a_add_done")
        pv_done = sem("a_pv_done")
        den_mm = sem("a_den_mm")
        raw_done = sem("a_raw_done")
        den_read = sem("a_den_read")
        out_done = sem("a_out_done")
        o_stored = [sem(f"a_o_stored{i}") for i in range(2)]
        img_in = sem("a_img_in")
        pool_step = sem("a_pool_step")
        conv_stored = sem("a_conv_stored")
        block = ctx.enter_context(nc.Block())

        @block.sync
        def _(sp):
            for counter in o_stored:
                sp.sem_inc(counter, 1)
            sp.dma_start(ident[:], eye[:]).then_inc(consts_in, 16)

            def load_kv(b, g):
                for r, part in enumerate((kh, kl, kh, kl)):
                    sp.dma_start(k_sb[r * HD:(r + 1) * HD, g].bitcast(F32),
                                 part[bass.ds(b * KT + g, 1)].rearrange("a (h d) n -> d (a h) n", d=HD)).then_inc(kv_in[g], 16)
                sp.dma_start(v_sb[:, g], v_tok[bass.ds(b, 1), :, g * P:(g + 1) * P].rearrange("a (t p) c -> p (a t) c", p=P)
                             ).then_inc(kv_in[g], 16)

            def load_q(n, i):
                for r, part in enumerate((qh, qh, ql, ql)):
                    sp.dma_start(q_sb[r * HD:(r + 1) * HD, i].bitcast(F32),
                                 part[bass.ds(n, 1)].rearrange("a (h d) n -> d (a h) n", d=HD)).then_inc(q_in[i], 16)

            def store_out(n, i):
                sp.wait_ge(out_done, 1 + n + 1)
                sp.dma_start(attn[bass.ds(n, 1)].rearrange("a p n -> p (a n)"), o_sb[:, i]).then_inc(o_stored[i], 16)

            def one_batch(b, last):
                for c in range(KT * NC):
                    n = b * KT * NC + c
                    if not (last and c == KT * NC - 1):
                        load_q(n + 1, (c + 1) % 2)
                    store_out(n, c % 2)
                    if c % NC == NC - 1 and not last:
                        load_kv(b + 1, c // NC)

            load_kv(0, 0)
            load_q(0, 0)
            load_kv(0, 1)
            with sp.Fori(0, B - 1) as b:
                one_batch(b, False)
            one_batch(B - 1, True)
            for i in range(2):
                sp.wait_ge(o_stored[i], 1 + CHUNKS // 2 * 16)

        @block.gpsimd
        def _(pool):
            pool.dma_start(wpe[:], w_pe.rearrange("(k p) t -> p k t", p=P)).then_inc(taps_in, 16)
            pool.dma_start(bpe[:], b_pe[:]).then_inc(taps_in, 16)
            pool.wait_ge(taps_in, 32)
            nc.gpsimd.memset(minus[:], -1.0).then_inc(consts_set, 1)
            nc.gpsimd.memset(ones[:], 1.0).then_inc(consts_set, 1)
            with pool.Fori(0, B) as b:
                for g in range(KT):
                    st = Steps(pool, pool_step, (b * KT + g) * 18)
                    pool.wait_ge(img_in, (b * KT + g + 1) * 16)
                    order = [4, 0, 1, 2, 3, 5, 6, 7, 8]
                    for t in order:
                        dy, dx = t // 3 - 1, t % 3 - 1
                        y0, y1 = max(0, -dy), IMG - max(0, dy)
                        x0, x1 = max(0, -dx), IMG - max(0, dx)
                        tap_w = wpe[:, g, t:t + 1].to_broadcast([P, N])
                        if t == 4:
                            pool.wait_ge(conv_stored, 1 + (b * KT + g) * 16)
                            st.then(nc.gpsimd.tensor_tensor(conv[:].rearrange("p y x -> p (y x)"), vc[:].rearrange("p y x -> p (y x)"),
                                                            tap_w, ALU.mult))
                            st.then(nc.gpsimd.tensor_tensor(conv[:].rearrange("p y x -> p (y x)"), conv[:].rearrange("p y x -> p (y x)"),
                                                            bpe[:, g:g + 1].to_broadcast([P, N]), ALU.add))
                        else:
                            st.then(nc.gpsimd.tensor_tensor(tap[:].rearrange("p y x -> p (y x)"), vc[:].rearrange("p y x -> p (y x)"),
                                                            tap_w, ALU.mult))
                            st.then(nc.gpsimd.tensor_tensor(conv[:, y0:y1, x0:x1], conv[:, y0:y1, x0:x1],
                                                            tap[:, y0 + dy:y1 + dy, x0 + dx:x1 + dx], ALU.add))
                    assert st.n == 18

        @block.vector
        def _(dve):
            for counter in (max_done, add_done, raw_done, den_read, out_done):
                dve.sem_inc(counter, 1)
            dve.sem_inc(add_done, HG)
            dve.wait_ge(consts_in, 16)

            def take_maxima(n):
                for u in range(MAXES):
                    dve.wait_ge(max_mm, 1 + n * MAXES + u + 1)
                    nc.vector.reduce_max(mx[:, u % 2, u // 2:u // 2 + 1], ps_s[u % 2][:, :, 0:W], AX.XY).then_inc(max_done, 1)
                dve.wait_ge(max_done, 1 + n * MAXES + MAXES)
                nc.vector.tensor_tensor(top[:], mx[:, 0], mx[:, 1], ALU.max).then_inc(top_done, 1)
                dve.wait_ge(top_done, n + 1)
                for h in range(HG):
                    for j in range(SUB):
                        last = nc.vector.tensor_scalar(diag[:, h, j * P:(j + 1) * P], ident[:], top[:, h * SUB + j:h * SUB + j + 1],
                                                       None, ALU.mult)
                last.then_inc(diag_done, 1)

            def add_probs(n, g3):
                for h in range(HG):
                    u = g3 * HG + h
                    dve.wait_ge(exp_done, 3 + n * UNITS + u + 1)
                    if g3 == 1:
                        first = probs[:, h]
                        dve.wait_ge(den_mm, 1 + n)
                    else:
                        first = sums[:, h]
                        dve.wait_ge(add_done, 1 + HG + n * ADDS + (g3 - 2) * HG + h + 1)
                    nc.vector.tensor_tensor(sums[:, h], first, probs[:, u % NP_SLOTS], ALU.add).then_inc(add_done, 1)

            def start_chunk(n, shifted):
                if shifted:
                    take_maxima(n)
                add_probs(n, 1)

            def finish_chunk(n, pair, i, shifted, more):
                for g3 in range(2, G3):
                    add_probs(n, g3)
                dve.wait_ge(pv_done, 3 + n * G3 + G3)
                dve.wait_ge(o_stored[i], 1 + pair * 16)
                nc.vector.tensor_copy(o_sb[:, i], ps_o[:, 0:W]).then_inc(raw_done, 1)
                if more:
                    start_chunk(n + 1, shifted)
                dve.wait_ge(den_mm, 1 + n + 1)
                nc.vector.reciprocal(rden[:], ps_d[:, 0:W]).then_inc(den_read, 1)
                dve.wait_ge(den_read, 1 + n + 1)
                dve.wait_ge(raw_done, 1 + n + 1)
                nc.vector.tensor_tensor(o_sb[:, i], o_sb[:, i], rden[:], ALU.mult).then_inc(out_done, 1)

            def attend(shifted):
                start_chunk(0, shifted)
                with dve.Fori(0, CHUNKS // 2 - 1) as pair:
                    for i in range(2):
                        finish_chunk(pair * 2 + i, pair, i, shifted, True)
                finish_chunk(CHUNKS - 2, CHUNKS // 2 - 1, 0, shifted, True)
                finish_chunk(CHUNKS - 1, CHUNKS // 2 - 1, 1, shifted, False)

            small = dve.value_load(small_scores[0:1, 0:1], min_val=0, max_val=1)
            with dve.If(small):
                attend(False)
            with dve.Else():
                attend(True)

        @block.scalar
        def _(act):
            act.sem_inc(exp_done, 3)
            act.sem_inc(conv_stored, 1)
            FREED = {0: 0, 1: 4, 2: 8, 3: 8, 4: 12, 5: 16}
            with act.Fori(0, B) as b:
                for g in range(KT):
                    act.dma_start(vc[:].rearrange("p y x -> p (y x)"),
                                  v_img[bass.ds(b * KT + g, 1)].rearrange("a p n -> p (a n)")).then_inc(img_in, 16)
                    with act.Fori(0, NC // 2) as cp:
                        for i in range(2):
                            n = (b * KT + g) * NC + cp * 2 + i
                            for u in range(UNITS):
                                if u % HG == 0:
                                    act.wait_ge(pv_done, 1 + n * G3 + u // HG + 1)
                                    act.wait_ge(add_done, 1 + n * ADDS + FREED[u // HG])
                                act.wait_ge(score_mm, 1 + n * UNITS + u + 1)
                                nc.scalar.activation(probs[:, u % NP_SLOTS], ps_s[u % 2][:, :, 0:W], ACT.Exp, scale=SCALE
                                                     ).then_inc(exp_done, 1)
                    act.wait_ge(pool_step, (b * KT + g + 1) * 18)
                    act.dma_start(pe_img[bass.ds(b * KT + g, 1)].rearrange("a p n -> p (a n)"),
                                  conv[:].rearrange("p y x -> p (y x)")).then_inc(conv_stored, 16)
            act.wait_ge(conv_stored, 1 + BG * 16)

        @block.tensor
        def _(pe):
            for counter in (max_mm, score_mm, pv_done, den_mm):
                pe.sem_inc(counter, 1)
            pe.sem_inc(pv_done, 2)
            pe.wait_ge(consts_set, 2)
            def first_pass(n, g, i):
                for u in range(MAXES):
                    h, j, half = u // (2 * SUB), u // 2 % SUB, u % 2
                    if u < 2:
                        pe.wait_ge(exp_done, 3 + n * UNITS)
                    else:
                        pe.wait_ge(max_done, 1 + n * MAXES + u - 1)
                    for a in range(SUB):
                        key = (half * SUB + a) * W
                        last = nc.tensor.matmul(ps_s[u % 2][:, a, 0:W], q_sb[:, i, h, j * P:(j + 1) * P],
                                                k_sb[:, g, h, key:key + W], start=True, stop=True)
                    last.then_inc(max_mm, 1)
                pe.wait_ge(max_done, 1 + n * MAXES + MAXES)
                pe.wait_ge(diag_done, n + 1)

            def scores(n, g, i, u, shifted):
                g3, h = u // HG, u % HG
                if u >= 2 or not shifted:
                    pe.wait_ge(exp_done, 1 + n * UNITS + u + 1)
                for a in range(SUB):
                    key = (g3 * SUB + a) * P
                    last = nc.tensor.matmul(ps_s[u % 2][:, a, 0:W], k_sb[:, g, h, key:key + P], q_sb[:, i, h, :],
                                            start=True, stop=not shifted)
                    if shifted:
                        last = nc.tensor.matmul(ps_s[u % 2][:, a, 0:W], minus[:], diag[:, h, :], start=False, stop=True)
                last.then_inc(score_mm, 1)

            def values(n, g, g3, a):
                kt = g3 * SUB + a
                for h in range(HG):
                    u = g3 * HG + h
                    if a == 0:
                        pe.wait_ge(exp_done, 3 + n * UNITS + u + 1)
                    if kt == 0 and h == 0:
                        pe.wait_ge(raw_done, 1 + n)
                    last = nc.tensor.matmul(ps_o[h * HD:(h + 1) * HD, 0:W], v_sb[:, g, kt, h * HD:(h + 1) * HD],
                                            probs[:, u % NP_SLOTS, a, :], start=(kt == 0), stop=(kt == NT - 1))
                if a == SUB - 1:
                    last.then_inc(pv_done, 1)

            def denominators(n):
                pe.wait_ge(add_done, 1 + HG + n * ADDS + ADDS)
                pe.wait_ge(den_read, 1 + n)
                for a in range(SUB):
                    for h in range(HG):
                        last = nc.tensor.matmul(ps_d[h * HD:(h + 1) * HD, 0:W], ones[:], sums[:, h, a, :],
                                                start=(a == 0), stop=(a == SUB - 1))
                last.then_inc(den_mm, 1)

            def middle(n, g, i, shifted):
                for g3 in range(1, G3):
                    for h in range(HG):
                        if g3 * HG + h >= EARLY:
                            scores(n, g, i, g3 * HG + h, shifted)
                        if h >= HG - SUB:
                            values(n, g, g3 - 1, h - (HG - SUB))

            def wait_inputs(b, g, cp, i):
                pe.wait_ge(kv_in[g], (b + 1) * 5 * 16)
                pe.wait_ge(q_in[i], ((b * KT + g) * (NC // 2) + cp + 1) * 4 * 16)

            def chunk_number(b, g, cp, i):
                return (b * KT + g) * NC + cp * 2 + i

            def attend_shifted():
                with pe.Fori(0, B) as b:
                    for g in range(KT):
                        with pe.Fori(0, NC // 2) as cp:
                            for i in range(2):
                                n = chunk_number(b, g, cp, i)
                                wait_inputs(b, g, cp, i)
                                first_pass(n, g, i)
                                for u in range(EARLY):
                                    scores(n, g, i, u, True)
                                middle(n, g, i, True)
                                for a in range(SUB):
                                    values(n, g, G3 - 1, a)
                                denominators(n)

            def middle_and_end(this, following):
                n, g = chunk_number(*this), this[1]
                middle(n, g, this[3], False)
                if following:
                    wait_inputs(*following)
                for u in range(EARLY):
                    if following:
                        scores(chunk_number(*following), following[1], following[3], u, False)
                    if u < SUB:
                        values(n, g, G3 - 1, u)
                denominators(n)

            def group(b, g, following):
                LAST = NC // 2 - 1
                with pe.Fori(0, LAST) as cp:
                    middle_and_end((b, g, cp, 0), (b, g, cp, 1))
                    middle_and_end((b, g, cp, 1), (b, g, cp + 1, 0))
                middle_and_end((b, g, LAST, 0), (b, g, LAST, 1))
                middle_and_end((b, g, LAST, 1), following)

            def attend_small():
                wait_inputs(0, 0, 0, 0)
                for u in range(EARLY):
                    scores(0, 0, 0, u, False)
                with pe.Fori(0, B - 1) as b:
                    for g in range(KT):
                        group(b, g, (b, g + 1, 0, 0) if g < KT - 1 else (b + 1, 0, 0, 0))
                for g in range(KT):
                    group(B - 1, g, (B - 1, g + 1, 0, 0) if g < KT - 1 else None)

            small = pe.value_load(small_scores[0:1, 0:1], min_val=0, max_val=1)
            with pe.If(small):
                attend_small()
            with pe.Else():
                attend_shifted()
def project_and_norm(nc, attn, pe_img, x, w_proj, bp_row, eye, w_key, temperature, bias, near_only, t1, xn_tok, xn_ch, key_ch):
    with ExitStack() as ctx:
        def sb(name, shape, dt=F32):
            return ctx.enter_context(nc.sbuf_tensor(name, shape, dt))

        def sem(name):
            return ctx.enter_context(nc.semaphore(name))

        CHUNKS = B * NC
        SLOTS = 3
        a_in = sb("pa", [P, SLOTS, KT, W])
        c_in = sb("pc", [P, SLOTS, KT, W])
        x_in = sb("px", [P, SLOTS, KT, W])
        both = sb("pboth", [P, 2, KT, W])
        wp = sb("pwp", [P, KT, CH])
        wk = sb("pwk", [P, KT, CH])
        bp = sb("pbp", [P, CH])
        ident = sb("pident", [P, P])
        tok = sb("ptok", [P, 2, SUB, CH])
        xn = sb("pxn", [P, 2, SUB, CH])
        xt = sb("pxt", [P, 2, KT, W])
        key = sb("pkey", [P, 2, KT, W])
        stats = sb("pstats", [P, SUB, BN6])
        mv = sb("pmv", [P, SUB, BN2])
        veps = sb("pveps", [P, SUB])
        rstd = sb("prstd", [P, SUB])
        mhalf = sb("pmhalf", [P, SUB])
        squares = sb("psquares", [P, KT, W], BF16)
        ones16 = sb("pones16", [P, P], BF16)
        norms = sb("pnorms", [P, CHUNKS])
        temp = sb("ptemp", [P, 1])
        bcol = sb("pbcol", [P, 1])
        test = sb("ptest", [P, 6])
        ps_t = [ctx.enter_context(nc.psum_tensor(f"ppt{i}", [P, 512], F32)) for i in range(SUB)]
        ps_x = [ctx.enter_context(nc.psum_tensor(f"ppx{i}", [P, 512], F32)) for i in range(KT)]
        ps_k = [ctx.enter_context(nc.psum_tensor(f"ppk{i}", [P, 512], F32)) for i in range(KT)]

        ps_n = ctx.enter_context(nc.psum_tensor("ppn", [P, 512], F32))
        ones_done = sem("p_ones_done")
        squares_done = sem("p_squares_done")
        norm_mm = sem("p_norm_mm")
        norm_done = sem("p_norm_done")
        consts_in = sem("p_consts_in")
        mhalf_done = sem("p_mhalf_done")
        chunk_in = [sem(f"p_chunk_in{i}") for i in range(SLOTS)]
        both_done = sem("p_both_done")
        tok_mm = sem("p_tok_mm")
        tok_done = sem("p_tok_done")
        dve_step = sem("p_dve_step")
        veps_done = sem("p_veps_done")
        rstd_done = sem("p_rstd_done")
        xn_done = sem("p_xn_done")
        xt_mm = sem("p_xt_mm")
        xt_done = sem("p_xt_done")
        key_mm = sem("p_key_mm")
        key_done = sem("p_key_done")
        stored = [sem(f"p_stored{i}") for i in range(2)]
        block = ctx.enter_context(nc.Block())
        STEPS = 3
        AHEAD = 1 + 2 * SUB
        ROUNDS = NC // SLOTS

        @block.sync
        def _(sp):
            sp.dma_start(wp[:], w_proj.rearrange("(k p) n -> p k n", p=P)).then_inc(consts_in, 16)
            sp.dma_start(wk[:], w_key.rearrange("(k p) n -> p k n", p=P)).then_inc(consts_in, 16)
            sp.dma_start(bp[:], bp_row.partition_broadcast(P)).then_inc(consts_in, 16)
            sp.dma_start(ident[:], eye[:]).then_inc(consts_in, 16)
            sp.dma_start(temp[:], temperature.partition_broadcast(P)).then_inc(consts_in, 16)
            sp.dma_start(bcol[:], bias.partition_broadcast(P)).then_inc(consts_in, 16)
            for counter in stored:
                sp.sem_inc(counter, 1)
            by_chunk = attn.rearrange("(g c) p n -> g c p n", c=NC)
            with sp.Fori(0, B) as b:
                for c in range(NC):
                    i = c % SLOTS
                    cols = slice(c * W, (c + 1) * W)
                    sp.wait_ge(tok_mm, AHEAD + (b * NC + c - SLOTS) * SUB + SUB)
                    for dst, src in ((a_in, by_chunk[bass.ds(b * KT, KT), c]),
                                     (c_in, pe_img[bass.ds(b * KT, KT), :, cols]),
                                     (x_in, x[bass.ds(b, 1), :, cols].rearrange("a (k p) n -> (a k) p n", p=P))):
                        sp.dma_start(dst[:, i], src.rearrange("k p n -> p k n")).then_inc(chunk_in[i], 16)

        @block.gpsimd
        def _(pool):
            nc.gpsimd.memset(ones16[:], 1.0).then_inc(ones_done, 1)
            nc.gpsimd.memset(mhalf[:], -0.5).then_inc(mhalf_done, 1)
            pool.wait_ge(mhalf_done, 1)
            with pool.Fori(0, CHUNKS) as n:
                pool.wait_ge(veps_done, n + 1)
                nc.gpsimd.tensor_tensor(rstd[:], veps[:], mhalf[:], ALU.pow).then_inc(rstd_done, 1)

        @block.vector
        def _(dve):
            dve.sem_inc(tok_done, 1)
            dve.sem_inc(xn_done, 1)
            dve.sem_inc(norm_done, 1)
            dve.wait_ge(consts_in, 6 * 16)

            def add_parts(b, c):
                dve.wait_ge(chunk_in[c % SLOTS], (b * ROUNDS + c // SLOTS + 1) * 3 * 16)
                nc.vector.tensor_tensor(both[:, c % 2], a_in[:, c % SLOTS], c_in[:, c % SLOTS], ALU.add).then_inc(both_done, 1)

            def tokens(b, c, last):
                n, i = b * NC + c, c % 2
                st = Steps(dve, dve_step, n * STEPS)
                dve.wait_ge(stored[i], 1 + (b * (NC // 2) + c // 2) * 4 * 16)
                for j in range(SUB):
                    dve.wait_ge(tok_mm, AHEAD + n * SUB + j + 1)
                    nc.vector.tensor_tensor(tok[:, i, j], ps_t[j][:, 0:CH], bp[:], ALU.add).then_inc(tok_done, 1)
                dve.wait_ge(tok_done, 1 + (n + 1) * SUB)
                for j in range(SUB):
                    step = nc.vector.bn_stats(stats[:, j], tok[:, i, j])
                st.then(step)
                nc.vector.memset(veps[:], 0.0)
                for j in range(SUB):
                    step = nc.vector.bn_aggr(mv[:, j], stats[:, j])
                st.then(step)
                nc.vector.tensor_scalar(veps[:], mv[:, :, 1], LN_EPS, None, ALU.add).then_inc(veps_done, 1)
                if not last:
                    add_parts(*((b, c + 1) if c < NC - 1 else (b + 1, 0)))
                dve.wait_ge(rstd_done, n + 1)
                dve.wait_ge(xt_mm, 1 + n * KT)
                for j in range(SUB):
                    step = nc.vector.tensor_scalar(xn[:, i, j], tok[:, i, j], mv[:, j, 0:1], rstd[:, j:j + 1],
                                                   ALU.subtract, ALU.mult)
                st.then(step)
                dve.sem_inc(xn_done, 1)
                assert st.n == STEPS
                if c:
                    take_norm(n - 1)

            def take_norm(n):
                dve.wait_ge(norm_mm, 1 + n + 1)
                nc.vector.reduce_max(norms[:, bass.ds(n, 1)], ps_n[:, 0:W], AX.X).then_inc(norm_done, 1)

            def tokens_of_batch(b, last):
                for c in range(NC):
                    tokens(b, c, last and c == NC - 1)
                take_norm(b * NC + NC - 1)

            add_parts(0, 0)
            with dve.Fori(0, B - 1) as b:
                tokens_of_batch(b, False)
            tokens_of_batch(B - 1, True)
            st = Steps(dve, dve_step, CHUNKS * STEPS)
            dve.wait_ge(norm_done, 1 + CHUNKS)
            st.then(nc.vector.reduce_max(test[:, 0:1], norms[:], AX.X))
            st.then(nc.vector.tensor_scalar(test[:, 1:2], temp[:], 1e-6, None, ALU.max))
            st.then(nc.vector.reciprocal(test[:, 2:3], test[:, 1:2]))
            st.then(nc.vector.tensor_scalar(test[:, 1:2], test[:, 2:3], -UNDERFLOW, OUTSIDE, ALU.mult, ALU.add))
            st.then(nc.vector.tensor_scalar(test[:, 2:3], bcol[:], -1.0, None, ALU.mult))
            st.then(nc.vector.tensor_tensor(test[:, 3:4], bcol[:], test[:, 2:3], ALU.max))
            st.then(nc.vector.tensor_tensor(test[:, 4:5], test[:, 1:2], test[:, 3:4], ALU.subtract))
            st.then(nc.vector.tensor_scalar(test[:, 4:5], test[:, 4:5], 0.0, None, ALU.max))
            st.then(nc.vector.tensor_tensor(test[:, 5:6], test[:, 4:5], test[:, 4:5], ALU.mult))
            st.then(nc.vector.tensor_scalar(test[:, 0:1], test[:, 0:1], 1.04 * CH, None, ALU.mult))
            st.then(nc.vector.tensor_tensor(near_only[:], test[0:1, 0:1], test[0:1, 5:6], ALU.is_lt))

        @block.scalar
        def _(act):
            act.sem_inc(xt_done, 1)
            act.sem_inc(key_done, 1)
            act.wait_ge(mhalf_done, 1)
            with act.Fori(0, B) as b:
                for c in range(NC):
                    i = c % 2
                    n = b * NC + c
                    cols = slice(c * W, (c + 1) * W)
                    rows = slice(c * W, (c + 1) * W)
                    act.wait_ge(stored[i], 1 + (b * (NC // 2) + c // 2) * 4 * 16)
                    for k in range(KT):
                        act.wait_ge(xt_mm, 1 + n * KT + k + 1)
                        nc.scalar.activation(xt[:, i, k], ps_x[k][:, 0:W], ACT.Identity).then_inc(xt_done, 1)
                    for k in range(KT):
                        act.wait_ge(key_mm, 1 + n * KT + k + 1)
                        if k == 0:
                            act.wait_ge(norm_mm, 1 + n)
                        nc.scalar.activation(squares[:, k], ps_k[k][:, 0:W], ACT.Square).then_inc(squares_done, 1)
                        nc.scalar.activation(key[:, i, k], ps_k[k][:, 0:W], ACT.Identity).then_inc(key_done, 1)
                    act.wait_ge(xn_done, 1 + n + 1)
                    for dram, src in ((t1, tok), (xn_tok, xn)):
                        act.dma_start(dram[bass.ds(b, 1), rows].rearrange("a (j p) n -> p (a j) n", p=P), src[:, i]
                                      ).then_inc(stored[i], 16)
                    act.wait_ge(key_done, 1 + (n + 1) * KT)
                    act.wait_ge(xt_done, 1 + (n + 1) * KT)
                    for dram, src in ((xn_ch, xt), (key_ch, key)):
                        act.dma_start(dram[bass.ds(b * KT, KT), :, cols].rearrange("k p n -> p k n"), src[:, i]
                                      ).then_inc(stored[i], 16)
            for i in range(2):
                act.wait_ge(stored[i], 1 + CHUNKS // 2 * 4 * 16)

        @block.tensor
        def _(pe):
            for counter in (tok_mm, xt_mm, key_mm, norm_mm):
                pe.sem_inc(counter, 1)
            pe.sem_inc(tok_mm, AHEAD - 1)
            pe.wait_ge(consts_in, 6 * 16)
            pe.wait_ge(ones_done, 1)

            def project(b, c):
                n, i, slot = b * NC + c, c % 2, c % SLOTS
                pe.wait_ge(both_done, n + 1)
                pe.wait_ge(chunk_in[slot], (b * ROUNDS + c // SLOTS + 1) * 3 * 16)
                for j in range(SUB):
                    pe.wait_ge(tok_done, 1 + n * SUB)
                    part = slice(j * P, (j + 1) * P)
                    for k in range(KT):
                        nc.tensor.matmul(ps_t[j][:, k * P:(k + 1) * P], x_in[:, slot, k, part], ident[:],
                                         start=(k == 0), stop=False, skip_group_check=True)
                    for k in range(KT):
                        last = nc.tensor.matmul(ps_t[j][:, 0:CH], both[:, i, k, part], wp[:, k, :],
                                                start=False, stop=(k == KT - 1), skip_group_check=True)
                    last.then_inc(tok_mm, 1)

            def norm_products(n, i):
                pe.wait_ge(xn_done, 1 + n + 1)
                for k in range(KT):
                    pe.wait_ge(xt_done, 1 + n * KT)
                    for j in range(SUB):
                        last = nc.tensor.transpose(ps_x[k][:, j * P:(j + 1) * P], xn[:, i, j, k * P:(k + 1) * P], ident[:])
                    last.then_inc(xt_mm, 1)
                pe.wait_ge(xt_done, 1 + (n + 1) * KT)
                for m in range(KT):
                    pe.wait_ge(key_done, 1 + n * KT)
                    for k in range(KT):
                        last = nc.tensor.matmul(ps_k[m][:, 0:W], wk[:, k, m * P:(m + 1) * P], xt[:, i, k, :],
                                                start=(k == 0), stop=(k == KT - 1))
                    last.then_inc(key_mm, 1)
                pe.wait_ge(squares_done, (n + 1) * KT)
                pe.wait_ge(norm_done, 1 + n)
                for k in range(KT):
                    last = nc.tensor.matmul(ps_n[:, 0:W], ones16[:], squares[:, k], start=(k == 0), stop=(k == KT - 1))
                last.then_inc(norm_mm, 1)

            def products_of_batch(b, last):
                for c in range(NC):
                    if not (last and c == NC - 1):
                        project(*((b, c + 1) if c < NC - 1 else (b + 1, 0)))
                    norm_products(b * NC + c, c % 2)

            project(0, 0)
            with pe.Fori(0, B - 1) as b:
                products_of_batch(b, False)
            products_of_batch(B - 1, True)


def near_attention(nc, t1, xn_tok, xn_ch, key_ch, near_masks, temperature, bias, eye, near_only, t2, t2_stats):
    with ExitStack() as ctx:
        def sb(name, shape, dt=F32):
            return ctx.enter_context(nc.sbuf_tensor(name, shape, dt))

        def sem(name):
            return ctx.enter_context(nc.semaphore(name))

        BEFORE = WINDOW // 2
        SPAN = P + WINDOW
        near = sb("nnear", [P, 3, SUB * SPAN])
        temp = sb("ntemp", [P, 1])
        bcol = sb("nbcol", [P, 1])
        ident = sb("nident", [P, P])
        SLOTS = 3
        keys = sb("nkeys", [P, SLOTS, KT, W])
        xw = sb("nxw", [P, SLOTS, KT, W + WINDOW])
        vw = sb("nvw", [P, SLOTS, SUB + 1, CH])
        t1_sb = sb("nt1", [P, SLOTS, SUB, CH])
        logit = sb("nlogit", [P, SUB, SPAN])
        prob = sb("nprob", [P, 2, SUB, SPAN])
        body_t = sb("nbody_t", [P, W])
        tail_t = sb("ntail_t", [WINDOW, W])
        mx = sb("nmx", [P, SUB])
        nmx = sb("nnmx", [P, SUB])
        rs = sb("nrs", [P, 2, SUB])
        rrs = sb("nrrs", [P, SUB])
        ps_l = [ctx.enter_context(nc.psum_tensor(f"npl{i}", [P, 512], F32)) for i in range(2)]
        ps_b = ctx.enter_context(nc.psum_tensor("npb", [P, 512], F32))
        ps_t = ctx.enter_context(nc.psum_tensor("npt", [P, 512], F32))
        ps_o = [ctx.enter_context(nc.psum_tensor(f"npo{i}", [P, 2, 512], F32)) for i in range(2)]

        consts_in = sem("n_consts_in")
        masks_done = sem("n_masks_done")
        chunk_in = [sem(f"n_chunk_in{i}") for i in range(SLOTS)]
        logit_mm = sem("n_logit_mm")
        relu_done = sem("n_relu_done")
        nmx_done = sem("n_nmx_done")
        exp_done = sem("n_exp_done")
        probt_mm = sem("n_probt_mm")
        probt_done = sem("n_probt_done")
        out_mm = sem("n_out_mm")
        t2_done = sem("n_t2_done")
        dve_step = sem("n_dve_step")
        block = ctx.enter_context(nc.Block())
        LOADS = [0] * SLOTS
        upto = []
        for c in range(NC):
            LOADS[c % SLOTS] += {0: 8, NC - 1: 7}.get(c, 5)
            upto.append(LOADS[c % SLOTS])

        AHEAD = 1 + (SLOTS - 1) * SUB

        def kind(c):
            return {0: 0, NC - 1: 2}.get(c, 1)

        @block.sync
        def _(sp):
            for dst, src in ((near[:], near_masks.rearrange("k p n -> p k n")),
                             (temp[:], temperature.partition_broadcast(P)), (bcol[:], bias.partition_broadcast(P)),
                             (ident[:], eye[:])):
                sp.dma_start(dst, src).then_inc(consts_in, 16)

            def load_chunk(b, c):
                i = c % SLOTS
                start = c * W - BEFORE
                loads = 0

                def load(dst, src):
                    nonlocal loads
                    loads += 1
                    sp.dma_start(dst, src).then_inc(chunk_in[i], 16)

                def channels(to, first, count):
                    load(xw[:, i, :, to:to + count],
                         xn_ch[bass.ds(b * KT, KT), :, first:first + count].rearrange("k p n -> p k n"))

                def value_tiles(tile, count, first):
                    load(vw[:, i, tile:tile + count],
                         xn_tok[bass.ds(b, 1), first:first + count * P].rearrange("a (t p) n -> p (a t) n", p=P))

                def value_rows(tile, row, count, first):
                    load(vw[row:row + count, i, tile], xn_tok[bass.ds(b, 1), first:first + count].rearrange("a p n -> p (a n)"))

                if c == 0:
                    channels(0, 0, BEFORE)
                    channels(BEFORE, 0, W + WINDOW - BEFORE)
                    value_rows(0, 0, BEFORE, 0)
                    value_rows(0, BEFORE, P - BEFORE, 0)
                    value_tiles(1, SUB - 1, P - BEFORE)
                    value_rows(SUB, 0, WINDOW, start + W)
                elif c == NC - 1:
                    channels(0, start, W + BEFORE)
                    channels(W + BEFORE, N - BEFORE, WINDOW - BEFORE)
                    value_tiles(0, SUB, start)
                    value_rows(SUB, 0, BEFORE, start + W)
                    value_rows(SUB, BEFORE, WINDOW - BEFORE, N - (WINDOW - BEFORE))
                else:
                    channels(0, start, W + WINDOW)
                    value_tiles(0, SUB, start)
                    value_rows(SUB, 0, WINDOW, start + W)
                load(keys[:, i], key_ch[bass.ds(b * KT, KT), :, c * W:(c + 1) * W].rearrange("k p n -> p k n"))
                load(t1_sb[:, i], t1[bass.ds(b, 1), c * W:(c + 1) * W].rearrange("a (j p) n -> p (a j) n", p=P))
                assert loads == upto[c] - (upto[c - SLOTS] if c >= SLOTS else 0)

            fast = sp.value_load(near_only[0:1, 0:1], min_val=0, max_val=1)
            with sp.If(fast):
                with sp.Fori(0, B) as b:
                    for c in range(NC):
                        sp.wait_ge(t2_done, 1 + (b * NC + c) * SUB)
                        load_chunk(b, c)

        @block.scalar
        def _(act):
            for counter in (relu_done, exp_done, probt_done):
                act.sem_inc(counter, 1)
            act.sem_inc(relu_done, 1)
            act.wait_ge(consts_in, 4 * 16)
            fast = act.value_load(near_only[0:1, 0:1], min_val=0, max_val=1)
            with act.If(fast):
                with act.Fori(0, B) as b:
                    for s in range(NC + 1):
                        if s < NC:
                            n = b * NC + s
                            act.wait_ge(exp_done, 1 + n * SUB)
                            act.wait_ge(logit_mm, 1 + n + 1)
                            nc.scalar.activation(logit[:].rearrange("p j n -> p (j n)"), ps_l[s % 2][:, 0:SUB * SPAN], ACT.Relu,
                                                 bias=bcol[:]).then_inc(relu_done, 1)
                        if s > 0:
                            n = b * NC + s - 1
                            act.wait_ge(out_mm, 1 + n)
                            act.wait_ge(probt_mm, 1 + n * 2 + 1)
                            nc.scalar.activation(body_t[:], ps_b[:, 0:W], ACT.Identity).then_inc(probt_done, 1)
                            act.wait_ge(probt_mm, 1 + n * 2 + 2)
                            nc.scalar.activation(tail_t[:], ps_t[0:WINDOW, 0:W], ACT.Identity).then_inc(probt_done, 1)
                        if s < NC:
                            n = b * NC + s
                            act.wait_ge(nmx_done, n + 1)
                            act.wait_ge(probt_mm, 1 + n * 2)
                            for j in range(SUB):
                                nc.scalar.activation(prob[:, s % 2, j], logit[:, j], ACT.Exp, bias=nmx[:, j:j + 1],
                                                     accum_out=rs[:, s % 2, j:j + 1]).then_inc(exp_done, 1)

        @block.vector
        def _(dve):
            dve.sem_inc(t2_done, AHEAD)
            dve.wait_ge(consts_in, 4 * 16)
            nc.vector.tensor_scalar(near[:], near[:], temp[:], None, ALU.mult).then_inc(masks_done, 1)
            dve.wait_ge(masks_done, 1)
            fast = dve.value_load(near_only[0:1, 0:1], min_val=0, max_val=1)
            STEPS = 3 * NC
            with dve.If(fast):
                with dve.Fori(0, B) as b:
                    st = Steps(dve, dve_step, b * STEPS)
                    for s in range(NC + 1):
                        if s < NC:
                            n = b * NC + s
                            dve.wait_ge(relu_done, 2 + n + 1)
                            flat = logit[:].rearrange("p j n -> p (j n)")
                            st.then(nc.vector.scalar_tensor_tensor(out=flat, in0=flat, scalar=temp[:], in1=near[:, kind(s)],
                                                                   op0=ALU.mult, op1=ALU.add))
                            st.then(nc.vector.reduce_max(mx[:], logit[:], AX.X))
                            dve.wait_ge(exp_done, 1 + n * SUB)
                            nc.vector.tensor_scalar(nmx[:], mx[:], -1.0, None, ALU.mult).then_inc(nmx_done, 1)
                        if s > 0:
                            n = b * NC + s - 1
                            i = (s - 1) % 2
                            dve.wait_ge(exp_done, 1 + (n + 1) * SUB)
                            slot = (s - 1) % SLOTS
                            dve.wait_ge(chunk_in[slot], (b * LOADS[slot] + upto[s - 1]) * 16)
                            dve.wait_ge(t2_done, AHEAD + n * SUB)
                            st.then(nc.vector.reciprocal(rrs[:], rs[:, i]))
                            dve.wait_ge(out_mm, 1 + n + 1)
                            for j in range(SUB):
                                nc.vector.scalar_tensor_tensor(out=t2[:, bass.ds(n * SUB + j, 1)].rearrange("p a n -> p (a n)"),
                                                               in0=ps_o[i][:, j // 2, j % 2 * CH:(j % 2 + 1) * CH],
                                                               scalar=rrs[:, j:j + 1], in1=t1_sb[:, slot, j],
                                                               op0=ALU.mult, op1=ALU.add).then_inc(t2_done, 1)
                            dve.wait_ge(t2_done, AHEAD + (n + 1) * SUB)
                            for j in range(SUB):
                                tile = bass.ds(n * SUB + j, 1)
                                nc.vector.bn_stats(t2_stats[:, tile].rearrange("p a n -> p (a n)"),
                                                   t2[:, tile].rearrange("p a n -> p (a n)"))
                    assert st.n == STEPS

        @block.tensor
        def _(pe):
            for counter in (logit_mm, probt_mm, out_mm):
                pe.sem_inc(counter, 1)
            pe.wait_ge(consts_in, 4 * 16)
            fast = pe.value_load(near_only[0:1, 0:1], min_val=0, max_val=1)
            with pe.If(fast):
                with pe.Fori(0, B) as b:
                    for s in range(NC + 1):
                        if s < NC:
                            n, i, slot = b * NC + s, s % 2, s % SLOTS
                            pe.wait_ge(chunk_in[slot], (b * LOADS[slot] + upto[s]) * 16)
                            pe.wait_ge(relu_done, 1 + n)
                            for j in range(SUB):
                                for k in range(KT):
                                    last = nc.tensor.matmul(ps_l[i][:, j * SPAN:(j + 1) * SPAN], keys[:, slot, k, j * P:(j + 1) * P],
                                                            xw[:, slot, k, j * P:j * P + SPAN], start=(k == 0), stop=(k == KT - 1))
                            last.then_inc(logit_mm, 1)
                        if s > 0:
                            n, i, slot = b * NC + s - 1, (s - 1) % 2, (s - 1) % SLOTS
                            pe.wait_ge(exp_done, 1 + n * SUB + SUB)
                            pe.wait_ge(probt_done, 1 + n * 2)
                            for j in range(SUB):
                                last = nc.tensor.transpose(ps_b[:, j * P:(j + 1) * P], prob[:, i, j, 0:P], ident[:])
                            last.then_inc(probt_mm, 1)
                            for j in range(SUB):
                                last = nc.tensor.transpose(ps_t[0:WINDOW, j * P:(j + 1) * P], prob[:, i, j, P:SPAN], ident[:])
                            last.then_inc(probt_mm, 1)
                            pe.wait_ge(probt_done, 1 + n * 2 + 2)
                            pe.wait_ge(t2_done, AHEAD - SUB + n * SUB)
                            for j in range(SUB):
                                to = ps_o[i][:, j // 2, j % 2 * CH:(j % 2 + 1) * CH]
                                part = slice(j * P, (j + 1) * P)
                                nc.tensor.matmul(to, body_t[:, part], vw[:, slot, j], start=True, stop=False)
                                last = nc.tensor.matmul(to, tail_t[:, part], vw[0:WINDOW, slot, j + 1], start=False, stop=True)
                            last.then_inc(out_mm, 1)


def dense_attention(nc, t1, xn_tok, xn_ch, key_ch, wide_mask, temperature, bias, eye, near_only, t2, t2_stats):
    with ExitStack() as ctx:
        def sb(name, shape, dt=F32):
            return ctx.enter_context(nc.sbuf_tensor(name, shape, dt))

        def sem(name):
            return ctx.enter_context(nc.semaphore(name))

        wide = sb("dwide", [P, (2 * NT - 1) * P])
        temp = sb("dtemp", [P, 1])
        bcol = sb("dbcol", [P, 1])
        ident = sb("dident", [P, P])
        keys = sb("dkeys", [P, KT, P])
        xw = sb("dxw", [P, KT, N])
        vw = sb("dvw", [P, NT, CH])
        t1_sb = sb("dt1", [P, CH])
        logit = sb("dlogit", [P, NC, W])
        probt = sb("dprobt", [P, NC, W])
        mx = sb("dmx", [P, 1])
        nmx = sb("dnmx", [P, 1])
        rs = sb("drs", [P, 1])
        rrs = sb("drrs", [P, 1])
        ps_l = [ctx.enter_context(nc.psum_tensor(f"dpl{i}", [P, 512], F32)) for i in range(NC)]
        ps_p = ctx.enter_context(nc.psum_tensor("dpp", [P, 512], F32))
        ps_o = ctx.enter_context(nc.psum_tensor("dpo", [P, 512], F32))

        consts_in = sem("d_consts_in")
        masks_done = sem("d_masks_done")
        batch_in = sem("d_batch_in")
        tile_in = sem("d_tile_in")
        logit_mm = sem("d_logit_mm")
        relu_done = sem("d_relu_done")
        nmx_done = sem("d_nmx_done")
        exp_done = sem("d_exp_done")
        probt_mm = sem("d_probt_mm")
        probt_done = sem("d_probt_done")
        out_mm = sem("d_out_mm")
        t2_done = sem("d_t2_done")
        dve_step = sem("d_dve_step")
        block = ctx.enter_context(nc.Block())

        @block.sync
        def _(sp):
            for dst, src in ((wide[:], wide_mask[:]), (temp[:], temperature.partition_broadcast(P)),
                             (bcol[:], bias.partition_broadcast(P)), (ident[:], eye[:])):
                sp.dma_start(dst, src).then_inc(consts_in, 16)
            near = sp.value_load(near_only[0:1, 0:1], min_val=0, max_val=1)
            with sp.If(1 - near):
                with sp.Fori(0, B) as b:
                    sp.wait_ge(t2_done, 1 + b * NT)
                    sp.dma_start(xw[:], xn_ch[bass.ds(b * KT, KT)].rearrange("k p n -> p k n")).then_inc(batch_in, 16)
                    sp.dma_start(vw[:], xn_tok[bass.ds(b, 1)].rearrange("a (t p) n -> p (a t) n", p=P)).then_inc(batch_in, 16)
                    with sp.Fori(0, NT) as t:
                        sp.wait_ge(t2_done, 1 + b * NT + t)
                        sp.dma_start(keys[:], key_ch[bass.ds(b * KT, KT), :, bass.ds(t * P, P)].rearrange("k p n -> p k n")
                                     ).then_inc(tile_in, 16)
                        sp.dma_start(t1_sb[:], t1[bass.ds(b, 1), bass.ds(t * P, P)].rearrange("a p n -> p (a n)")
                                     ).then_inc(tile_in, 16)

        @block.scalar
        def _(act):
            act.wait_ge(consts_in, 4 * 16)
            near = act.value_load(near_only[0:1, 0:1], min_val=0, max_val=1)
            with act.If(1 - near):
                with act.Fori(0, TT) as n:
                    for c in range(NC):
                        act.wait_ge(logit_mm, n * NC + c + 1)
                        nc.scalar.activation(logit[:, c], ps_l[c][:, 0:W], ACT.Relu, bias=bcol[:]).then_inc(relu_done, 1)
                    act.wait_ge(nmx_done, n + 1)
                    nc.scalar.activation(logit[:], logit[:], ACT.Exp, bias=nmx[:], accum_out=rs[:]).then_inc(exp_done, 1)
                    for c in range(NC):
                        act.wait_ge(probt_mm, n * NC + c + 1)
                        nc.scalar.activation(probt[:, c], ps_p[:, 0:W], ACT.Identity).then_inc(probt_done, 1)

        @block.vector
        def _(dve):
            dve.sem_inc(t2_done, 1)
            dve.wait_ge(consts_in, 4 * 16)
            nc.vector.tensor_scalar(wide[:], wide[:], temp[:], None, ALU.mult).then_inc(masks_done, 1)
            dve.wait_ge(masks_done, 1)
            near = dve.value_load(near_only[0:1, 0:1], min_val=0, max_val=1)
            STEPS = 3
            with dve.If(1 - near):
                with dve.Fori(0, B) as b:
                    with dve.Fori(0, NT) as t:
                        n = b * NT + t
                        st = Steps(dve, dve_step, n * STEPS)
                        dve.wait_ge(relu_done, (n + 1) * NC)
                        flat = logit[:].rearrange("p c n -> p (c n)")
                        st.then(nc.vector.scalar_tensor_tensor(out=flat, in0=flat, scalar=temp[:],
                                                               in1=wide[:, bass.ds((NT - 1) * P - t * P, N)],
                                                               op0=ALU.mult, op1=ALU.add))
                        st.then(nc.vector.reduce_max(mx[:], flat, AX.X))
                        nc.vector.tensor_scalar(nmx[:], mx[:], -1.0, None, ALU.mult).then_inc(nmx_done, 1)
                        dve.wait_ge(exp_done, n + 1)
                        dve.wait_ge(t2_done, 1 + n)
                        st.then(nc.vector.reciprocal(rrs[:], rs[:]))
                        dve.wait_ge(tile_in, (n + 1) * 2 * 16)
                        dve.wait_ge(out_mm, n + 1)
                        nc.vector.scalar_tensor_tensor(out=t2[:, bass.ds(n, 1)].rearrange("p a n -> p (a n)"), in0=ps_o[:, 0:CH],
                                                       scalar=rrs[:], in1=t1_sb[:], op0=ALU.mult, op1=ALU.add).then_inc(t2_done, 1)
                        dve.wait_ge(t2_done, 1 + n + 1)
                        nc.vector.bn_stats(t2_stats[:, bass.ds(n, 1)].rearrange("p a n -> p (a n)"),
                                           t2[:, bass.ds(n, 1)].rearrange("p a n -> p (a n)"))

        @block.tensor
        def _(pe):
            pe.wait_ge(consts_in, 4 * 16)
            near = pe.value_load(near_only[0:1, 0:1], min_val=0, max_val=1)
            with pe.If(1 - near):
                with pe.Fori(0, B) as b:
                    with pe.Fori(0, NT) as t:
                        n = b * NT + t
                        pe.wait_ge(batch_in, (b + 1) * 2 * 16)
                        pe.wait_ge(tile_in, (n + 1) * 2 * 16)
                        for c in range(NC):
                            for k in range(KT):
                                last = nc.tensor.matmul(ps_l[c][:, 0:W], keys[:, k], xw[:, k, c * W:(c + 1) * W],
                                                        start=(k == 0), stop=(k == KT - 1))
                            last.then_inc(logit_mm, 1)
                        pe.wait_ge(exp_done, n + 1)
                        for c in range(NC):
                            if c:
                                pe.wait_ge(probt_done, n * NC + c)
                            for a in range(SUB):
                                last = nc.tensor.transpose(ps_p[:, a * P:(a + 1) * P], logit[:, c, a * P:(a + 1) * P], ident[:])
                            last.then_inc(probt_mm, 1)
                        pe.wait_ge(probt_done, (n + 1) * NC)
                        for c in range(NC):
                            for a in range(SUB):
                                last = nc.tensor.matmul(ps_o[:, 0:CH], probt[:, c, a * P:(a + 1) * P], vw[:, c * SUB + a],
                                                        start=(c + a == 0), stop=(c * SUB + a == NT - 1))
                        last.then_inc(out_mm, 1)


def norm_and_gate(nc, t2, t2_stats, gate_w, gate_b_row, eye, xn2, gate_logits, slots_used, slots):
    with ExitStack() as ctx:
        def sb(name, shape, dt=F32):
            return ctx.enter_context(nc.sbuf_tensor(name, shape, dt))

        def sem(name):
            return ctx.enter_context(nc.semaphore(name))

        E = gate_w.shape[1]
        CHUNKS = TT // SUB
        FILLS = 18
        ident = sb("gident", [P, P])
        gw = sb("ggw", [P, KT, E])
        gb = sb("ggb", [P, E])
        mv = sb("gmv", [P, TT, BN2])
        veps = sb("gveps", [P, TT])
        rstd = sb("grstd", [P, TT])
        mhalf = sb("gmhalf", [P, TT])
        zeros = sb("gzeros", [P, slots_used // P * CH // FILLS])
        xn = sb("gxn", [P, 2, SUB, CH])
        xt = sb("gxt", [P, 2, KT, W])
        ps_x = [[ctx.enter_context(nc.psum_tensor(f"gpx{i}{k}", [P, 512], F32)) for k in range(KT)] for i in range(2)]
        ps_g = [ctx.enter_context(nc.psum_tensor(f"gpg{i}", [P, 512], F32)) for i in range(2)]

        consts_in = sem("g_consts_in")
        mhalf_done = sem("g_mhalf_done")
        zeros_set = sem("g_zeros_set")
        zeroed = sem("g_zeroed")
        veps_done = sem("g_veps_done")
        rstd_done = sem("g_rstd_done")
        dve_step = sem("g_dve_step")
        xn_done = sem("g_xn_done")
        xt_mm = sem("g_xt_mm")
        xt_done = sem("g_xt_done")
        gate_mm = sem("g_gate_mm")
        gate_done = sem("g_gate_done")
        block = ctx.enter_context(nc.Block())

        PAIRS = (CHUNKS - 2) // 2

        @block.sync
        def _(sp):
            for dst, src in ((ident[:], eye[:]), (gw[:], gate_w.rearrange("(k p) e -> p k e", p=P)),
                             (gb[:], gate_b_row.partition_broadcast(P))):
                sp.dma_start(dst, src).then_inc(consts_in, 16)
            sp.wait_ge(zeros_set, 1)
            rows = slots_used // FILLS
            for a in range(FILLS):
                sp.dma_start(slots[a * rows:(a + 1) * rows].rearrange("(p r) n -> p (r n)", p=P), zeros[:]).then_inc(zeroed, 16)
            sp.wait_ge(zeroed, FILLS * 16)

        @block.gpsimd
        def _(pool):
            nc.gpsimd.memset(zeros[:], 0.0).then_inc(zeros_set, 1)
            nc.gpsimd.memset(mhalf[:], -0.5).then_inc(mhalf_done, 1)
            pool.wait_ge(mhalf_done, 1)
            pool.wait_ge(veps_done, 1)
            with pool.Fori(0, CHUNKS) as n:
                tiles = bass.ds(n * SUB, SUB)
                nc.gpsimd.tensor_tensor(rstd[:, tiles], veps[:, tiles], mhalf[:, 0:SUB], ALU.pow).then_inc(rstd_done, 1)

        @block.vector
        def _(dve):
            dve.sem_inc(gate_done, 2)
            st = Steps(dve, dve_step)
            nc.vector.memset(veps[:, 0:1], 0.0)
            for n in range(TT):
                last = nc.vector.bn_aggr(mv[:, n], t2_stats[:, n])
            st.then(last)
            nc.vector.tensor_scalar(veps[:], mv[:, :, 1], LN_EPS, None, ALU.add).then_inc(veps_done, 1)
            dve.wait_ge(consts_in, 3 * 16)

            def normalise(n, i):
                dve.wait_ge(rstd_done, n + 1)
                dve.wait_ge(xt_mm, 1 + n * KT)
                for j in range(SUB):
                    at = bass.ds(n * SUB + j, 1)
                    token_tile = t2[:, at].rearrange("p a n -> p (a n)")
                    mean, scale = mv[:, at, 0:1].rearrange("p a n -> p (a n)"), rstd[:, at]
                    nc.vector.tensor_scalar(xn[:, i, j], token_tile, mean, scale, ALU.subtract, ALU.mult).then_inc(xn_done, 1)
                for j in range(SUB):
                    at = bass.ds(n * SUB + j, 1)
                    token_tile = t2[:, at].rearrange("p a n -> p (a n)")
                    mean, scale = mv[:, at, 0:1].rearrange("p a n -> p (a n)"), rstd[:, at]
                    nc.vector.tensor_scalar(xn2[:, at].rearrange("p a n -> p (a n)"), token_tile, mean, scale,
                                            ALU.subtract, ALU.mult)

            def add_bias(n, i):
                dve.wait_ge(gate_mm, n + 1)
                for j in range(SUB):
                    last = nc.vector.tensor_tensor(gate_logits[:, :, bass.ds(n * SUB + j, 1)].rearrange("p e a -> p (e a)"),
                                                   ps_g[i][:, j * E:(j + 1) * E], gb[:], ALU.add)
                last.then_inc(gate_done, 1)

            normalise(0, 0)
            normalise(1, 1)
            with dve.Fori(0, PAIRS) as pair:
                for i in range(2):
                    normalise(pair * 2 + i + 2, i)
                    add_bias(pair * 2 + i, i)
            add_bias(CHUNKS - 2, 0)
            add_bias(CHUNKS - 1, 1)

        @block.scalar
        def _(act):
            act.sem_inc(xt_done, 1 + KT)
            with act.Fori(0, CHUNKS // 2) as pair:
                for i in range(2):
                    n = pair * 2 + i
                    for k in range(KT):
                        act.wait_ge(xt_mm, 1 + KT + n * KT + k + 1)
                        nc.scalar.activation(xt[:, i, k], ps_x[i][k][:, 0:W], ACT.Identity).then_inc(xt_done, 1)

        @block.tensor
        def _(pe):
            pe.sem_inc(xt_mm, 1 + KT)
            pe.wait_ge(consts_in, 3 * 16)

            def transposes(n, i):
                pe.wait_ge(xn_done, (n + 1) * SUB)
                pe.wait_ge(xt_done, 1 + n * KT)
                for k in range(KT):
                    for j in range(SUB):
                        last = nc.tensor.transpose(ps_x[i][k][:, j * P:(j + 1) * P], xn[:, i, j, k * P:(k + 1) * P], ident[:])
                    last.then_inc(xt_mm, 1)

            def gate_products(n, i):
                pe.wait_ge(xt_done, 1 + KT + (n + 1) * KT)
                pe.wait_ge(gate_done, 1 + n)
                for j in range(SUB):
                    for k in range(KT):
                        last = nc.tensor.matmul(ps_g[i][:, j * E:(j + 1) * E], xt[:, i, k, j * P:(j + 1) * P], gw[:, k],
                                                start=(k == 0), stop=(k == KT - 1))
                last.then_inc(gate_mm, 1)

            transposes(0, 0)
            with pe.Fori(0, PAIRS) as pair:
                for i in (1, 2):
                    transposes(pair * 2 + i, i % 2)
                    gate_products(pair * 2 + i - 1, (i - 1) % 2)
            transposes(CHUNKS - 1, 1)
            gate_products(CHUNKS - 2, 0)
            gate_products(CHUNKS - 1, 1)


def route(nc, gate_logits, capacity, rank, base, trash_place, prefix, to_slot, from_slot, weight):
    with ExitStack() as ctx:
        E = gate_logits.shape[1]

        def sb(name, shape, dt=F32):
            return ctx.enter_context(nc.sbuf_tensor(name, shape, dt))

        def sem(name):
            return ctx.enter_context(nc.semaphore(name))

        HALF = E // 2
        rk = sb("rrank", [P, E, TT])
        bs = sb("rbase", [P, E, TT])
        trash = sb("rtrash", [P, TT])
        tri = sb("rtri", [P, P])
        ones = sb("rones", [P, P])
        zeros = sb("rzeros", [P, TT])
        best = sb("rbest", [P, TT])
        prob = sb("rprob", [P, E, TT])
        total = sb("rtotal", [P, TT])
        inv = sb("rinv", [P, TT])
        top = sb("rtop", [P, TT])
        hot = sb("rhot", [P, E, TT])
        pick = sb("rpick", [P, TT])
        count = sb("rcount", [P, E, TT])
        scan = sb("rscan", [P, E, TT])
        place = sb("rplace", [P, E, TT])
        pos = sb("rpos", [P, TT])
        off = sb("roff", [P, TT])
        kept = sb("rkept", [P, TT])
        tmp = sb("rtmp", [P, TT])
        ps_c = [ctx.enter_context(nc.psum_tensor(f"rpc{i}", [P, 512], F32)) for i in range(2)]
        ps_t = [ctx.enter_context(nc.psum_tensor(f"rpt{i}", [P, 512], F32)) for i in range(2)]

        consts_in = sem("r_consts_in")
        ones_done = sem("r_ones_done")
        dve_step = sem("r_dve_step")
        exp_done = sem("r_exp_done")
        hot_done = sem("r_hot_done")
        counts_mm = sem("r_counts_mm")
        block = ctx.enter_context(nc.Block())

        def over_experts(t):
            return t[:].rearrange("p e t -> p t e")

        def to_experts(t):
            return t[:].rearrange("p (a t) -> p a t", a=1).to_broadcast([P, E, TT])

        @block.sync
        def _(sp):
            for dst, src in ((rk[:], rank[:]), (bs[:], base[:]), (trash[:], trash_place[:]), (tri[:], prefix[:])):
                sp.dma_start(dst, src).then_inc(consts_in, 16)

        @block.gpsimd
        def _(pool):
            nc.gpsimd.memset(zeros[:], 0.0).then_inc(ones_done, 1)
            nc.gpsimd.memset(ones[:], 1.0).then_inc(ones_done, 1)

        @block.scalar
        def _(act):
            act.wait_ge(dve_step, 2)
            nc.scalar.activation(prob[:], gate_logits[:], ACT.Exp).then_inc(exp_done, 1)

        @block.tensor
        def _(pe):
            pe.wait_ge(consts_in, 4 * 16)
            pe.wait_ge(ones_done, 2)
            pe.wait_ge(hot_done, 1)
            for i in range(2):
                half = hot[:, i * HALF:(i + 1) * HALF].rearrange("p e t -> p (e t)")
                nc.tensor.matmul(ps_c[i][:, 0:HALF * TT], tri[:], half, start=True, stop=True)
                last = nc.tensor.matmul(ps_t[i][:, 0:HALF * TT], ones[:], half, start=True, stop=True)
            last.then_inc(counts_mm, 1)

        @block.vector
        def _(dve):
            st = Steps(dve, dve_step)
            tt, ts = nc.vector.tensor_tensor, nc.vector.tensor_scalar
            st.then(nc.vector.reduce_max(best[:], over_experts(gate_logits), AX.X))
            st.then(tt(gate_logits[:], gate_logits[:], to_experts(best), ALU.subtract))
            dve.wait_ge(exp_done, 1)
            st.then(nc.vector.reduce_sum(total[:], over_experts(prob), AX.X))
            st.then(nc.vector.reciprocal(inv[:], total[:]))
            st.then(tt(prob[:], prob[:], to_experts(inv), ALU.mult))
            st.then(nc.vector.reduce_max(top[:], over_experts(prob), AX.X))
            st.then(tt(hot[:], prob[:], to_experts(top), ALU.is_equal))
            dve.wait_ge(consts_in, 4 * 16)
            st.then(tt(hot[:], hot[:], rk[:], ALU.mult))
            st.then(nc.vector.reduce_max(pick[:], over_experts(hot), AX.X))
            st.then(tt(count[:], rk[:], to_experts(pick), ALU.is_equal))
            nc.vector.tensor_copy(hot[:], count[:]).then_inc(hot_done, 1)
            dve.wait_ge(counts_mm, 1)
            dve.wait_ge(ones_done, 2)
            for i in range(2):
                es = slice(i * HALF, (i + 1) * HALF)
                last = nc.vector.tensor_copy(count[:, es].rearrange("p e t -> p (e t)"), ps_t[i][:, 0:HALF * TT])
            st.then(last)
            for e in range(E):
                last = nc.vector.tensor_tensor_scan(scan[:, e], count[:, e], zeros[:], initial=0.0, op0=ALU.add, op1=ALU.add)
            st.then(last)
            st.then(tt(scan[:], scan[:], count[:], ALU.subtract))
            for i in range(2):
                es = slice(i * HALF, (i + 1) * HALF)
                last = tt(place[:, es].rearrange("p e t -> p (e t)"), ps_c[i][:, 0:HALF * TT],
                          scan[:, es].rearrange("p e t -> p (e t)"), ALU.add)
            st.then(last)
            st.then(tt(place[:], place[:], hot[:], ALU.mult))
            st.then(nc.vector.reduce_sum(pos[:], over_experts(place), AX.X))
            st.then(ts(pos[:], pos[:], -1.0, None, ALU.add))
            st.then(tt(hot[:], hot[:], bs[:], ALU.mult))
            st.then(nc.vector.reduce_sum(off[:], over_experts(hot), AX.X))
            st.then(ts(kept[:], pos[:], float(capacity), None, ALU.is_lt))
            st.then(tt(weight[:], top[:], kept[:], ALU.mult))
            st.then(ts(tmp[:], pos[:], float(capacity - 1), None, ALU.min))
            st.then(tt(tmp[:], tmp[:], off[:], ALU.add))
            st.then(nc.vector.tensor_copy(from_slot[:], tmp[:]))
            st.then(tt(pos[:], pos[:], off[:], ALU.add))
            st.then(tt(pos[:], pos[:], trash[:], ALU.subtract))
            st.then(tt(pos[:], pos[:], kept[:], ALU.mult))
            st.then(tt(pos[:], pos[:], trash[:], ALU.add))
            st.then(nc.vector.tensor_copy(to_slot[:], pos[:]))


def scatter_tokens(nc, xn2, to_slot, slots):
    with ExitStack() as ctx:
        scattered = ctx.enter_context(nc.semaphore("s_scattered"))
        block = ctx.enter_context(nc.Block())

        @block.gpsimd
        def _(pool):
            for n in range(TT):
                pool.indirect_dma_start(slots[:], bass.IndirectOffsetOnAxis(ap=to_slot[:, n:n + 1], axis=0), xn2[:, n], None
                                        ).then_inc(scattered, 16)
            pool.wait_ge(scattered, TT * 16)


def experts(nc, slots, w1, b1_cols, w2, b2, eye, capacity, results, weight, all_finite):
    with ExitStack() as ctx:
        def sb(name, shape, dt=F32):
            return ctx.enter_context(nc.sbuf_tensor(name, shape, dt))

        def sem(name):
            return ctx.enter_context(nc.semaphore(name))

        E, _, F = w1.shape
        FT = F // P
        RT = 3
        S = 4
        R = capacity // (RT * S)
        RW = S * R
        w1_sb = sb("ew1", [P, 2, KT, F])
        w2_sb = sb("ew2", [P, 2, FT, CH])
        b1_sb = sb("eb1", [P, 2, FT])
        b2_sb = sb("eb2", [P, 2, CH])
        ident = sb("eident", [P, P])
        x = sb("ex", [R, 2, S, CH])
        xt = sb("ext", [P, KT, RW])
        hid = sb("ehid", [P, FT, RW])
        y = sb("ey", [R, 2, S, CH])
        TILES = E * RT
        nought = sb("enought", [R, S * CH])
        noughts = sb("enoughts", [R, TILES])
        total = sb("etotal", [R, 1])
        finite = sb("efinite", [R, 1])
        weight_noughts = sb("eweight_noughts", [P, TT])
        weight_total = sb("eweight_total", [P, 1])
        weight_finite = sb("eweight_finite", [P, 1])
        fewest = sb("efewest", [1, 1])
        ps_x = [ctx.enter_context(nc.psum_tensor(f"epx{i}", [P, 512], F32)) for i in range(KT)]
        ps_h = [ctx.enter_context(nc.psum_tensor(f"eph{i}", [P, 512], F32)) for i in range(4)]
        ps_y = [ctx.enter_context(nc.psum_tensor(f"epy{i}", [P, 512], F32)) for i in range(2)]

        consts_in = sem("e_consts_in")
        w_in = [sem(f"e_w_in{i}") for i in range(2)]
        x_in = [sem(f"e_x_in{i}") for i in range(2)]
        xt_mm = sem("e_xt_mm")
        xt_done = sem("e_xt_done")
        hid_mm = sem("e_hid_mm")
        hid_done = sem("e_hid_done")
        y_mm = sem("e_y_mm")
        y_done = sem("e_y_done")
        dve_step = sem("e_dve_step")
        finite_done = sem("e_finite_done")
        finite_mm = sem("e_finite_mm")
        stored = [sem(f"e_stored{i}") for i in range(2)]
        block = ctx.enter_context(nc.Block())
        rows = slots[0:E * capacity].rearrange("(n s r) c -> n r s c", s=S, r=R)
        rows_out = results.rearrange("(n s r) c -> n r s c", s=S, r=R)

        def tiles(it):
            for j in range(2 * RT):
                yield j, it * 2 * RT + j, j // RT, j % 2

        @block.sync
        def _(sp):
            sp.dma_start(ident[:], eye[:]).then_inc(consts_in, 16)

            def load_rows(n, i):
                sp.dma_start(x[:, i], rows[bass.ds(n, 1)].rearrange("a r s c -> r (a s) c")).then_inc(x_in[i], 16)

            def load_weights(expert, e):
                one = bass.ds(expert, 1)
                for dst, src in ((w1_sb[:, e], w1[one].rearrange("a (k p) f -> p (a k) f", p=P)),
                                 (w2_sb[:, e], w2[one].rearrange("a (f p) c -> p (a f) c", p=P)),
                                 (b1_sb[:, e], b1_cols[one].rearrange("a p f -> p (a f)")),
                                 (b2_sb[:, e], b2[one].rearrange("a c -> (a c)").partition_broadcast(P))):
                    sp.dma_start(dst, src).then_inc(w_in[e], 16)

            def two_experts(it, last):
                for j, n, e, i in tiles(it):
                    if not (last and j == 2 * RT - 1):
                        load_rows(n + 1, 1 - i)
                    sp.wait_ge(y_done, 3 + (n + 1) * S)
                    sp.dma_start(rows_out[bass.ds(n, 1)].rearrange("a r s c -> r (a s) c"), y[:, i]).then_inc(stored[i], 16)
                    if j % RT == RT - 1 and not last:
                        load_weights(it * 2 + 2 + e, e)

            load_rows(0, 0)
            load_weights(0, 0)
            load_weights(1, 1)
            with sp.Fori(0, E // 2 - 1) as it:
                two_experts(it, False)
            two_experts(E // 2 - 1, True)
            for i in range(2):
                sp.wait_ge(stored[i], 1 + TILES // 2 * 16)

        @block.scalar
        def _(act):
            act.sem_inc(xt_done, 1)
            act.sem_inc(hid_done, 1 + FT)
            with act.Fori(0, E // 2) as it:
                for j, n, e, i in tiles(it):
                    for k in range(KT):
                        act.wait_ge(xt_mm, 2 + n)
                        nc.scalar.activation(xt[:, k], ps_x[k][:, 0:RW], ACT.Identity).then_inc(xt_done, 1)
                    act.wait_ge(w_in[e], (it + 1) * 4 * 16)
                    for f in range(FT):
                        act.wait_ge(hid_mm, 1 + n * FT + f + 1)
                        act.wait_ge(y_mm, 1 + n * S)
                        nc.scalar.activation(hid[:, f], ps_h[f % 4][:, 0:RW], ACT.Relu,
                                             bias=b1_sb[:, e, f:f + 1]).then_inc(hid_done, 1)

        @block.vector
        def _(dve):
            dve.sem_inc(y_done, 1 + 2)
            for counter in stored:
                dve.sem_inc(counter, 1)
            with dve.Fori(0, E // 2) as it:
                for j, n, e, i in tiles(it):
                    dve.wait_ge(w_in[e], (it + 1) * 4 * 16)
                    dve.wait_ge(stored[i], 1 + (it * RT + j // 2) * 16)
                    for s in range(S):
                        dve.wait_ge(y_mm, 1 + n * S + s + 1)
                        nc.vector.tensor_tensor(y[:, i, s], ps_y[s % 2][0:R, 0:CH], b2_sb[0:R, e], ALU.add).then_inc(y_done, 1)
                    st = Steps(dve, dve_step, n * 2)
                    dve.wait_ge(y_done, 3 + (n + 1) * S)
                    st.then(nc.vector.tensor_scalar(nought[:], y[:, i].rearrange("r s c -> r (s c)"), 0.0, None, ALU.mult))
                    st.then(nc.vector.reduce_sum(noughts[:, bass.ds(n, 1)], nought[:], AX.X))
            st = Steps(dve, dve_step, TILES * 2)
            st.then(nc.vector.reduce_sum(total[:], noughts[:], AX.X))
            nc.vector.tensor_scalar(finite[:], total[:], 0.0, None, ALU.is_equal).then_inc(finite_done, 1)
            st.then(nc.vector.tensor_scalar(weight_noughts[:], weight[:], 0.0, None, ALU.mult))
            st.then(nc.vector.reduce_sum(weight_total[:], weight_noughts[:], AX.X))
            nc.vector.tensor_scalar(weight_finite[:], weight_total[:], 0.0, None, ALU.is_equal).then_inc(finite_done, 1)
            dve.wait_ge(finite_mm, 1)
            st.then(nc.vector.tensor_reduce(fewest[:], ps_x[0][0:1, 0:R + P], AX.X, ALU.min))
            st.then(nc.vector.tensor_copy(all_finite[:], fewest[:]))

        @block.tensor
        def _(pe):
            for counter in (xt_mm, hid_mm, y_mm):
                pe.sem_inc(counter, 1)
            pe.wait_ge(consts_in, 16)
            with pe.Fori(0, E // 2) as it:
                for j, n, e, i in tiles(it):
                    pe.wait_ge(x_in[i], (it * RT + j // 2 + 1) * 16)
                    pe.wait_ge(xt_done, 1 + n * KT)
                    for k in range(KT):
                        for s in range(S):
                            last = nc.tensor.transpose(ps_x[k][:, s * R:(s + 1) * R], x[:, i, s, k * P:(k + 1) * P], ident[0:R, 0:R])
                    last.then_inc(xt_mm, 1)
                    pe.wait_ge(xt_done, 1 + (n + 1) * KT)
                    pe.wait_ge(w_in[e], (it + 1) * 4 * 16)
                    for f in range(FT):
                        pe.wait_ge(hid_done, 1 + FT + n * FT + f - 3)
                        for k in range(KT):
                            last = nc.tensor.matmul(ps_h[f % 4][:, 0:RW], w1_sb[:, e, k, f * P:(f + 1) * P], xt[:, k],
                                                    start=(k == 0), stop=(k == KT - 1))
                        last.then_inc(hid_mm, 1)
                    for s in range(S):
                        pe.wait_ge(y_done, 3 + n * S + s - 1)
                        for f in range(FT):
                            if s == 0:
                                pe.wait_ge(hid_done, 1 + FT + n * FT + f + 1)
                            last = nc.tensor.matmul(ps_y[s % 2][0:R, 0:CH], hid[:, f, s * R:(s + 1) * R], w2_sb[:, e, f],
                                                    start=(f == 0), stop=(f == FT - 1))
                        last.then_inc(y_mm, 1)
            pe.wait_ge(finite_done, 2)
            pe.wait_ge(xt_done, 1 + TILES * KT)
            nc.tensor.transpose(ps_x[0][0:1, 0:R], finite[:], ident[0:R, 0:R])
            nc.tensor.transpose(ps_x[0][0:1, R:R + P], weight_finite[:], ident[:]).then_inc(finite_mm, 1)


def combine(nc, results, from_slot, weight, t2, eye, all_finite, out):
    with ExitStack() as ctx:
        def sb(name, shape, dt=F32):
            return ctx.enter_context(nc.sbuf_tensor(name, shape, dt))

        def sem(name):
            return ctx.enter_context(nc.semaphore(name))

        FLT_MAX = 3.4028234e38
        NAN_TO_NUM = 10000.0
        SLOTS = 4
        rows = sb("orows", [P, SLOTS, SUB, CH])
        pos = sb("opos", [P, SUB, CH])
        neg = sb("oneg", [P, SUB, CH])
        cap = sb("ocap", [P, 2, SUB, CH])
        tok = sb("otok", [P, 2, SUB, CH])
        img = sb("oimg", [P, 2, KT, W])
        ident = sb("oident", [P, P])
        ps = [[ctx.enter_context(nc.psum_tensor(f"op{i}{k}", [P, 512], F32)) for k in range(KT)] for i in range(2)]
        CHUNKS = B * NC

        consts_in = sem("o_consts_in")
        rows_in = [sem(f"o_rows_in{i}") for i in range(SLOTS)]
        rows_used = sem("o_rows_used")
        dve_step = sem("o_dve_step")
        tok_done = sem("o_tok_done")
        tok_mm = sem("o_tok_mm")
        img_done = sem("o_img_done")
        stored = [sem(f"o_stored{i}") for i in range(2)]
        block = ctx.enter_context(nc.Block())

        @block.sync
        def _(sp):
            sp.dma_start(ident[:], eye[:]).then_inc(consts_in, 16)
            for counter in stored:
                sp.sem_inc(counter, 1)
            with sp.Fori(0, B) as b:
                for c in range(NC):
                    sp.wait_ge(img_done, 1 + KT + (b * NC + c + 1) * KT)
                    sp.dma_start(out[bass.ds(b, 1), :, c * W:(c + 1) * W].rearrange("a (k p) n -> p (a k) n", p=P), img[:, c % 2]
                                 ).then_inc(stored[c % 2], 16)
            for i in range(2):
                sp.wait_ge(stored[i], 1 + CHUNKS // 2 * 16)

        @block.gpsimd
        def _(pool):
            for n in range(CHUNKS):
                if n >= SLOTS:
                    pool.wait_ge(rows_used, n - SLOTS + 1)
                for j in range(SUB):
                    at = n * SUB + j
                    pool.indirect_dma_start(rows[:, n % SLOTS, j], None, results[:],
                                            bass.IndirectOffsetOnAxis(ap=from_slot[:, at:at + 1], axis=0)
                                            ).then_inc(rows_in[n % SLOTS], 16)

        @block.vector
        def _(dve):
            STEPS = 4

            def add_rows(n, turn, slot, i):
                dve.wait_ge(rows_in[slot], (turn + 1) * SUB * 16)
                dve.wait_ge(tok_mm, 1 + n * KT)
                for j in range(SUB):
                    at = bass.ds(n * SUB + j, 1)
                    nc.vector.scalar_tensor_tensor(out=tok[:, i, j], in0=rows[:, slot, j], scalar=weight[:, at],
                                                   in1=t2[:, at].rearrange("p a n -> p (a n)"), op0=ALU.mult, op1=ALU.add
                                                   ).then_inc(tok_done, 1)
                dve.wait_ge(tok_done, (n + 1) * SUB)
                dve.sem_inc(rows_used, 1)

            def add_mended_rows(n, turn, slot, i):
                st = Steps(dve, dve_step, n * STEPS)
                dve.wait_ge(rows_in[slot], (turn + 1) * SUB * 16)
                for j in range(SUB):
                    w = weight[:, bass.ds(n * SUB + j, 1)]
                    nc.vector.tensor_scalar(pos[:, j], rows[:, slot, j], w, 0.0, ALU.mult, ALU.max)
                    last = nc.vector.tensor_scalar(neg[:, j], rows[:, slot, j], w, 0.0, ALU.mult, ALU.min)
                st.then(last)
                dve.sem_inc(rows_used, 1)
                nc.vector.tensor_scalar(cap[:, 0], pos[:], FLT_MAX, FLT_MAX, ALU.is_le, ALU.mult)
                st.then(nc.vector.tensor_scalar(cap[:, 1], neg[:], -FLT_MAX, -FLT_MAX, ALU.is_ge, ALU.mult))
                nc.vector.scalar_tensor_tensor(out=pos[:], in0=cap[:, 0], scalar=NAN_TO_NUM, in1=pos[:],
                                               op0=ALU.max, op1=ALU.min)
                st.then(nc.vector.scalar_tensor_tensor(out=neg[:], in0=cap[:, 1], scalar=-NAN_TO_NUM, in1=neg[:],
                                                       op0=ALU.min, op1=ALU.max))
                st.then(nc.vector.tensor_tensor(pos[:], pos[:], neg[:], ALU.add))
                dve.wait_ge(tok_mm, 1 + n * KT)
                for j in range(SUB):
                    nc.vector.tensor_tensor(tok[:, i, j], pos[:, j], t2[:, bass.ds(n * SUB + j, 1)].rearrange("p a n -> p (a n)"),
                                            ALU.add).then_inc(tok_done, 1)
                dve.wait_ge(tok_done, (n + 1) * SUB)

            def each_chunk(add):
                with dve.Fori(0, CHUNKS // SLOTS) as turn:
                    for slot in range(SLOTS):
                        add(turn * SLOTS + slot, turn, slot, slot % 2)

            fast = dve.value_load(all_finite[0:1, 0:1], min_val=0, max_val=1)
            with dve.If(fast):
                each_chunk(add_rows)
            with dve.Else():
                each_chunk(add_mended_rows)

        @block.scalar
        def _(act):
            act.sem_inc(img_done, 1 + KT)
            with act.Fori(0, CHUNKS // 2) as pair:
                for i in range(2):
                    n = pair * 2 + i
                    act.wait_ge(stored[i], 1 + pair * 16)
                    for k in range(KT):
                        act.wait_ge(tok_mm, 1 + KT + n * KT + k + 1)
                        nc.scalar.activation(img[:, i, k], ps[i][k][:, 0:W], ACT.Identity).then_inc(img_done, 1)

        @block.tensor
        def _(pe):
            pe.sem_inc(tok_mm, 1 + KT)
            pe.wait_ge(consts_in, 16)
            with pe.Fori(0, CHUNKS // 2) as pair:
                for i in range(2):
                    n = pair * 2 + i
                    pe.wait_ge(tok_done, (n + 1) * SUB)
                    for k in range(KT):
                        pe.wait_ge(img_done, 1 + n * KT)
                        for j in range(SUB):
                            last = nc.tensor.transpose(ps[i][k][:, j * P:(j + 1) * P], tok[:, i, j, k * P:(k + 1) * P], ident[:])
                        last.then_inc(tok_mm, 1)


_INS = []


def kernel(**inputs):
    import numpy as _np
    import concourse.bacc as _bacc
    from concourse.bass_utils import run_bass_kernel_spmd as _run

    g = inputs
    w_qk = _np.asarray(g["L0_conv_w_qk"]).reshape(HEADS, 2, HD, CH)
    w_q, w_k = w_qk[:, 0].reshape(CH, CH), w_qk[:, 1].reshape(CH, CH)
    b_qk = _np.asarray(g["L0_conv_b_qk"]).reshape(HEADS, 2, HD)
    b_all = _np.stack([b_qk[:, 0].reshape(CH), b_qk[:, 1].reshape(CH), _np.asarray(g["L0_conv_b_v"])])
    eye = _np.eye(P, dtype=_np.float32)
    arrays = {
        "x": _np.asarray(g["x"]).reshape(B, CH, N),
        "w_qkv": _np.concatenate([w_q.T, w_k.T, _np.asarray(g["L0_conv_w_v"])[:, :, 0, 0].T], axis=1),
        "b_qkv": b_all.reshape(3 * KT, P).T,
        "bv_row": _np.asarray(g["L0_conv_b_v"]),
        "group_mean": _np.kron(_np.eye(P // GN_GROUP, dtype=_np.float32), _np.full((GN_GROUP, GN_GROUP), 1 / GN_GROUP, _np.float32)),
    }
    arrays["w_pe"] = _np.asarray(g["L0_conv_w_pe"]).reshape(CH, 9)
    arrays["b_pe"] = _np.asarray(g["L0_conv_b_pe"]).reshape(KT, P).T
    arrays["w_proj"] = _np.asarray(g["L0_conv_w_proj"])[:, :, 0, 0].T
    arrays["bp_row"] = _np.asarray(g["L0_conv_b_proj"])
    arrays["eye"] = eye
    arrays["head_sum"] = _np.kron(_np.eye(HG, dtype=_np.float32), _np.ones((HD, HD), _np.float32))
    arrays["w_key"] = _np.asarray(g["L1_attn_K"])
    arrays["temperature"] = _np.asarray(g["L1_attn_temperature"])
    arrays["bias"] = _np.asarray(g["L1_attn_bias"])
    ahead = _np.arange(-(NT - 1) * P, NT * P)[None, :] - _np.arange(P)[:, None]
    outside = (ahead < -(WINDOW // 2)) | (ahead >= WINDOW - WINDOW // 2)
    arrays["wide_mask"] = _np.where(outside, _np.float32(-OUTSIDE), _np.float32(0))
    at = (NT - 1) * P - WINDOW // 2
    inner = arrays["wide_mask"][:, at:at + P + WINDOW]
    near_masks = _np.repeat(_np.stack([inner] * SUB, axis=1)[None], 3, axis=0)
    near_masks[0, :, 0, :WINDOW // 2] = near_masks[2, :, SUB - 1, P + WINDOW // 2:] = GONE
    near_masks = near_masks.reshape(3, P, -1)
    arrays["near_masks"] = near_masks
    capacity = -(-T * 5 // (4 * EXPERTS))
    arrays["gate_w"] = _np.asarray(g["L1_ffn_gate_w"])
    arrays["gate_b"] = _np.asarray(g["L1_ffn_gate_b"])
    arrays["w1"] = _np.asarray(g["L1_ffn_w1"])
    arrays["w2"] = _np.asarray(g["L1_ffn_w2"])
    arrays["b1_cols"] = _np.asarray(g["L1_ffn_b1"]).reshape(EXPERTS, -1, P).transpose(0, 2, 1)
    arrays["b2"] = _np.asarray(g["L1_ffn_b2"])
    table = _np.zeros((P, EXPERTS, TT), _np.float32)
    expert = _np.arange(EXPERTS, dtype=_np.float32)[None, :, None]
    arrays["rank"] = table + (EXPERTS - expert)
    arrays["base"] = table + expert * capacity
    arrays["trash_place"] = _np.float32(EXPERTS * capacity) + _np.arange(T, dtype=_np.float32).reshape(TT, P).T
    arrays["prefix"] = _np.triu(_np.ones((P, P), _np.float32))
    nc = _bacc.Bacc("TRN2", target_bir_lowering=False, num_devices=1)
    arrays = {k: _np.ascontiguousarray(v) for k, v in arrays.items()}
    ap = {k: nc.dram_tensor(k, v.shape, mybir.dt.from_np(v.dtype), kind="ExternalInput").ap() for k, v in arrays.items()}
    def scratch(name, shape, dt=F32):
        return nc.dram_tensor(name, shape, dt).ap()
    small_scores = nc.alloc_sbuf_tensor("small_scores", [1, 1], I32)
    qh, ql = (scratch(n, (BG * NC, P, W)) for n in ("qh", "ql"))
    kh, kl, v_img, pe_img, xn_ch, key_ch = (scratch(n, (BG, P, N)) for n in ("kh", "kl", "v_img", "pe_img", "xn_ch", "key_ch"))
    v_tok, xn_tok = (scratch(n, (B, N, CH)) for n in ("v_tok", "xn_tok"))
    attn = scratch("attn", (BG * NC, P, W))
    conv_inputs(nc, ap["x"], ap["w_qkv"], ap["b_qkv"], ap["bv_row"], ap["group_mean"], ap["head_sum"], ap["eye"], qh, ql, kh, kl, v_img, v_tok, small_scores)
    conv_attention(nc, qh, ql, kh, kl, v_img, v_tok, ap["w_pe"], ap["b_pe"], ap["eye"], small_scores, attn, pe_img)
    out = nc.dram_tensor("out_0", (B, CH, N), F32, kind="ExternalOutput").ap()
    t1 = scratch("t1", (B, N, CH))
    near_only = nc.alloc_sbuf_tensor("near_only", [1, 1], I32)
    all_finite = nc.alloc_sbuf_tensor("all_finite", [1, 1], I32)
    t2_stats = nc.alloc_sbuf_tensor("t2_stats", [P, TT, BN6], F32)
    t2 = nc.alloc_sbuf_tensor("t2", [P, TT, CH], F32)
    project_and_norm(nc, attn, pe_img, ap["x"], ap["w_proj"], ap["bp_row"], ap["eye"], ap["w_key"], ap["temperature"],
                     ap["bias"], near_only, t1, xn_tok, xn_ch, key_ch)
    near_attention(nc, t1, xn_tok, xn_ch, key_ch, ap["near_masks"], ap["temperature"], ap["bias"], ap["eye"], near_only, t2, t2_stats)
    dense_attention(nc, t1, xn_tok, xn_ch, key_ch, ap["wide_mask"], ap["temperature"], ap["bias"], ap["eye"], near_only, t2, t2_stats)
    gate_logits = nc.alloc_sbuf_tensor("gate_logits", [P, EXPERTS, TT], F32)
    to_slot = nc.alloc_sbuf_tensor("to_slot", [P, TT], U32)
    from_slot = nc.alloc_sbuf_tensor("from_slot", [P, TT], U32)
    weight = nc.alloc_sbuf_tensor("weight", [P, TT], F32)
    slots = scratch("slots", (EXPERTS * capacity + T, CH))
    results = scratch("results", (EXPERTS * capacity, CH))
    with nc.sbuf_tensor("xn2", [P, TT, CH], F32) as xn2:
        norm_and_gate(nc, t2, t2_stats, ap["gate_w"], ap["gate_b"], ap["eye"], xn2, gate_logits, EXPERTS * capacity, slots)
        route(nc, gate_logits, capacity, ap["rank"], ap["base"], ap["trash_place"], ap["prefix"], to_slot, from_slot, weight)
        scatter_tokens(nc, xn2, to_slot, slots)
    experts(nc, slots, ap["w1"], ap["b1_cols"], ap["w2"], ap["b2"], ap["eye"], capacity, results, weight, all_finite)
    combine(nc, results, from_slot, weight, t2, ap["eye"], all_finite, out)
    r = _run(nc, [arrays], core_ids=[0])
    return r.results[0]["out_0"].reshape(B, CH, IMG, IMG)
```

```python
from contextlib import ExitStack

import concourse.bass as bass
from concourse import mybir

F32 = mybir.dt.float32
F32R = mybir.dt.float32r
BF16 = mybir.dt.bfloat16
I32 = mybir.dt.int32
U32 = mybir.dt.uint32
ALU = mybir.AluOpType
ACT = mybir.ActivationFunctionType
AX = mybir.AxisListType

P = 128
B, CH, IMG = 4, 256, 48
N = IMG * IMG
T = B * N
KT = CH // P
NT = N // P
TT = T // P
W = 384
NC = N // W
SUB = W // P
HEADS, HD = 8, 32
EXPERTS = 8
HG = P // HD
SCALE = HD ** -0.5
MAX_SCORE = 30.0
GN_GROUP = 8
GN_EPS, LN_EPS = 1e-5, 1e-5
WINDOW = 24
OUTSIDE = 10000.0
UNDERFLOW = 110.0
GONE = -1e30
BG = B * KT
BN6, BN2 = 6, 2


class Steps:

    def __init__(self, engine, sem, base=0):
        self.engine, self.sem, self.base, self.n = engine, sem, base, 0

    def then(self, instruction):
        self.n += 1
        instruction.then_inc(self.sem, 1)
        self.engine.wait_ge(self.sem, self.base + self.n)


def conv_inputs(nc, x, w_qkv, b_qkv, bv_row, group_mean, head_sum, eye, qh, ql, kh, kl, v_img, v_tok, small_scores,
                k_first, v_first, q_first):
    with ExitStack() as ctx:
        def sb(name, shape, dt=F32):
            return ctx.enter_context(nc.sbuf_tensor(name, shape, dt))

        def sem(name):
            return ctx.enter_context(nc.semaphore(name))

        x_sb = sb("cx", [P, KT, N])
        xnf = sb("cxnf", [P, KT, W])
        xn = sb("cxn", [P, 2, KT, N], F32R)
        wq_split = sb("cwq_split", [P, 2, KT, 3 * CH], F32R)
        wq = sb("cw", [P, KT, 3 * CH])
        bq = sb("cb", [P, 3 * KT])
        bv = sb("cbv", [P, CH])
        gm = sb("cgm", [P, P])
        stats = sb("cstats", [P, KT, NC, BN6])
        mv = sb("cmv", [P, KT, BN2])
        dev = sb("cdev", [P, KT])
        dev2 = sb("cdev2", [P, KT])
        mean = sb("cmean", [P, KT])
        mhalf = sb("cmhalf", [P, KT])
        rstd = sb("crstd", [P, KT])
        veps = sb("cveps", [P, KT])
        qkf = sb("cqkf", [P, 2, 2 * KT, W])
        hi = sb("chi", [P, 2, 2 * KT, W], F32R)
        lo = sb("clo", [P, 2, 2 * KT, W], F32R)
        vi = sb("cvi", [P, 2, KT, W])
        vt = sb("cvt", [P, 2, SUB, CH])
        heads = sb("cheads", [P, P])
        heads16 = sb("cheads16", [P, P], BF16)
        ident = sb("cident", [P, P])
        squares = sb("csquares", [P, 2, 2 * KT, W], BF16)
        norms = sb("cnorms", [P, 2 * KT, B * NC])
        peaks = sb("cpeaks", [P, 2 * KT, B])
        bound = sb("cbound", [P, KT, B])
        worst = sb("cworst", [P, 1])
        worst_all = sb("cworst_all", [1, 1])
        NB_IMG, NB_TOK, NB_NORM = 3, 2, 2
        ps_img = [ctx.enter_context(nc.psum_tensor(f"cpi{i}", [P, 512], F32)) for i in range(NB_IMG)]
        ps_tok = [ctx.enter_context(nc.psum_tensor(f"cpt{i}", [P, 512], F32)) for i in range(NB_TOK)]
        ps_norm = [ctx.enter_context(nc.psum_tensor(f"cpn{i}", [P, 512], F32)) for i in range(NB_NORM)]
        ps_st = ctx.enter_context(nc.psum_tensor("cps", [P, 512], F32))

        consts_in = sem("c_consts_in")
        x_in = sem("c_x_in")
        xn_done = sem("c_xn_done")
        aggr_done = sem("c_aggr_done")
        mean_mm = sem("c_mean_mm")
        dev_done = sem("c_dev_done")
        var_mm = sem("c_var_mm")
        veps_done = sem("c_veps_done")
        rstd_done = sem("c_rstd_done")
        mhalf_done = sem("c_mhalf_done")
        dve_step = sem("c_dve_step")
        img_mm = sem("c_img_mm")
        img_out = sem("c_img_out")
        tok_mm = sem("c_tok_mm")
        tok_out = sem("c_tok_out")
        high_done = sem("c_high_done")
        split_done = sem("c_split_done")
        heads_done = sem("c_heads_done")
        squares_done = sem("c_squares_done")
        norm_mm = sem("c_norm_mm")
        norm_done = sem("c_norm_done")
        worst_done = sem("c_worst_done")
        worst_mm = sem("c_worst_mm")
        first_in = sem("c_first_in")
        stored = [sem(f"c_stored{i}") for i in range(2)]
        block = ctx.enter_context(nc.Block())
        HI, LO = 0, 1
        PARTS = ((HI, HI), (HI, LO), (LO, HI))
        MEAN_AT, VAR_AT = 2, 3
        MI, MQK = 3 * KT, 2 * KT
        SLOT_STORES = 6 * 16
        SPLIT_WQ = 2
        PREPARE = 4 + 2 * NC

        @block.sync
        def _(sp):
            def load_x(b):
                sp.dma_start(x_sb[:], x[bass.ds(b, 1)].rearrange("a (k p) n -> p (a k) n", p=P)).then_inc(x_in, 16)

            load_x(0)
            sp.dma_start(wq[:], w_qkv.rearrange("(k p) n -> p k n", p=P)).then_inc(consts_in, 16)
            sp.dma_start(bq[:], b_qkv[:]).then_inc(consts_in, 16)
            sp.dma_start(bv[:], bv_row.partition_broadcast(P)).then_inc(consts_in, 16)
            sp.dma_start(gm[:], group_mean[:]).then_inc(consts_in, 16)
            sp.dma_start(heads[:], head_sum[:]).then_inc(consts_in, 16)
            sp.dma_start(ident[:], eye[:]).then_inc(consts_in, 16)

            def store_chunks(b):
                for c in range(NC):
                    s = c % 2
                    cols = slice(c * W, (c + 1) * W)
                    sp.wait_ge(tok_out, 1 + (b * NC + c) * SUB + SUB)
                    sp.dma_start(v_tok[bass.ds(b, 1), c * W:(c + 1) * W, :].rearrange("a (j p) n -> p (a j) n", p=P),
                                 vt[:, s]).then_inc(stored[s], 16)
                    sp.wait_ge(split_done, 1 + b * NC + c + 1)
                    for dram, part, m in ((qh, hi, 0), (kh, hi, KT), (ql, lo, 0), (kl, lo, KT)):
                        if m == 0:
                            to = dram.rearrange("(g c) p n -> g c p n", c=NC)[bass.ds(b * KT, KT), c]
                        else:
                            to = dram[bass.ds(b * KT, KT), :, cols]
                        sp.dma_start(to.rearrange("k p n -> p k n"),
                                     part[:, s, m:m + KT, :].bitcast(F32)).then_inc(stored[s], 16)
                    sp.wait_ge(img_out, 1 + (b * NC + c) * MI + MI)
                    sp.dma_start(v_img[bass.ds(b * KT, KT), :, cols].rearrange("k p n -> p k n"),
                                 vi[:, s]).then_inc(stored[s], 16)

            for counter in stored:
                sp.sem_inc(counter, 1)
            with sp.Fori(0, B - 1) as b:
                sp.wait_ge(xn_done, (b + 1) * NC)
                load_x(b + 1)
                store_chunks(b)
            for counter in stored:
                sp.wait_ge(counter, 1 + (NC // 2) * SLOT_STORES)
            load_queries(sp, q_first, (qh, ql), 0, first_in)
            load_keys(sp, k_first, (kh, kl), 0, range(4), first_in)
            load_values(sp, v_first, v_tok, 0, 0, first_in)
            store_chunks(B - 1)
            sp.wait_ge(first_in, (4 + 4 + 1) * 16)
            for s in range(2):
                sp.wait_ge(stored[s], 1 + B * (NC // 2) * SLOT_STORES)

        @block.vector
        def _(dve):
            for counter in (veps_done, tok_out, norm_done):
                dve.sem_inc(counter, 1)
            dve.sem_inc(norm_done, NB_NORM - 1)
            dve.wait_ge(consts_in, 6 * 16)
            nc.vector.tensor_copy(heads16[:], heads[:]).then_inc(heads_done, 1)

            def statistics(b, st):
                dve.wait_ge(x_in, b * 16 + 16)
                for k in range(KT):
                    for c in range(NC):
                        i = nc.vector.bn_stats(stats[:, k, c, :], x_sb[:, k, c * W:(c + 1) * W])
                st.then(i)
                nc.vector.memset(dev[:], 0.0)
                for k in range(KT):
                    i = nc.vector.bn_aggr(mv[:, k, :], stats[:, k].rearrange("p c s -> p (c s)"))
                i.then_inc(aggr_done, 1)

            def deviations(b, st):
                dve.wait_ge(mean_mm, b + 1)
                dve.wait_ge(aggr_done, b + 1)
                st.then(nc.vector.tensor_copy(mean[:], ps_st[:, 0:KT]))
                st.then(nc.vector.tensor_tensor(dev[:], mv[:, :, 0], mean[:], ALU.subtract))
                st.then(nc.vector.tensor_tensor(dev2[:], dev[:], dev[:], ALU.mult))
                nc.vector.tensor_tensor(dev2[:], dev2[:], mv[:, :, 1], ALU.add).then_inc(dev_done, 1)

            def variances(b):
                dve.wait_ge(var_mm, b + 1)
                nc.vector.tensor_scalar(veps[:], ps_st[:, 8:8 + KT], GN_EPS, None, ALU.add).then_inc(veps_done, 1)

            def normalise(b, chunks, last_used, st):
                dve.wait_ge(rstd_done, b + 1)
                for c in chunks:
                    if last_used:
                        dve.wait_ge(img_mm, 1 + ((b - 1) * NC + c + 1) * MI)
                        dve.wait_ge(tok_mm, 1 + ((b - 1) * NC + c + 1) * SUB)
                    cols = slice(c * W, (c + 1) * W)
                    for k in range(KT):
                        i = nc.vector.tensor_scalar(xnf[:, k], x_sb[:, k, cols], mean[:, k:k + 1], rstd[:, k:k + 1],
                                                    ALU.subtract, ALU.mult)
                    st.then(i)
                    st.then(nc.vector.tensor_copy(xn[:, HI, :, cols], xnf[:]))
                    nc.vector.tensor_tensor(xn[:, LO, :, cols], xnf[:], xn[:, HI, :, cols].bitcast(F32), ALU.subtract
                                            ).then_inc(xn_done, 1)
                    dve.wait_ge(xn_done, b * NC + c + 1)

            def finish_chunk(b, c):
                s = c % 2
                if c < 2:
                    dve.wait_ge(stored[s], 1 + b * (NC // 2) * SLOT_STORES)
                else:
                    dve.wait_ge(stored[s], 1 + (b * (NC // 2) + c // 2) * SLOT_STORES)
                for j in range(SUB):
                    dve.wait_ge(tok_mm, 1 + (b * NC + c) * SUB + j + 1)
                    nc.vector.tensor_tensor(vt[:, s, j, :], ps_tok[(c * SUB + j) % NB_TOK][:, 0:CH], bv[:],
                                            ALU.add).then_inc(tok_out, 1)
                dve.wait_ge(img_out, 1 + (b * NC + c) * MI + MQK)
                nc.vector.tensor_copy(hi[:, s], qkf[:, s]).then_inc(high_done, 1)
                for m in range(MQK):
                    dve.wait_ge(norm_mm, 1 + MQK + (b * NC + c) * MQK + m + 1)
                    nc.vector.reduce_max(norms[:, m, bass.ds(b * NC + c, 1)], ps_norm[m % NB_NORM][:, 0:W],
                                         AX.X).then_inc(norm_done, 1)

            def one_batch(b, more):
                st = Steps(dve, dve_step, SPLIT_WQ + (b + 1) * PREPARE)
                for c in range(NC):
                    finish_chunk(b, c)
                    if more and c == 1:
                        statistics(b + 1, st)
                    if more and c == MEAN_AT:
                        deviations(b + 1, st)
                    if more and c == VAR_AT:
                        variances(b + 1)
                    if more and c == NC - 2:
                        normalise(b + 1, range(NC - 2), True, st)
                if more:
                    normalise(b + 1, range(NC - 2, NC), True, st)

            first = Steps(dve, dve_step)
            first.then(nc.vector.tensor_copy(wq_split[:, HI], wq[:]))
            first.then(nc.vector.tensor_tensor(wq_split[:, LO], wq[:], wq_split[:, HI].bitcast(F32), ALU.subtract))
            assert first.n == SPLIT_WQ
            statistics(0, first)
            deviations(0, first)
            variances(0)
            normalise(0, range(NC), False, first)
            with dve.Fori(0, B - 1) as b:
                one_batch(b, True)
            one_batch(B - 1, False)
            st = Steps(dve, dve_step, SPLIT_WQ + B * PREPARE)
            dve.wait_ge(norm_done, NB_NORM + B * NC * MQK)
            st.then(nc.vector.reduce_max(peaks[:], norms[:].rearrange("p m (b c) -> p m b c", b=B), AX.X))
            st.then(nc.vector.tensor_tensor(bound[:], peaks[:, 0:KT], peaks[:, KT:MQK], ALU.mult))
            nc.vector.reduce_max(worst[:], bound[:], AX.XY).then_inc(worst_done, 1)
            dve.wait_ge(worst_mm, 1)
            st.then(nc.vector.reduce_max(worst_all[:], ps_st[0:1, 128:256], AX.X))
            st.then(nc.vector.tensor_scalar(small_scores[:], worst_all[:], 0.98 * (MAX_SCORE / SCALE) ** 2, None, ALU.is_lt))

        @block.gpsimd
        def _(pool):
            nc.gpsimd.memset(mhalf[:], -0.5).then_inc(mhalf_done, 1)
            pool.wait_ge(mhalf_done, 1)
            pool.sem_inc(split_done, 1)

            def deviation(b):
                pool.wait_ge(veps_done, 1 + b + 1)
                nc.gpsimd.tensor_tensor(rstd[:], veps[:], mhalf[:], ALU.pow).then_inc(rstd_done, 1)

            def one_batch(b, more):
                for c in range(NC):
                    pool.wait_ge(high_done, b * NC + c + 1)
                    nc.gpsimd.tensor_tensor(lo[:, c % 2], qkf[:, c % 2], hi[:, c % 2].bitcast(F32), ALU.subtract
                                            ).then_inc(split_done, 1)
                    if more and c == VAR_AT:
                        deviation(b + 1)

            deviation(0)
            with pool.Fori(0, B - 1) as b:
                one_batch(b, True)
            one_batch(B - 1, False)

        @block.scalar
        def _(act):
            act.sem_inc(img_out, 1)
            with act.Fori(0, B) as b:
                for c in range(NC):
                    s = c % 2
                    act.wait_ge(stored[s], 1 + (b * (NC // 2) + c // 2) * SLOT_STORES)
                    act.wait_ge(split_done, 1 + b * NC + c - 1) if c else act.wait_ge(split_done, 1 + b * NC)
                    for m in range(MI):
                        act.wait_ge(img_mm, 1 + (b * NC + c) * MI + m + 1)
                        dst = qkf[:, s, m, :] if m < MQK else vi[:, s, m - MQK, :]
                        src = ps_img[(c * MI + m) % NB_IMG][:, 0:W]
                        if m == 0:
                            act.wait_ge(norm_mm, 1 + (b * NC + c) * MQK)
                        if m < MQK:
                            nc.scalar.activation(squares[:, s, m, :], src, ACT.Square, bias=bq[:, m:m + 1]
                                                 ).then_inc(squares_done, 1)
                        nc.scalar.activation(dst, src, ACT.Identity, bias=bq[:, m:m + 1]).then_inc(img_out, 1)

        @block.tensor
        def _(pe):
            for counter in (img_mm, tok_mm, norm_mm):
                pe.sem_inc(counter, 1)
            pe.sem_inc(norm_mm, MQK)
            pe.wait_ge(consts_in, 6 * 16)
            pe.wait_ge(heads_done, 1)
            pe.wait_ge(dve_step, SPLIT_WQ)

            def group_means(b):
                pe.wait_ge(aggr_done, b + 1)
                pe.wait_ge(veps_done, 1 + b)
                nc.tensor.matmul(ps_st[:, 0:KT], gm[:], mv[:, :, 0], start=True, stop=True).then_inc(mean_mm, 1)

            def group_variances(b):
                pe.wait_ge(dev_done, b + 1)
                nc.tensor.matmul(ps_st[:, 8:8 + KT], gm[:], dev2[:], start=True, stop=True).then_inc(var_mm, 1)

            def norm_products(b, c):
                for m in range(MQK):
                    u = (b * NC + c) * MQK + m
                    pe.wait_ge(squares_done, u + 1)
                    pe.wait_ge(norm_done, 1 + u)
                    nc.tensor.matmul(ps_norm[m % NB_NORM][:, 0:W], heads16[:], squares[:, c % 2, m, :],
                                     start=True, stop=True).then_inc(norm_mm, 1)

            def one_batch(b, more):
                for c in range(NC):
                    pe.wait_ge(xn_done, b * NC + c + 1)
                    cols = slice(c * W, (c + 1) * W)
                    for m in range(MI):
                        u = c * MI + m
                        if u >= NB_IMG:
                            pe.wait_ge(img_out, 1 + b * NC * MI + u - NB_IMG + 1)
                        else:
                            pe.wait_ge(img_out, 1 + b * NC * MI)
                        for k in range(KT):
                            for p, q in PARTS:
                                i = nc.tensor.matmul(ps_img[u % NB_IMG][:, 0:W], wq_split[:, p, k, m * P:(m + 1) * P],
                                                     xn[:, q, k, cols], start=(k == 0 and (p, q) == PARTS[0]),
                                                     stop=(k == KT - 1 and (p, q) == PARTS[-1]))
                        i.then_inc(img_mm, 1)
                        if m == 1 and c > 0:
                            norm_products(b, c - 1)
                        if m % 2:
                            j = m // 2
                            u = c * SUB + j
                            if u >= NB_TOK:
                                pe.wait_ge(tok_out, 1 + b * NC * SUB + u - NB_TOK + 1)
                            else:
                                pe.wait_ge(tok_out, 1 + b * NC * SUB)
                            for k in range(KT):
                                for p, q in PARTS:
                                    i = nc.tensor.matmul(ps_tok[u % NB_TOK][:, 0:CH],
                                                         xn[:, p, k, c * W + j * P:c * W + (j + 1) * P],
                                                         wq_split[:, q, k, 2 * CH:3 * CH], start=(k == 0 and (p, q) == PARTS[0]),
                                                         stop=(k == KT - 1 and (p, q) == PARTS[-1]))
                            i.then_inc(tok_mm, 1)
                    if c == NC - 1:
                        norm_products(b, c)
                    if more and c == MEAN_AT:
                        group_means(b + 1)
                    if more and c == VAR_AT:
                        group_variances(b + 1)

            group_means(0)
            group_variances(0)
            with pe.Fori(0, B - 1) as b:
                one_batch(b, True)
            one_batch(B - 1, False)
            pe.wait_ge(worst_done, 1)
            nc.tensor.transpose(ps_st[0:1, 128:256], worst[:], ident[:]).then_inc(worst_mm, 1)


def load_queries(queue, q_tile, parts, chunk, loaded):
    qh, ql = parts
    for r, part in enumerate((qh, qh, ql, ql)):
        queue.dma_start(q_tile[r * HD:(r + 1) * HD].bitcast(F32),
                        part[bass.ds(chunk, 1)].rearrange("a (h d) n -> d (a h) n", d=HD)).then_inc(loaded, 16)


def load_keys(queue, k_tile, parts, group, rows, loaded):
    kh, kl = parts
    for r, part in enumerate((kh, kl, kh, kl)):
        if r in rows:
            queue.dma_start(k_tile[r * HD:(r + 1) * HD].bitcast(F32),
                            part[bass.ds(group, 1)].rearrange("a (h d) n -> d (a h) n", d=HD)).then_inc(loaded, 16)


def load_values(queue, v_tile, v_tok, b, g, loaded):
    queue.dma_start(v_tile[:], v_tok[bass.ds(b, 1), :, g * P:(g + 1) * P].rearrange("a (t p) c -> p (a t) c", p=P)
                    ).then_inc(loaded, 16)


def conv_attention(nc, k_first, v_first, q_first, qh, ql, kh, kl, v_img, v_tok, w_pe, b_pe, eye, small_scores, attn, pe_img):
    with ExitStack() as ctx:
        def sb(name, shape, dt=F32):
            return ctx.enter_context(nc.sbuf_tensor(name, shape, dt))

        def sem(name):
            return ctx.enter_context(nc.semaphore(name))

        G3 = NT // SUB
        NP_SLOTS = 2 * HG
        MAXES = HG * SUB * 2
        UNITS = G3 * HG
        ADDS = (G3 - 1) * HG
        DIRECT = 2
        EARLY = HG + 1
        CHUNKS = BG * NC
        k_sb = [k_first, sb("ak", [P, HG, N], F32R)]
        v_sb = [v_first, sb("av", [P, NT, P])]
        q_sb = [q_first, sb("aq", [P, HG, W], F32R)]
        probs = sb("aprobs", [P, NP_SLOTS, SUB, W])
        sums = sb("asums", [P, HG, SUB, W])
        mx = sb("amx", [P, 2, HG * SUB])
        top = sb("atop", [P, HG * SUB])
        diag = sb("adiag", [P, HG, W])
        ident = sb("aident", [P, P])
        minus = sb("aminus", [P, P])
        ones = sb("aones", [P, HD])
        rden = sb("arden", [P, W])
        o_sb = sb("ao", [P, 2, W])
        vc = sb("avc", [P, IMG, IMG])
        tap = sb("atap", [P, IMG, IMG])
        conv = sb("aconv", [P, IMG, IMG])
        wpe = sb("awpe", [P, KT, 9])
        bpe = sb("abpe", [P, KT])
        ps_s = [ctx.enter_context(nc.psum_tensor(f"ass{i}", [P, SUB, 512], F32)) for i in range(2)]
        ps_o = ctx.enter_context(nc.psum_tensor("aso", [P, 512], F32))
        ps_d = ctx.enter_context(nc.psum_tensor("asd", [P, 512], F32))

        consts_in = sem("a_consts_in")
        taps_in = sem("a_taps_in")
        consts_set = sem("a_consts_set")
        kv_in = [sem(f"a_kv_in{g}") for g in range(KT)]
        q_in = [sem(f"a_q_in{i}") for i in range(2)]
        max_mm = sem("a_max_mm")
        max_done = sem("a_max_done")
        diag_done = sem("a_diag_done")
        top_done = sem("a_top_done")
        score_mm = sem("a_score_mm")
        exp_done = sem("a_exp_done")
        add_done = sem("a_add_done")
        pv_done = sem("a_pv_done")
        den_mm = sem("a_den_mm")
        raw_done = sem("a_raw_done")
        den_read = sem("a_den_read")
        out_done = sem("a_out_done")
        o_stored = [sem(f"a_o_stored{i}") for i in range(2)]
        img_in = sem("a_img_in")
        pool_step = sem("a_pool_step")
        conv_stored = sem("a_conv_stored")
        block = ctx.enter_context(nc.Block())

        @block.sync
        def _(sp):
            for counter in o_stored:
                sp.sem_inc(counter, 1)
            sp.sem_inc(kv_in[0], 5 * 16)
            sp.sem_inc(q_in[0], 4 * 16)
            sp.dma_start(ident[:], eye[:]).then_inc(consts_in, 16)

            KV_LOADS = 3

            def load_kv(b, g, piece):
                if piece < 2:
                    load_keys(sp, k_sb[g], (kh, kl), b * KT + g, (2 * piece, 2 * piece + 1), kv_in[g])
                else:
                    load_values(sp, v_sb[g], v_tok, b, g, kv_in[g])

            def load_q(n, i):
                load_queries(sp, q_sb[i], (qh, ql), n, q_in[i])

            def store_out(n, i):
                sp.wait_ge(out_done, 1 + n + 1)
                sp.dma_start(attn[bass.ds(n, 1)].rearrange("a p n -> p (a n)"), o_sb[:, i]).then_inc(o_stored[i], 16)

            def one_batch(b, last):
                for c in range(KT * NC):
                    n = b * KT * NC + c
                    if not (last and c == KT * NC - 1):
                        load_q(n + 1, (c + 1) % 2)
                    piece = c % NC - 1
                    if 0 <= piece < KV_LOADS:
                        if c < NC:
                            load_kv(b, 1, piece)
                        elif not last:
                            load_kv(b + 1, 0, piece)
                    store_out(n, c % 2)

            with sp.Fori(0, B - 1) as b:
                one_batch(b, False)
            one_batch(B - 1, True)
            for i in range(2):
                sp.wait_ge(o_stored[i], 1 + CHUNKS // 2 * 16)

        @block.gpsimd
        def _(pool):
            pool.dma_start(wpe[:], w_pe.rearrange("(k p) t -> p k t", p=P)).then_inc(taps_in, 16)
            pool.dma_start(bpe[:], b_pe[:]).then_inc(taps_in, 16)
            pool.wait_ge(taps_in, 32)
            nc.gpsimd.memset(minus[:], -1.0).then_inc(consts_set, 1)
            nc.gpsimd.memset(ones[:], 1.0).then_inc(consts_set, 1)
            with pool.Fori(0, B) as b:
                for g in range(KT):
                    st = Steps(pool, pool_step, (b * KT + g) * 18)
                    pool.wait_ge(img_in, (b * KT + g + 1) * 16)
                    order = [4, 0, 1, 2, 3, 5, 6, 7, 8]
                    for t in order:
                        dy, dx = t // 3 - 1, t % 3 - 1
                        y0, y1 = max(0, -dy), IMG - max(0, dy)
                        x0, x1 = max(0, -dx), IMG - max(0, dx)
                        tap_w = wpe[:, g, t:t + 1].to_broadcast([P, N])
                        if t == 4:
                            pool.wait_ge(conv_stored, 1 + (b * KT + g) * 16)
                            st.then(nc.gpsimd.tensor_tensor(conv[:].rearrange("p y x -> p (y x)"), vc[:].rearrange("p y x -> p (y x)"),
                                                            tap_w, ALU.mult))
                            st.then(nc.gpsimd.tensor_tensor(conv[:].rearrange("p y x -> p (y x)"), conv[:].rearrange("p y x -> p (y x)"),
                                                            bpe[:, g:g + 1].to_broadcast([P, N]), ALU.add))
                        else:
                            st.then(nc.gpsimd.tensor_tensor(tap[:].rearrange("p y x -> p (y x)"), vc[:].rearrange("p y x -> p (y x)"),
                                                            tap_w, ALU.mult))
                            st.then(nc.gpsimd.tensor_tensor(conv[:, y0:y1, x0:x1], conv[:, y0:y1, x0:x1],
                                                            tap[:, y0 + dy:y1 + dy, x0 + dx:x1 + dx], ALU.add))
                    assert st.n == 18

        @block.vector
        def _(dve):
            for counter in (max_done, add_done, raw_done, den_read, out_done):
                dve.sem_inc(counter, 1)
            dve.sem_inc(add_done, HG)
            dve.wait_ge(consts_in, 16)

            def take_maxima(n):
                for u in range(MAXES):
                    dve.wait_ge(max_mm, 1 + n * MAXES + u + 1)
                    nc.vector.reduce_max(mx[:, u % 2, u // 2:u // 2 + 1], ps_s[u % 2][:, :, 0:W], AX.XY).then_inc(max_done, 1)
                dve.wait_ge(max_done, 1 + n * MAXES + MAXES)
                nc.vector.tensor_tensor(top[:], mx[:, 0], mx[:, 1], ALU.max).then_inc(top_done, 1)
                dve.wait_ge(top_done, n + 1)
                for h in range(HG):
                    for j in range(SUB):
                        last = nc.vector.tensor_scalar(diag[:, h, j * P:(j + 1) * P], ident[:], top[:, h * SUB + j:h * SUB + j + 1],
                                                       None, ALU.mult)
                last.then_inc(diag_done, 1)

            def add_probs(n, g3):
                for h in range(HG):
                    u = g3 * HG + h
                    dve.wait_ge(exp_done, 3 + n * UNITS + u + 1)
                    tiles = slice(0, SUB - DIRECT * (g3 == G3 - 1))
                    if g3 == 1:
                        first = probs[:, h]
                        dve.wait_ge(den_mm, 1 + n)
                    else:
                        first = sums[:, h]
                        dve.wait_ge(add_done, 1 + HG + n * ADDS + (g3 - 2) * HG + h + 1)
                    nc.vector.tensor_tensor(sums[:, h, tiles], first[:, tiles], probs[:, u % NP_SLOTS, tiles], ALU.add
                                            ).then_inc(add_done, 1)

            def start_chunk(n, shifted):
                if shifted:
                    take_maxima(n)
                add_probs(n, 1)

            def finish_chunk(n, pair, i, shifted, more):
                for g3 in range(2, G3):
                    add_probs(n, g3)
                dve.wait_ge(pv_done, 3 + n * G3 + G3)
                dve.wait_ge(o_stored[i], 1 + pair * 16)
                nc.vector.tensor_copy(o_sb[:, i], ps_o[:, 0:W]).then_inc(raw_done, 1)
                if more:
                    start_chunk(n + 1, shifted)
                dve.wait_ge(den_mm, 1 + n + 1)
                nc.vector.reciprocal(rden[:], ps_d[:, 0:W]).then_inc(den_read, 1)
                dve.wait_ge(den_read, 1 + n + 1)
                dve.wait_ge(raw_done, 1 + n + 1)
                nc.vector.tensor_tensor(o_sb[:, i], o_sb[:, i], rden[:], ALU.mult).then_inc(out_done, 1)

            def attend(shifted):
                start_chunk(0, shifted)
                with dve.Fori(0, CHUNKS // 2 - 1) as pair:
                    for i in range(2):
                        finish_chunk(pair * 2 + i, pair, i, shifted, True)
                finish_chunk(CHUNKS - 2, CHUNKS // 2 - 1, 0, shifted, True)
                finish_chunk(CHUNKS - 1, CHUNKS // 2 - 1, 1, shifted, False)

            small = dve.value_load(small_scores[0:1, 0:1], min_val=0, max_val=1)
            with dve.If(small):
                attend(False)
            with dve.Else():
                attend(True)

        @block.scalar
        def _(act):
            act.sem_inc(exp_done, 3)
            act.sem_inc(conv_stored, 1)
            FREED = [None, 0] + [HG * max(1, g3 - 2) for g3 in range(2, G3)]
            with act.Fori(0, B) as b:
                for g in range(KT):
                    act.dma_start(vc[:].rearrange("p y x -> p (y x)"),
                                  v_img[bass.ds(b * KT + g, 1)].rearrange("a p n -> p (a n)")).then_inc(img_in, 16)
                    with act.Fori(0, NC // 2) as cp:
                        for i in range(2):
                            n = (b * KT + g) * NC + cp * 2 + i
                            for u in range(UNITS):
                                if u % HG == 0:
                                    act.wait_ge(pv_done, 1 + n * G3 + u // HG + 1)
                                if u < HG:
                                    act.wait_ge(add_done, 1 + n * ADDS)
                                else:
                                    act.wait_ge(add_done, 1 + n * ADDS + FREED[u // HG] + u % HG + 1)
                                act.wait_ge(score_mm, 1 + n * UNITS + u + 1)
                                nc.scalar.activation(probs[:, u % NP_SLOTS], ps_s[u % 2][:, :, 0:W], ACT.Exp, scale=SCALE
                                                     ).then_inc(exp_done, 1)
                    act.wait_ge(pool_step, (b * KT + g + 1) * 18)
                    act.dma_start(pe_img[bass.ds(b * KT + g, 1)].rearrange("a p n -> p (a n)"),
                                  conv[:].rearrange("p y x -> p (y x)")).then_inc(conv_stored, 16)
            act.wait_ge(conv_stored, 1 + BG * 16)

        @block.tensor
        def _(pe):
            for counter in (max_mm, score_mm, pv_done, den_mm):
                pe.sem_inc(counter, 1)
            pe.sem_inc(pv_done, 2)
            pe.wait_ge(consts_set, 2)
            def first_pass(n, g, i):
                for u in range(MAXES):
                    h, j, half = u // (2 * SUB), u // 2 % SUB, u % 2
                    if u < 2:
                        pe.wait_ge(exp_done, 3 + n * UNITS)
                    else:
                        pe.wait_ge(max_done, 1 + n * MAXES + u - 1)
                    for a in range(SUB):
                        key = (half * SUB + a) * W
                        last = nc.tensor.matmul(ps_s[u % 2][:, a, 0:W], q_sb[i][:, h, j * P:(j + 1) * P],
                                                k_sb[g][:, h, key:key + W], start=True, stop=True)
                    last.then_inc(max_mm, 1)
                pe.wait_ge(max_done, 1 + n * MAXES + MAXES)
                pe.wait_ge(diag_done, n + 1)

            def scores(n, g, i, u, shifted):
                g3, h = u // HG, u % HG
                if u >= 2 or not shifted:
                    pe.wait_ge(exp_done, 1 + n * UNITS + u + 1)
                for a in range(SUB):
                    key = (g3 * SUB + a) * P
                    last = nc.tensor.matmul(ps_s[u % 2][:, a, 0:W], k_sb[g][:, h, key:key + P], q_sb[i][:, h, :],
                                            start=True, stop=not shifted)
                    if shifted:
                        last = nc.tensor.matmul(ps_s[u % 2][:, a, 0:W], minus[:], diag[:, h, :], start=False, stop=True)
                last.then_inc(score_mm, 1)

            def values(n, g, g3, a):
                kt = g3 * SUB + a
                for h in range(HG):
                    u = g3 * HG + h
                    if a == 0:
                        pe.wait_ge(exp_done, 3 + n * UNITS + u + 1)
                    if kt == 0 and h == 0:
                        pe.wait_ge(raw_done, 1 + n)
                    last = nc.tensor.matmul(ps_o[h * HD:(h + 1) * HD, 0:W], v_sb[g][:, kt, h * HD:(h + 1) * HD],
                                            probs[:, u % NP_SLOTS, a, :], start=(kt == 0), stop=(kt == NT - 1))
                if kt >= NT - DIRECT:
                    if kt == NT - DIRECT:
                        pe.wait_ge(den_read, 1 + n)
                    for h in range(HG):
                        last = nc.tensor.matmul(ps_d[h * HD:(h + 1) * HD, 0:W], ones[:], probs[:, (g3 * HG + h) % NP_SLOTS, a, :],
                                                start=(kt == NT - DIRECT), stop=False)
                if a == SUB - 1:
                    last.then_inc(pv_done, 1)

            def denominators(n):
                pe.wait_ge(add_done, 1 + HG + n * ADDS + ADDS)
                for a in range(SUB):
                    for h in range(HG):
                        last = nc.tensor.matmul(ps_d[h * HD:(h + 1) * HD, 0:W], ones[:], sums[:, h, a, :],
                                                start=False, stop=(a == SUB - 1))
                last.then_inc(den_mm, 1)

            def middle(n, g, i, shifted):
                for g3 in range(1, G3):
                    for h in range(HG):
                        if g3 * HG + h >= EARLY:
                            scores(n, g, i, g3 * HG + h, shifted)
                        if h >= HG - SUB:
                            values(n, g, g3 - 1, h - (HG - SUB))

            def wait_inputs(b, g, cp, i):
                pe.wait_ge(kv_in[g], (b + 1) * 5 * 16)
                pe.wait_ge(q_in[i], ((b * KT + g) * (NC // 2) + cp + 1) * 4 * 16)

            def chunk_number(b, g, cp, i):
                return (b * KT + g) * NC + cp * 2 + i

            def attend_shifted():
                with pe.Fori(0, B) as b:
                    for g in range(KT):
                        with pe.Fori(0, NC // 2) as cp:
                            for i in range(2):
                                n = chunk_number(b, g, cp, i)
                                wait_inputs(b, g, cp, i)
                                first_pass(n, g, i)
                                for u in range(EARLY):
                                    scores(n, g, i, u, True)
                                middle(n, g, i, True)
                                for a in range(SUB):
                                    values(n, g, G3 - 1, a)
                                denominators(n)

            def middle_and_end(this, following):
                n, g = chunk_number(*this), this[1]
                middle(n, g, this[3], False)
                if following:
                    wait_inputs(*following)
                for u in range(EARLY):
                    if following:
                        scores(chunk_number(*following), following[1], following[3], u, False)
                    if u < SUB:
                        values(n, g, G3 - 1, u)
                denominators(n)

            def group(b, g, following):
                LAST = NC // 2 - 1
                with pe.Fori(0, LAST) as cp:
                    middle_and_end((b, g, cp, 0), (b, g, cp, 1))
                    middle_and_end((b, g, cp, 1), (b, g, cp + 1, 0))
                middle_and_end((b, g, LAST, 0), (b, g, LAST, 1))
                middle_and_end((b, g, LAST, 1), following)

            def attend_small():
                wait_inputs(0, 0, 0, 0)
                for u in range(EARLY):
                    scores(0, 0, 0, u, False)
                with pe.Fori(0, B - 1) as b:
                    for g in range(KT):
                        group(b, g, (b, g + 1, 0, 0) if g < KT - 1 else (b + 1, 0, 0, 0))
                for g in range(KT):
                    group(B - 1, g, (B - 1, g + 1, 0, 0) if g < KT - 1 else None)

            small = pe.value_load(small_scores[0:1, 0:1], min_val=0, max_val=1)
            with pe.If(small):
                attend_small()
            with pe.Else():
                attend_shifted()
def project_and_norm(nc, attn, pe_img, x, w_proj, bp_row, eye, w_key, temperature, bias, near_only, t_sb, xn_tok, xn_ch, key_ch):
    with ExitStack() as ctx:
        def sb(name, shape, dt=F32):
            return ctx.enter_context(nc.sbuf_tensor(name, shape, dt))

        def sem(name):
            return ctx.enter_context(nc.semaphore(name))

        CHUNKS = B * NC
        SLOTS = 3
        a_in = sb("pa", [P, SLOTS, KT, W])
        c_in = sb("pc", [P, SLOTS, KT, W])
        x_in = sb("px", [P, SLOTS, KT, W])
        both = sb("pboth", [P, 2, KT, W])
        wp = sb("pwp", [P, KT, CH])
        wk = sb("pwk", [P, KT, CH])
        bp = sb("pbp", [P, CH])
        ident = sb("pident", [P, P])
        xn = sb("pxn", [P, 2, SUB, CH])
        xt = sb("pxt", [P, 2, KT, W])
        key = sb("pkey", [P, 2, KT, W])
        stats = sb("pstats", [P, SUB, BN6])
        mv = sb("pmv", [P, SUB, BN2])
        veps = sb("pveps", [P, SUB])
        rstd = sb("prstd", [P, SUB])
        mhalf = sb("pmhalf", [P, SUB])
        squares = sb("psquares", [P, KT, W], BF16)
        ones16 = sb("pones16", [P, P], BF16)
        norms = sb("pnorms", [P, CHUNKS])
        temp = sb("ptemp", [P, 1])
        bcol = sb("pbcol", [P, 1])
        test = sb("ptest", [P, 6])
        ps_t = [ctx.enter_context(nc.psum_tensor(f"ppt{i}", [P, 512], F32)) for i in range(SUB)]
        ps_x = [ctx.enter_context(nc.psum_tensor(f"ppx{i}", [P, 512], F32)) for i in range(KT)]
        ps_k = [ctx.enter_context(nc.psum_tensor(f"ppk{i}", [P, 512], F32)) for i in range(KT)]

        ps_n = ctx.enter_context(nc.psum_tensor("ppn", [P, 512], F32))
        ones_done = sem("p_ones_done")
        squares_done = sem("p_squares_done")
        norm_mm = sem("p_norm_mm")
        norm_done = sem("p_norm_done")
        consts_in = sem("p_consts_in")
        mhalf_done = sem("p_mhalf_done")
        chunk_in = [sem(f"p_chunk_in{i}") for i in range(SLOTS)]
        both_done = sem("p_both_done")
        tok_mm = sem("p_tok_mm")
        tok_done = sem("p_tok_done")
        dve_step = sem("p_dve_step")
        veps_done = sem("p_veps_done")
        rstd_done = sem("p_rstd_done")
        xn_done = sem("p_xn_done")
        xt_mm = sem("p_xt_mm")
        xt_done = sem("p_xt_done")
        key_mm = sem("p_key_mm")
        key_done = sem("p_key_done")
        stored = [sem(f"p_stored{i}") for i in range(2)]
        block = ctx.enter_context(nc.Block())
        STEPS = 3
        AHEAD = 1 + 2 * SUB
        ROUNDS = NC // SLOTS

        @block.sync
        def _(sp):
            sp.dma_start(wp[:], w_proj.rearrange("(k p) n -> p k n", p=P)).then_inc(consts_in, 16)
            sp.dma_start(wk[:], w_key.rearrange("(k p) n -> p k n", p=P)).then_inc(consts_in, 16)
            sp.dma_start(bp[:], bp_row.partition_broadcast(P)).then_inc(consts_in, 16)
            sp.dma_start(ident[:], eye[:]).then_inc(consts_in, 16)
            sp.dma_start(temp[:], temperature.partition_broadcast(P)).then_inc(consts_in, 16)
            sp.dma_start(bcol[:], bias.partition_broadcast(P)).then_inc(consts_in, 16)
            for counter in stored:
                sp.sem_inc(counter, 1)
            by_chunk = attn.rearrange("(g c) p n -> g c p n", c=NC)
            with sp.Fori(0, B) as b:
                for c in range(NC):
                    i = c % SLOTS
                    cols = slice(c * W, (c + 1) * W)
                    sp.wait_ge(tok_mm, AHEAD + (b * NC + c - SLOTS) * SUB + SUB)
                    for dst, src in ((a_in, by_chunk[bass.ds(b * KT, KT), c]),
                                     (c_in, pe_img[bass.ds(b * KT, KT), :, cols]),
                                     (x_in, x[bass.ds(b, 1), :, cols].rearrange("a (k p) n -> (a k) p n", p=P))):
                        sp.dma_start(dst[:, i], src.rearrange("k p n -> p k n")).then_inc(chunk_in[i], 16)

        @block.gpsimd
        def _(pool):
            nc.gpsimd.memset(ones16[:], 1.0).then_inc(ones_done, 1)
            nc.gpsimd.memset(mhalf[:], -0.5).then_inc(mhalf_done, 1)
            pool.wait_ge(mhalf_done, 1)
            with pool.Fori(0, CHUNKS) as n:
                pool.wait_ge(veps_done, n + 1)
                nc.gpsimd.tensor_tensor(rstd[:], veps[:], mhalf[:], ALU.pow).then_inc(rstd_done, 1)

        @block.vector
        def _(dve):
            dve.sem_inc(tok_done, 1)
            dve.sem_inc(xn_done, 1)
            dve.sem_inc(norm_done, 1)
            dve.wait_ge(consts_in, 6 * 16)

            def add_parts(b, c):
                dve.wait_ge(chunk_in[c % SLOTS], (b * ROUNDS + c // SLOTS + 1) * 3 * 16)
                nc.vector.tensor_tensor(both[:, c % 2], a_in[:, c % SLOTS], c_in[:, c % SLOTS], ALU.add).then_inc(both_done, 1)

            def tokens(b, c, last):
                n, i = b * NC + c, c % 2
                st = Steps(dve, dve_step, n * STEPS)
                token_tiles = [t_sb[:, bass.ds(n * SUB + j, 1)].rearrange("p a n -> p (a n)") for j in range(SUB)]
                for j in range(SUB):
                    dve.wait_ge(tok_mm, AHEAD + n * SUB + j + 1)
                    nc.vector.tensor_tensor(token_tiles[j], ps_t[j][:, 0:CH], bp[:], ALU.add).then_inc(tok_done, 1)
                dve.wait_ge(tok_done, 1 + (n + 1) * SUB)
                nc.vector.memset(veps[:], 0.0)
                for j in range(SUB):
                    step = nc.vector.bn_stats(stats[:, j], token_tiles[j])
                st.then(step)
                nc.vector.memset(veps[:], 0.0)
                for j in range(SUB):
                    step = nc.vector.bn_aggr(mv[:, j], stats[:, j])
                st.then(step)
                nc.vector.tensor_scalar(veps[:], mv[:, :, 1], LN_EPS, None, ALU.add).then_inc(veps_done, 1)
                if not last:
                    add_parts(*((b, c + 1) if c < NC - 1 else (b + 1, 0)))
                dve.wait_ge(rstd_done, n + 1)
                dve.wait_ge(xt_mm, 1 + n * KT)
                dve.wait_ge(stored[i], 1 + (b * (NC // 2) + c // 2) * 3 * 16)
                for j in range(SUB):
                    step = nc.vector.tensor_scalar(xn[:, i, j], token_tiles[j], mv[:, j, 0:1], rstd[:, j:j + 1],
                                                   ALU.subtract, ALU.mult)
                st.then(step)
                dve.sem_inc(xn_done, 1)
                assert st.n == STEPS
                if c:
                    take_norm(n - 1)

            def take_norm(n):
                dve.wait_ge(norm_mm, 1 + n + 1)
                nc.vector.reduce_max(norms[:, bass.ds(n, 1)], ps_n[:, 0:W], AX.X).then_inc(norm_done, 1)

            def tokens_of_batch(b, last):
                for c in range(NC):
                    tokens(b, c, last and c == NC - 1)
                take_norm(b * NC + NC - 1)

            add_parts(0, 0)
            with dve.Fori(0, B - 1) as b:
                tokens_of_batch(b, False)
            tokens_of_batch(B - 1, True)
            st = Steps(dve, dve_step, CHUNKS * STEPS)
            dve.wait_ge(norm_done, 1 + CHUNKS)
            st.then(nc.vector.reduce_max(test[:, 0:1], norms[:], AX.X))
            st.then(nc.vector.tensor_scalar(test[:, 1:2], temp[:], 1e-6, None, ALU.max))
            st.then(nc.vector.reciprocal(test[:, 2:3], test[:, 1:2]))
            st.then(nc.vector.tensor_scalar(test[:, 1:2], test[:, 2:3], -UNDERFLOW, OUTSIDE, ALU.mult, ALU.add))
            st.then(nc.vector.tensor_scalar(test[:, 2:3], bcol[:], -1.0, None, ALU.mult))
            st.then(nc.vector.tensor_tensor(test[:, 3:4], bcol[:], test[:, 2:3], ALU.max))
            st.then(nc.vector.tensor_tensor(test[:, 4:5], test[:, 1:2], test[:, 3:4], ALU.subtract))
            st.then(nc.vector.tensor_scalar(test[:, 4:5], test[:, 4:5], 0.0, None, ALU.max))
            st.then(nc.vector.tensor_tensor(test[:, 5:6], test[:, 4:5], test[:, 4:5], ALU.mult))
            st.then(nc.vector.tensor_scalar(test[:, 0:1], test[:, 0:1], 1.04 * CH, None, ALU.mult))
            st.then(nc.vector.tensor_tensor(near_only[:], test[0:1, 0:1], test[0:1, 5:6], ALU.is_lt))

        @block.scalar
        def _(act):
            act.sem_inc(xt_done, 1)
            act.sem_inc(key_done, 1)
            act.wait_ge(mhalf_done, 1)
            with act.Fori(0, B) as b:
                for c in range(NC):
                    i = c % 2
                    n = b * NC + c
                    cols = slice(c * W, (c + 1) * W)
                    rows = slice(c * W, (c + 1) * W)
                    act.wait_ge(stored[i], 1 + (b * (NC // 2) + c // 2) * 3 * 16)
                    for k in range(KT):
                        act.wait_ge(xt_mm, 1 + n * KT + k + 1)
                        nc.scalar.activation(xt[:, i, k], ps_x[k][:, 0:W], ACT.Identity).then_inc(xt_done, 1)
                    for k in range(KT):
                        act.wait_ge(key_mm, 1 + n * KT + k + 1)
                        if k == 0:
                            act.wait_ge(norm_mm, 1 + n)
                        nc.scalar.activation(squares[:, k], ps_k[k][:, 0:W], ACT.Square).then_inc(squares_done, 1)
                        nc.scalar.activation(key[:, i, k], ps_k[k][:, 0:W], ACT.Identity).then_inc(key_done, 1)
                    act.wait_ge(xn_done, 1 + n + 1)
                    act.dma_start(xn_tok[bass.ds(b, 1), rows].rearrange("a (j p) n -> p (a j) n", p=P), xn[:, i]
                                  ).then_inc(stored[i], 16)
                    act.wait_ge(key_done, 1 + (n + 1) * KT)
                    act.wait_ge(xt_done, 1 + (n + 1) * KT)
                    for dram, src in ((xn_ch, xt), (key_ch, key)):
                        act.dma_start(dram[bass.ds(b * KT, KT), :, cols].rearrange("k p n -> p k n"), src[:, i]
                                      ).then_inc(stored[i], 16)
            for i in range(2):
                act.wait_ge(stored[i], 1 + CHUNKS // 2 * 3 * 16)

        @block.tensor
        def _(pe):
            for counter in (tok_mm, xt_mm, key_mm, norm_mm):
                pe.sem_inc(counter, 1)
            pe.sem_inc(tok_mm, AHEAD - 1)
            pe.wait_ge(consts_in, 6 * 16)
            pe.wait_ge(ones_done, 1)

            def project(b, c):
                n, i, slot = b * NC + c, c % 2, c % SLOTS
                pe.wait_ge(both_done, n + 1)
                pe.wait_ge(chunk_in[slot], (b * ROUNDS + c // SLOTS + 1) * 3 * 16)
                for j in range(SUB):
                    pe.wait_ge(tok_done, 1 + n * SUB)
                    part = slice(j * P, (j + 1) * P)
                    for k in range(KT):
                        nc.tensor.matmul(ps_t[j][:, k * P:(k + 1) * P], x_in[:, slot, k, part], ident[:],
                                         start=(k == 0), stop=False, skip_group_check=True)
                    for k in range(KT):
                        last = nc.tensor.matmul(ps_t[j][:, 0:CH], both[:, i, k, part], wp[:, k, :],
                                                start=False, stop=(k == KT - 1), skip_group_check=True)
                    last.then_inc(tok_mm, 1)

            def transposes(n, i):
                pe.wait_ge(xn_done, 1 + n + 1)
                for k in range(KT):
                    pe.wait_ge(xt_done, 1 + n * KT)
                    for j in range(SUB):
                        last = nc.tensor.transpose(ps_x[k][:, j * P:(j + 1) * P], xn[:, i, j, k * P:(k + 1) * P], ident[:])
                    last.then_inc(xt_mm, 1)

            def key_products(n, i):
                pe.wait_ge(xt_done, 1 + (n + 1) * KT)
                for m in range(KT):
                    pe.wait_ge(key_done, 1 + n * KT)
                    for k in range(KT):
                        last = nc.tensor.matmul(ps_k[m][:, 0:W], wk[:, k, m * P:(m + 1) * P], xt[:, i, k, :],
                                                start=(k == 0), stop=(k == KT - 1))
                    last.then_inc(key_mm, 1)

            def norm_products(n):
                pe.wait_ge(squares_done, (n + 1) * KT)
                pe.wait_ge(norm_done, 1 + n)
                for k in range(KT):
                    last = nc.tensor.matmul(ps_n[:, 0:W], ones16[:], squares[:, k], start=(k == 0), stop=(k == KT - 1))
                last.then_inc(norm_mm, 1)

            def products_of_batch(b, last):
                for c in range(NC):
                    n = b * NC + c
                    if not (last and c == NC - 1):
                        project(*((b, c + 1) if c < NC - 1 else (b + 1, 0)))
                    transposes(n, c % 2)
                    if c:
                        norm_products(n - 1)
                    key_products(n, c % 2)
                norm_products(b * NC + NC - 1)

            project(0, 0)
            with pe.Fori(0, B - 1) as b:
                products_of_batch(b, False)
            products_of_batch(B - 1, True)


def near_attention(nc, xn_tok, xn_ch, key_ch, near_masks, temperature, bias, eye, near_only, t2, t2_stats):
    with ExitStack() as ctx:
        def sb(name, shape, dt=F32):
            return ctx.enter_context(nc.sbuf_tensor(name, shape, dt))

        def sem(name):
            return ctx.enter_context(nc.semaphore(name))

        BEFORE = WINDOW // 2
        SPAN = P + WINDOW
        near = sb("nnear", [P, 3, SUB * SPAN])
        temp = sb("ntemp", [P, 1])
        bcol = sb("nbcol", [P, 1])
        ident = sb("nident", [P, P])
        SLOTS = 3
        keys = sb("nkeys", [P, SLOTS, KT, W])
        xw = sb("nxw", [P, SLOTS, KT, W + WINDOW])
        vw = sb("nvw", [P, SLOTS, SUB + 1, CH])
        logit = sb("nlogit", [P, SUB, SPAN])
        prob = sb("nprob", [P, 2, SUB, SPAN])
        body_t = sb("nbody_t", [P, W])
        tail_t = sb("ntail_t", [WINDOW, W])
        mx = sb("nmx", [P, SUB])
        nmx = sb("nnmx", [P, SUB])
        rs = sb("nrs", [P, 2, SUB])
        rrs = sb("nrrs", [P, SUB])
        ps_l = [ctx.enter_context(nc.psum_tensor(f"npl{i}", [P, 512], F32)) for i in range(2)]
        ps_b = ctx.enter_context(nc.psum_tensor("npb", [P, 512], F32))
        ps_t = ctx.enter_context(nc.psum_tensor("npt", [P, 512], F32))
        ps_o = [ctx.enter_context(nc.psum_tensor(f"npo{i}", [P, 2, 512], F32)) for i in range(2)]

        consts_in = sem("n_consts_in")
        masks_done = sem("n_masks_done")
        chunk_in = [sem(f"n_chunk_in{i}") for i in range(SLOTS)]
        logit_mm = sem("n_logit_mm")
        relu_done = sem("n_relu_done")
        nmx_done = sem("n_nmx_done")
        exp_done = sem("n_exp_done")
        probt_mm = sem("n_probt_mm")
        probt_done = sem("n_probt_done")
        out_mm = sem("n_out_mm")
        t2_done = sem("n_t2_done")
        dve_step = sem("n_dve_step")
        block = ctx.enter_context(nc.Block())
        LOADS = [0] * SLOTS
        upto = []
        for c in range(NC):
            LOADS[c % SLOTS] += {0: 7, NC - 1: 6}.get(c, 4)
            upto.append(LOADS[c % SLOTS])

        AHEAD = 1 + (SLOTS - 1) * SUB

        def kind(c):
            return {0: 0, NC - 1: 2}.get(c, 1)

        @block.sync
        def _(sp):
            for dst, src in ((near[:], near_masks.rearrange("k p n -> p k n")),
                             (temp[:], temperature.partition_broadcast(P)), (bcol[:], bias.partition_broadcast(P)),
                             (ident[:], eye[:])):
                sp.dma_start(dst, src).then_inc(consts_in, 16)

            def load_chunk(b, c):
                i = c % SLOTS
                start = c * W - BEFORE
                loads = 0

                def load(dst, src):
                    nonlocal loads
                    loads += 1
                    sp.dma_start(dst, src).then_inc(chunk_in[i], 16)

                def channels(to, first, count):
                    load(xw[:, i, :, to:to + count],
                         xn_ch[bass.ds(b * KT, KT), :, first:first + count].rearrange("k p n -> p k n"))

                def value_tiles(tile, count, first):
                    load(vw[:, i, tile:tile + count],
                         xn_tok[bass.ds(b, 1), first:first + count * P].rearrange("a (t p) n -> p (a t) n", p=P))

                def value_rows(tile, row, count, first):
                    load(vw[row:row + count, i, tile], xn_tok[bass.ds(b, 1), first:first + count].rearrange("a p n -> p (a n)"))

                if c == 0:
                    channels(0, 0, BEFORE)
                    channels(BEFORE, 0, W + WINDOW - BEFORE)
                    value_rows(0, 0, BEFORE, 0)
                    value_rows(0, BEFORE, P - BEFORE, 0)
                    value_tiles(1, SUB - 1, P - BEFORE)
                    value_rows(SUB, 0, WINDOW, start + W)
                elif c == NC - 1:
                    channels(0, start, W + BEFORE)
                    channels(W + BEFORE, N - BEFORE, WINDOW - BEFORE)
                    value_tiles(0, SUB, start)
                    value_rows(SUB, 0, BEFORE, start + W)
                    value_rows(SUB, BEFORE, WINDOW - BEFORE, N - (WINDOW - BEFORE))
                else:
                    channels(0, start, W + WINDOW)
                    value_tiles(0, SUB, start)
                    value_rows(SUB, 0, WINDOW, start + W)
                load(keys[:, i], key_ch[bass.ds(b * KT, KT), :, c * W:(c + 1) * W].rearrange("k p n -> p k n"))
                assert loads == upto[c] - (upto[c - SLOTS] if c >= SLOTS else 0)

            fast = sp.value_load(near_only[0:1, 0:1], min_val=0, max_val=1)
            with sp.If(fast):
                with sp.Fori(0, B) as b:
                    for c in range(NC):
                        sp.wait_ge(t2_done, 1 + (b * NC + c) * SUB)
                        load_chunk(b, c)

        @block.scalar
        def _(act):
            for counter in (relu_done, exp_done, probt_done):
                act.sem_inc(counter, 1)
            act.sem_inc(relu_done, 1)
            act.wait_ge(consts_in, 4 * 16)
            fast = act.value_load(near_only[0:1, 0:1], min_val=0, max_val=1)
            with act.If(fast):
                with act.Fori(0, B) as b:
                    for s in range(NC + 1):
                        if s < NC:
                            n = b * NC + s
                            act.wait_ge(exp_done, 1 + n * SUB)
                            act.wait_ge(logit_mm, 1 + n + 1)
                            nc.scalar.activation(logit[:].rearrange("p j n -> p (j n)"), ps_l[s % 2][:, 0:SUB * SPAN], ACT.Relu,
                                                 bias=bcol[:]).then_inc(relu_done, 1)
                        if s > 0:
                            n = b * NC + s - 1
                            act.wait_ge(out_mm, 1 + n)
                            act.wait_ge(probt_mm, 1 + n * 2 + 1)
                            nc.scalar.activation(body_t[:], ps_b[:, 0:W], ACT.Identity).then_inc(probt_done, 1)
                            act.wait_ge(probt_mm, 1 + n * 2 + 2)
                            nc.scalar.activation(tail_t[:], ps_t[0:WINDOW, 0:W], ACT.Identity).then_inc(probt_done, 1)
                        if s < NC:
                            n = b * NC + s
                            act.wait_ge(nmx_done, n + 1)
                            act.wait_ge(probt_mm, 1 + n * 2)
                            for j in range(SUB):
                                nc.scalar.activation(prob[:, s % 2, j], logit[:, j], ACT.Exp, bias=nmx[:, j:j + 1],
                                                     accum_out=rs[:, s % 2, j:j + 1]).then_inc(exp_done, 1)

        @block.vector
        def _(dve):
            dve.sem_inc(t2_done, AHEAD)
            dve.wait_ge(consts_in, 4 * 16)
            nc.vector.tensor_scalar(near[:], near[:], temp[:], None, ALU.mult).then_inc(masks_done, 1)
            dve.wait_ge(masks_done, 1)
            fast = dve.value_load(near_only[0:1, 0:1], min_val=0, max_val=1)
            STEPS = 3 * NC
            with dve.If(fast):
                with dve.Fori(0, B) as b:
                    st = Steps(dve, dve_step, b * STEPS)
                    for s in range(NC + 1):
                        if s < NC:
                            n = b * NC + s
                            dve.wait_ge(relu_done, 2 + n + 1)
                            flat = logit[:].rearrange("p j n -> p (j n)")
                            st.then(nc.vector.scalar_tensor_tensor(out=flat, in0=flat, scalar=temp[:], in1=near[:, kind(s)],
                                                                   op0=ALU.mult, op1=ALU.add))
                            st.then(nc.vector.reduce_max(mx[:], logit[:], AX.X))
                            dve.wait_ge(exp_done, 1 + n * SUB)
                            nc.vector.tensor_scalar(nmx[:], mx[:], -1.0, None, ALU.mult).then_inc(nmx_done, 1)
                        if s > 0:
                            n = b * NC + s - 1
                            i = (s - 1) % 2
                            dve.wait_ge(exp_done, 1 + (n + 1) * SUB)
                            dve.wait_ge(t2_done, AHEAD + n * SUB)
                            st.then(nc.vector.reciprocal(rrs[:], rs[:, i]))
                            dve.wait_ge(out_mm, 1 + n + 1)
                            for j in range(SUB):
                                token_tile = t2[:, bass.ds(n * SUB + j, 1)].rearrange("p a n -> p (a n)")
                                nc.vector.scalar_tensor_tensor(out=token_tile, in0=ps_o[i][:, j // 2, j % 2 * CH:(j % 2 + 1) * CH],
                                                               scalar=rrs[:, j:j + 1], in1=token_tile,
                                                               op0=ALU.mult, op1=ALU.add).then_inc(t2_done, 1)
                            dve.wait_ge(t2_done, AHEAD + (n + 1) * SUB)
                            for j in range(SUB):
                                tile = bass.ds(n * SUB + j, 1)
                                nc.vector.bn_stats(t2_stats[:, tile].rearrange("p a n -> p (a n)"),
                                                   t2[:, tile].rearrange("p a n -> p (a n)"))
                    assert st.n == STEPS

        @block.tensor
        def _(pe):
            for counter in (logit_mm, probt_mm, out_mm):
                pe.sem_inc(counter, 1)
            pe.wait_ge(consts_in, 4 * 16)
            fast = pe.value_load(near_only[0:1, 0:1], min_val=0, max_val=1)
            with pe.If(fast):
                with pe.Fori(0, B) as b:
                    for s in range(NC + 1):
                        if s < NC:
                            n, i, slot = b * NC + s, s % 2, s % SLOTS
                            pe.wait_ge(chunk_in[slot], (b * LOADS[slot] + upto[s]) * 16)
                            pe.wait_ge(relu_done, 1 + n)
                            for j in range(SUB):
                                for k in range(KT):
                                    last = nc.tensor.matmul(ps_l[i][:, j * SPAN:(j + 1) * SPAN], keys[:, slot, k, j * P:(j + 1) * P],
                                                            xw[:, slot, k, j * P:j * P + SPAN], start=(k == 0), stop=(k == KT - 1))
                            last.then_inc(logit_mm, 1)
                        if s > 0:
                            n, i, slot = b * NC + s - 1, (s - 1) % 2, (s - 1) % SLOTS
                            pe.wait_ge(exp_done, 1 + n * SUB + SUB)
                            pe.wait_ge(probt_done, 1 + n * 2)
                            for j in range(SUB):
                                last = nc.tensor.transpose(ps_b[:, j * P:(j + 1) * P], prob[:, i, j, 0:P], ident[:])
                            last.then_inc(probt_mm, 1)
                            for j in range(SUB):
                                last = nc.tensor.transpose(ps_t[0:WINDOW, j * P:(j + 1) * P], prob[:, i, j, P:SPAN], ident[:])
                            last.then_inc(probt_mm, 1)
                            pe.wait_ge(probt_done, 1 + n * 2 + 2)
                            pe.wait_ge(t2_done, AHEAD - SUB + n * SUB)
                            for j in range(SUB):
                                to = ps_o[i][:, j // 2, j % 2 * CH:(j % 2 + 1) * CH]
                                part = slice(j * P, (j + 1) * P)
                                nc.tensor.matmul(to, body_t[:, part], vw[:, slot, j], start=True, stop=False)
                                last = nc.tensor.matmul(to, tail_t[:, part], vw[0:WINDOW, slot, j + 1], start=False, stop=True)
                            last.then_inc(out_mm, 1)


def dense_attention(nc, xn_tok, xn_ch, key_ch, wide_mask, temperature, bias, eye, near_only, t2, t2_stats):
    with ExitStack() as ctx:
        def sb(name, shape, dt=F32):
            return ctx.enter_context(nc.sbuf_tensor(name, shape, dt))

        def sem(name):
            return ctx.enter_context(nc.semaphore(name))

        wide = sb("dwide", [P, (2 * NT - 1) * P])
        temp = sb("dtemp", [P, 1])
        bcol = sb("dbcol", [P, 1])
        ident = sb("dident", [P, P])
        keys = sb("dkeys", [P, KT, P])
        xw = sb("dxw", [P, KT, N])
        vw = sb("dvw", [P, NT, CH])
        logit = sb("dlogit", [P, NC, W])
        probt = sb("dprobt", [P, NC, W])
        mx = sb("dmx", [P, 1])
        nmx = sb("dnmx", [P, 1])
        rs = sb("drs", [P, 1])
        rrs = sb("drrs", [P, 1])
        ps_l = [ctx.enter_context(nc.psum_tensor(f"dpl{i}", [P, 512], F32)) for i in range(NC)]
        ps_p = ctx.enter_context(nc.psum_tensor("dpp", [P, 512], F32))
        ps_o = ctx.enter_context(nc.psum_tensor("dpo", [P, 512], F32))

        consts_in = sem("d_consts_in")
        masks_done = sem("d_masks_done")
        batch_in = sem("d_batch_in")
        tile_in = sem("d_tile_in")
        logit_mm = sem("d_logit_mm")
        relu_done = sem("d_relu_done")
        nmx_done = sem("d_nmx_done")
        exp_done = sem("d_exp_done")
        probt_mm = sem("d_probt_mm")
        probt_done = sem("d_probt_done")
        out_mm = sem("d_out_mm")
        t2_done = sem("d_t2_done")
        dve_step = sem("d_dve_step")
        block = ctx.enter_context(nc.Block())

        @block.sync
        def _(sp):
            for dst, src in ((wide[:], wide_mask[:]), (temp[:], temperature.partition_broadcast(P)),
                             (bcol[:], bias.partition_broadcast(P)), (ident[:], eye[:])):
                sp.dma_start(dst, src).then_inc(consts_in, 16)
            near = sp.value_load(near_only[0:1, 0:1], min_val=0, max_val=1)
            with sp.If(1 - near):
                with sp.Fori(0, B) as b:
                    sp.wait_ge(t2_done, 1 + b * NT)
                    sp.dma_start(xw[:], xn_ch[bass.ds(b * KT, KT)].rearrange("k p n -> p k n")).then_inc(batch_in, 16)
                    sp.dma_start(vw[:], xn_tok[bass.ds(b, 1)].rearrange("a (t p) n -> p (a t) n", p=P)).then_inc(batch_in, 16)
                    with sp.Fori(0, NT) as t:
                        sp.wait_ge(t2_done, 1 + b * NT + t)
                        sp.dma_start(keys[:], key_ch[bass.ds(b * KT, KT), :, bass.ds(t * P, P)].rearrange("k p n -> p k n")
                                     ).then_inc(tile_in, 16)

        @block.scalar
        def _(act):
            act.wait_ge(consts_in, 4 * 16)
            near = act.value_load(near_only[0:1, 0:1], min_val=0, max_val=1)
            with act.If(1 - near):
                with act.Fori(0, TT) as n:
                    for c in range(NC):
                        act.wait_ge(logit_mm, n * NC + c + 1)
                        nc.scalar.activation(logit[:, c], ps_l[c][:, 0:W], ACT.Relu, bias=bcol[:]).then_inc(relu_done, 1)
                    act.wait_ge(nmx_done, n + 1)
                    nc.scalar.activation(logit[:], logit[:], ACT.Exp, bias=nmx[:], accum_out=rs[:]).then_inc(exp_done, 1)
                    for c in range(NC):
                        act.wait_ge(probt_mm, n * NC + c + 1)
                        nc.scalar.activation(probt[:, c], ps_p[:, 0:W], ACT.Identity).then_inc(probt_done, 1)

        @block.vector
        def _(dve):
            dve.sem_inc(t2_done, 1)
            dve.wait_ge(consts_in, 4 * 16)
            nc.vector.tensor_scalar(wide[:], wide[:], temp[:], None, ALU.mult).then_inc(masks_done, 1)
            dve.wait_ge(masks_done, 1)
            near = dve.value_load(near_only[0:1, 0:1], min_val=0, max_val=1)
            STEPS = 3
            with dve.If(1 - near):
                with dve.Fori(0, B) as b:
                    with dve.Fori(0, NT) as t:
                        n = b * NT + t
                        st = Steps(dve, dve_step, n * STEPS)
                        dve.wait_ge(relu_done, (n + 1) * NC)
                        flat = logit[:].rearrange("p c n -> p (c n)")
                        st.then(nc.vector.scalar_tensor_tensor(out=flat, in0=flat, scalar=temp[:],
                                                               in1=wide[:, bass.ds((NT - 1) * P - t * P, N)],
                                                               op0=ALU.mult, op1=ALU.add))
                        st.then(nc.vector.reduce_max(mx[:], flat, AX.X))
                        nc.vector.tensor_scalar(nmx[:], mx[:], -1.0, None, ALU.mult).then_inc(nmx_done, 1)
                        dve.wait_ge(exp_done, n + 1)
                        dve.wait_ge(t2_done, 1 + n)
                        st.then(nc.vector.reciprocal(rrs[:], rs[:]))
                        dve.wait_ge(out_mm, n + 1)
                        nc.vector.scalar_tensor_tensor(out=t2[:, bass.ds(n, 1)].rearrange("p a n -> p (a n)"), in0=ps_o[:, 0:CH],
                                                       scalar=rrs[:], in1=t2[:, bass.ds(n, 1)].rearrange("p a n -> p (a n)"),
                                                       op0=ALU.mult, op1=ALU.add).then_inc(t2_done, 1)
                        dve.wait_ge(t2_done, 1 + n + 1)
                        nc.vector.bn_stats(t2_stats[:, bass.ds(n, 1)].rearrange("p a n -> p (a n)"),
                                           t2[:, bass.ds(n, 1)].rearrange("p a n -> p (a n)"))

        @block.tensor
        def _(pe):
            pe.wait_ge(consts_in, 4 * 16)
            near = pe.value_load(near_only[0:1, 0:1], min_val=0, max_val=1)
            with pe.If(1 - near):
                with pe.Fori(0, B) as b:
                    with pe.Fori(0, NT) as t:
                        n = b * NT + t
                        pe.wait_ge(batch_in, (b + 1) * 2 * 16)
                        pe.wait_ge(tile_in, (n + 1) * 16)
                        for c in range(NC):
                            for k in range(KT):
                                last = nc.tensor.matmul(ps_l[c][:, 0:W], keys[:, k], xw[:, k, c * W:(c + 1) * W],
                                                        start=(k == 0), stop=(k == KT - 1))
                            last.then_inc(logit_mm, 1)
                        pe.wait_ge(exp_done, n + 1)
                        for c in range(NC):
                            if c:
                                pe.wait_ge(probt_done, n * NC + c)
                            for a in range(SUB):
                                last = nc.tensor.transpose(ps_p[:, a * P:(a + 1) * P], logit[:, c, a * P:(a + 1) * P], ident[:])
                            last.then_inc(probt_mm, 1)
                        pe.wait_ge(probt_done, (n + 1) * NC)
                        for c in range(NC):
                            for a in range(SUB):
                                last = nc.tensor.matmul(ps_o[:, 0:CH], probt[:, c, a * P:(a + 1) * P], vw[:, c * SUB + a],
                                                        start=(c + a == 0), stop=(c * SUB + a == NT - 1))
                        last.then_inc(out_mm, 1)


def norm_and_gate(nc, t2, t2_stats, gate_w, gate_b_row, eye, xn2, gate_logits, slots_used, slots):
    with ExitStack() as ctx:
        def sb(name, shape, dt=F32):
            return ctx.enter_context(nc.sbuf_tensor(name, shape, dt))

        def sem(name):
            return ctx.enter_context(nc.semaphore(name))

        E = gate_w.shape[1]
        CHUNKS = TT // SUB
        FILLS = 18
        ident = sb("gident", [P, P])
        gw = sb("ggw", [P, KT, E])
        gb = sb("ggb", [P, E])
        mv = sb("gmv", [P, TT, BN2])
        veps = sb("gveps", [P, TT])
        rstd = sb("grstd", [P, TT])
        mhalf = sb("gmhalf", [P, TT])
        zeros = sb("gzeros", [P, slots_used // P * CH // FILLS])
        xn = sb("gxn", [P, 2, SUB, CH])
        xt = sb("gxt", [P, 2, KT, W])
        ps_x = [[ctx.enter_context(nc.psum_tensor(f"gpx{i}{k}", [P, 512], F32)) for k in range(KT)] for i in range(2)]
        ps_g = [ctx.enter_context(nc.psum_tensor(f"gpg{i}", [P, 512], F32)) for i in range(2)]

        consts_in = sem("g_consts_in")
        mhalf_done = sem("g_mhalf_done")
        zeros_set = sem("g_zeros_set")
        zeroed = sem("g_zeroed")
        veps_done = sem("g_veps_done")
        rstd_done = sem("g_rstd_done")
        dve_step = sem("g_dve_step")
        xn_done = sem("g_xn_done")
        xt_mm = sem("g_xt_mm")
        xt_done = sem("g_xt_done")
        gate_mm = sem("g_gate_mm")
        gate_done = sem("g_gate_done")
        block = ctx.enter_context(nc.Block())

        PAIRS = (CHUNKS - 2) // 2

        @block.sync
        def _(sp):
            for dst, src in ((ident[:], eye[:]), (gw[:], gate_w.rearrange("(k p) e -> p k e", p=P)),
                             (gb[:], gate_b_row.partition_broadcast(P))):
                sp.dma_start(dst, src).then_inc(consts_in, 16)
            sp.wait_ge(zeros_set, 1)
            rows = slots_used // FILLS
            for a in range(FILLS):
                sp.dma_start(slots[a * rows:(a + 1) * rows].rearrange("(p r) n -> p (r n)", p=P), zeros[:]).then_inc(zeroed, 16)
            sp.wait_ge(zeroed, FILLS * 16)

        @block.gpsimd
        def _(pool):
            nc.gpsimd.memset(zeros[:], 0.0).then_inc(zeros_set, 1)
            nc.gpsimd.memset(mhalf[:], -0.5).then_inc(mhalf_done, 1)
            pool.wait_ge(mhalf_done, 1)
            pool.wait_ge(veps_done, 1)
            with pool.Fori(0, CHUNKS) as n:
                tiles = bass.ds(n * SUB, SUB)
                nc.gpsimd.tensor_tensor(rstd[:, tiles], veps[:, tiles], mhalf[:, 0:SUB], ALU.pow).then_inc(rstd_done, 1)

        @block.vector
        def _(dve):
            dve.sem_inc(gate_done, 2)
            st = Steps(dve, dve_step)
            nc.vector.memset(veps[:, 0:1], 0.0)
            for n in range(TT):
                last = nc.vector.bn_aggr(mv[:, n], t2_stats[:, n])
            st.then(last)
            nc.vector.tensor_scalar(veps[:], mv[:, :, 1], LN_EPS, None, ALU.add).then_inc(veps_done, 1)
            dve.wait_ge(consts_in, 3 * 16)

            def normalise(n, i):
                dve.wait_ge(rstd_done, n + 1)
                dve.wait_ge(xt_mm, 1 + n * KT)
                for j in range(SUB):
                    at = bass.ds(n * SUB + j, 1)
                    token_tile = t2[:, at].rearrange("p a n -> p (a n)")
                    mean, scale = mv[:, at, 0:1].rearrange("p a n -> p (a n)"), rstd[:, at]
                    nc.vector.tensor_scalar(xn[:, i, j], token_tile, mean, scale, ALU.subtract, ALU.mult).then_inc(xn_done, 1)
                for j in range(SUB):
                    at = bass.ds(n * SUB + j, 1)
                    token_tile = t2[:, at].rearrange("p a n -> p (a n)")
                    mean, scale = mv[:, at, 0:1].rearrange("p a n -> p (a n)"), rstd[:, at]
                    nc.vector.tensor_scalar(xn2[:, at].rearrange("p a n -> p (a n)"), token_tile, mean, scale,
                                            ALU.subtract, ALU.mult)

            def add_bias(n, i):
                dve.wait_ge(gate_mm, n + 1)
                for j in range(SUB):
                    last = nc.vector.tensor_tensor(gate_logits[:, :, bass.ds(n * SUB + j, 1)].rearrange("p e a -> p (e a)"),
                                                   ps_g[i][:, j * E:(j + 1) * E], gb[:], ALU.add)
                last.then_inc(gate_done, 1)

            normalise(0, 0)
            normalise(1, 1)
            with dve.Fori(0, PAIRS) as pair:
                for i in range(2):
                    normalise(pair * 2 + i + 2, i)
                    add_bias(pair * 2 + i, i)
            add_bias(CHUNKS - 2, 0)
            add_bias(CHUNKS - 1, 1)

        @block.scalar
        def _(act):
            act.sem_inc(xt_done, 1 + KT)
            with act.Fori(0, CHUNKS // 2) as pair:
                for i in range(2):
                    n = pair * 2 + i
                    for k in range(KT):
                        act.wait_ge(xt_mm, 1 + KT + n * KT + k + 1)
                        nc.scalar.activation(xt[:, i, k], ps_x[i][k][:, 0:W], ACT.Identity).then_inc(xt_done, 1)

        @block.tensor
        def _(pe):
            pe.sem_inc(xt_mm, 1 + KT)
            pe.wait_ge(consts_in, 3 * 16)

            def transposes(n, i):
                pe.wait_ge(xn_done, (n + 1) * SUB)
                pe.wait_ge(xt_done, 1 + n * KT)
                for k in range(KT):
                    for j in range(SUB):
                        last = nc.tensor.transpose(ps_x[i][k][:, j * P:(j + 1) * P], xn[:, i, j, k * P:(k + 1) * P], ident[:])
                    last.then_inc(xt_mm, 1)

            def gate_products(n, i):
                pe.wait_ge(xt_done, 1 + KT + (n + 1) * KT)
                pe.wait_ge(gate_done, 1 + n)
                for j in range(SUB):
                    for k in range(KT):
                        last = nc.tensor.matmul(ps_g[i][:, j * E:(j + 1) * E], xt[:, i, k, j * P:(j + 1) * P], gw[:, k],
                                                start=(k == 0), stop=(k == KT - 1))
                last.then_inc(gate_mm, 1)

            transposes(0, 0)
            with pe.Fori(0, PAIRS) as pair:
                for i in (1, 2):
                    transposes(pair * 2 + i, i % 2)
                    gate_products(pair * 2 + i - 1, (i - 1) % 2)
            transposes(CHUNKS - 1, 1)
            gate_products(CHUNKS - 2, 0)
            gate_products(CHUNKS - 1, 1)


def route(nc, gate_logits, capacity, rank, base, trash_place, prefix, to_slot, from_slot, weight):
    with ExitStack() as ctx:
        E = gate_logits.shape[1]

        def sb(name, shape, dt=F32):
            return ctx.enter_context(nc.sbuf_tensor(name, shape, dt))

        def sem(name):
            return ctx.enter_context(nc.semaphore(name))

        HALF = E // 2
        rk = sb("rrank", [P, E, TT])
        bs = sb("rbase", [P, E, TT])
        trash = sb("rtrash", [P, TT])
        tri = sb("rtri", [P, P])
        ones = sb("rones", [P, P])
        zeros = sb("rzeros", [P, TT])
        best = sb("rbest", [P, TT])
        prob = sb("rprob", [P, E, TT])
        total = sb("rtotal", [P, TT])
        inv = sb("rinv", [P, TT])
        top = sb("rtop", [P, TT])
        hot = sb("rhot", [P, E, TT])
        pick = sb("rpick", [P, TT])
        count = sb("rcount", [P, E, TT])
        scan = sb("rscan", [P, E, TT])
        place = sb("rplace", [P, E, TT])
        pos = sb("rpos", [P, TT])
        off = sb("roff", [P, TT])
        kept = sb("rkept", [P, TT])
        tmp = sb("rtmp", [P, TT])
        ps_c = [ctx.enter_context(nc.psum_tensor(f"rpc{i}", [P, 512], F32)) for i in range(2)]
        ps_t = [ctx.enter_context(nc.psum_tensor(f"rpt{i}", [P, 512], F32)) for i in range(2)]

        consts_in = sem("r_consts_in")
        ones_done = sem("r_ones_done")
        dve_step = sem("r_dve_step")
        exp_done = sem("r_exp_done")
        hot_done = sem("r_hot_done")
        counts_mm = sem("r_counts_mm")
        block = ctx.enter_context(nc.Block())

        def over_experts(t):
            return t[:].rearrange("p e t -> p t e")

        def to_experts(t):
            return t[:].rearrange("p (a t) -> p a t", a=1).to_broadcast([P, E, TT])

        @block.sync
        def _(sp):
            for dst, src in ((rk[:], rank[:]), (bs[:], base[:]), (trash[:], trash_place[:]), (tri[:], prefix[:])):
                sp.dma_start(dst, src).then_inc(consts_in, 16)

        @block.gpsimd
        def _(pool):
            nc.gpsimd.memset(zeros[:], 0.0).then_inc(ones_done, 1)
            nc.gpsimd.memset(ones[:], 1.0).then_inc(ones_done, 1)

        @block.scalar
        def _(act):
            act.wait_ge(dve_step, 2)
            nc.scalar.activation(prob[:], gate_logits[:], ACT.Exp).then_inc(exp_done, 1)

        @block.tensor
        def _(pe):
            pe.wait_ge(consts_in, 4 * 16)
            pe.wait_ge(ones_done, 2)
            pe.wait_ge(hot_done, 1)
            for i in range(2):
                half = hot[:, i * HALF:(i + 1) * HALF].rearrange("p e t -> p (e t)")
                nc.tensor.matmul(ps_c[i][:, 0:HALF * TT], tri[:], half, start=True, stop=True)
                last = nc.tensor.matmul(ps_t[i][:, 0:HALF * TT], ones[:], half, start=True, stop=True)
            last.then_inc(counts_mm, 1)

        @block.vector
        def _(dve):
            st = Steps(dve, dve_step)
            tt, ts = nc.vector.tensor_tensor, nc.vector.tensor_scalar
            st.then(nc.vector.reduce_max(best[:], over_experts(gate_logits), AX.X))
            st.then(tt(gate_logits[:], gate_logits[:], to_experts(best), ALU.subtract))
            dve.wait_ge(exp_done, 1)
            st.then(nc.vector.reduce_sum(total[:], over_experts(prob), AX.X))
            st.then(nc.vector.reciprocal(inv[:], total[:]))
            st.then(tt(prob[:], prob[:], to_experts(inv), ALU.mult))
            st.then(nc.vector.reduce_max(top[:], over_experts(prob), AX.X))
            st.then(tt(hot[:], prob[:], to_experts(top), ALU.is_equal))
            dve.wait_ge(consts_in, 4 * 16)
            st.then(tt(hot[:], hot[:], rk[:], ALU.mult))
            st.then(nc.vector.reduce_max(pick[:], over_experts(hot), AX.X))
            st.then(tt(count[:], rk[:], to_experts(pick), ALU.is_equal))
            nc.vector.tensor_copy(hot[:], count[:]).then_inc(hot_done, 1)
            dve.wait_ge(counts_mm, 1)
            dve.wait_ge(ones_done, 2)
            for i in range(2):
                es = slice(i * HALF, (i + 1) * HALF)
                last = nc.vector.tensor_copy(count[:, es].rearrange("p e t -> p (e t)"), ps_t[i][:, 0:HALF * TT])
            st.then(last)
            for e in range(E):
                last = nc.vector.tensor_tensor_scan(scan[:, e], count[:, e], zeros[:], initial=0.0, op0=ALU.add, op1=ALU.add)
            st.then(last)
            st.then(tt(scan[:], scan[:], count[:], ALU.subtract))
            for i in range(2):
                es = slice(i * HALF, (i + 1) * HALF)
                last = tt(place[:, es].rearrange("p e t -> p (e t)"), ps_c[i][:, 0:HALF * TT],
                          scan[:, es].rearrange("p e t -> p (e t)"), ALU.add)
            st.then(last)
            st.then(tt(place[:], place[:], hot[:], ALU.mult))
            st.then(nc.vector.reduce_sum(pos[:], over_experts(place), AX.X))
            st.then(ts(pos[:], pos[:], -1.0, None, ALU.add))
            st.then(tt(hot[:], hot[:], bs[:], ALU.mult))
            st.then(nc.vector.reduce_sum(off[:], over_experts(hot), AX.X))
            st.then(ts(kept[:], pos[:], float(capacity), None, ALU.is_lt))
            st.then(tt(weight[:], top[:], kept[:], ALU.mult))
            st.then(ts(tmp[:], pos[:], float(capacity - 1), None, ALU.min))
            st.then(tt(tmp[:], tmp[:], off[:], ALU.add))
            st.then(nc.vector.tensor_copy(from_slot[:], tmp[:]))
            st.then(tt(pos[:], pos[:], off[:], ALU.add))
            st.then(tt(pos[:], pos[:], trash[:], ALU.subtract))
            st.then(tt(pos[:], pos[:], kept[:], ALU.mult))
            st.then(tt(pos[:], pos[:], trash[:], ALU.add))
            st.then(nc.vector.tensor_copy(to_slot[:], pos[:]))


def scatter_tokens(nc, xn2, to_slot, slots):
    with ExitStack() as ctx:
        scattered = ctx.enter_context(nc.semaphore("s_scattered"))
        block = ctx.enter_context(nc.Block())

        @block.gpsimd
        def _(pool):
            for n in range(TT):
                pool.indirect_dma_start(slots[:], bass.IndirectOffsetOnAxis(ap=to_slot[:, n:n + 1], axis=0), xn2[:, n], None
                                        ).then_inc(scattered, 16)
            pool.wait_ge(scattered, TT * 16)


def experts(nc, slots, w1, b1_cols, w2, b2, eye, capacity, results, weight, all_finite):
    with ExitStack() as ctx:
        def sb(name, shape, dt=F32):
            return ctx.enter_context(nc.sbuf_tensor(name, shape, dt))

        def sem(name):
            return ctx.enter_context(nc.semaphore(name))

        E, _, F = w1.shape
        FT = F // P
        RT = 3
        S = 4
        R = capacity // (RT * S)
        RW = S * R
        TILES = E * RT
        HI, LO = 0, 1
        PARTS = ((HI, HI), (HI, LO), (LO, HI))
        w1_in_sb = sb("ew1_in", [P, KT, F])
        w2_in_sb = sb("ew2_in", [P, FT, CH])
        w1_sb = sb("ew1", [P, 2, KT, F], F32R)
        w2_sb = sb("ew2", [P, 2, FT, CH], F32R)
        b1_sb = sb("eb1", [P, 2, FT])
        b2_sb = sb("eb2", [P, 2, CH])
        ident = sb("eident", [P, P])
        x = sb("ex", [R, 2, S, CH])
        xt = sb("ext", [P, 2, KT, RW], F32R)
        relu = sb("erelu", [P, 2, RW])
        hid = sb("ehid", [P, 2, FT, RW], F32R)
        y = sb("ey", [R, 2, S, CH])
        nought = sb("enought", [R, CH])
        noughts = sb("enoughts", [R, TILES * S])
        total = sb("etotal", [R, 1])
        finite = sb("efinite", [R, 1])
        weight_noughts = sb("eweight_noughts", [P, TT])
        weight_total = sb("eweight_total", [P, 1])
        weight_finite = sb("eweight_finite", [P, 1])
        fewest = sb("efewest", [1, 1])
        ps_x = [ctx.enter_context(nc.psum_tensor(f"epx{i}", [P, 512], F32)) for i in range(KT)]
        ps_h = [ctx.enter_context(nc.psum_tensor(f"eph{i}", [P, 512], F32)) for i in range(4)]
        ps_y = [ctx.enter_context(nc.psum_tensor(f"epy{i}", [P, 512], F32)) for i in range(2)]

        consts_in = sem("e_consts_in")
        w1_in = sem("e_w1_in")
        w2_in = sem("e_w2_in")
        w_high = sem("e_w_high")
        w1_split = sem("e_w1_split")
        w2_split = sem("e_w2_split")
        b_in = [sem(f"e_b_in{i}") for i in range(2)]
        x_in = [sem(f"e_x_in{i}") for i in range(2)]
        xt_mm = sem("e_xt_mm")
        xt_high = sem("e_xt_high")
        xt_split = sem("e_xt_split")
        hid_mm = sem("e_hid_mm")
        relu_done = sem("e_relu_done")
        hid_high = sem("e_hid_high")
        hid_split = sem("e_hid_split")
        y_mm = sem("e_y_mm")
        y_done = sem("e_y_done")
        nought_step = sem("e_nought_step")
        finite_done = sem("e_finite_done")
        finite_mm = sem("e_finite_mm")
        stored = [sem(f"e_stored{i}") for i in range(2)]
        block = ctx.enter_context(nc.Block())
        rows = slots[0:E * capacity].rearrange("(n s r) c -> n r s c", s=S, r=R)
        rows_out = results.rearrange("(n s r) c -> n r s c", s=S, r=R)

        def tiles(it):
            for j in range(2 * RT):
                yield j, it * 2 * RT + j, it * 2 + j // RT, j // RT, j % 2

        def each_pair(engine, two_experts):
            with engine.Fori(0, E // 2 - 1) as it:
                two_experts(it, False)
            two_experts(E // 2 - 1, True)

        @block.sync
        def _(sp):
            def load_rows(n, i):
                sp.dma_start(x[:, i], rows[bass.ds(n, 1)].rearrange("a r s c -> r (a s) c")).then_inc(x_in[i], 16)

            def load_weights(expert, e):
                one = bass.ds(expert, 1)
                sp.dma_start(w1_in_sb[:], w1[one].rearrange("a (k p) f -> p (a k) f", p=P)).then_inc(w1_in, 16)
                sp.dma_start(w2_in_sb[:], w2[one].rearrange("a (f p) c -> p (a f) c", p=P)).then_inc(w2_in, 16)
                sp.dma_start(b1_sb[:, e], b1_cols[one].rearrange("a p f -> p (a f)")).then_inc(b_in[e], 16)
                sp.dma_start(b2_sb[:, e], b2[one].rearrange("a c -> (a c)").partition_broadcast(P)).then_inc(b_in[e], 16)

            def two_experts(it, last):
                for j, n, expert, e, i in tiles(it):
                    if not (last and j == 2 * RT - 1):
                        load_rows(n + 1, 1 - i)
                    sp.wait_ge(y_done, 3 + (n + 1) * S)
                    sp.dma_start(rows_out[bass.ds(n, 1)].rearrange("a r s c -> r (a s) c"), y[:, i]).then_inc(stored[i], 16)
                    if j % RT == 0 and not (last and e == 1):
                        sp.wait_ge(w1_split, expert + 1)
                        sp.wait_ge(w2_split, expert + 1)
                        load_weights(expert + 1, 1 - e)

            load_rows(0, 0)
            sp.dma_start(ident[:], eye[:]).then_inc(consts_in, 16)
            load_weights(0, 0)
            each_pair(sp, two_experts)
            for i in range(2):
                sp.wait_ge(stored[i], 1 + TILES // 2 * 16)

        @block.scalar
        def _(act):
            act.sem_inc(relu_done, 4)
            with act.Fori(0, E // 2) as it:
                for j, n, expert, e, i in tiles(it):
                    act.wait_ge(b_in[e], (it + 1) * 2 * 16)
                    for f in range(FT):
                        act.wait_ge(hid_mm, n * FT + f + 1)
                        act.wait_ge(hid_split, n * FT + f + 1)
                        nc.scalar.activation(relu[:, f % 2], ps_h[f % 4][:, 0:RW], ACT.Relu,
                                             bias=b1_sb[:, e, f:f + 1]).then_inc(relu_done, 1)

        @block.vector
        def _(dve):
            dve.sem_inc(y_done, 1 + 2)
            dve.sem_inc(hid_split, 2)
            for counter in stored:
                dve.sem_inc(counter, 1)

            def split(high, low, whole, high_done, count, done):
                nc.vector.tensor_copy(high, whole).then_inc(high_done, 1)
                dve.wait_ge(high_done, count)
                nc.vector.tensor_tensor(low, whole, high.bitcast(F32), ALU.subtract).then_inc(done, 1)

            def split_w1(expert):
                dve.wait_ge(w1_in, (expert + 1) * 16)
                split(w1_sb[:, HI], w1_sb[:, LO], w1_in_sb[:], w_high, expert * 2 + 1, w1_split)

            def split_w2(expert):
                dve.wait_ge(w2_in, (expert + 1) * 16)
                split(w2_sb[:, HI], w2_sb[:, LO], w2_in_sb[:], w_high, expert * 2 + 2, w2_split)

            def split_xt(n):
                dve.wait_ge(xt_mm, n + 1)
                for k in range(KT):
                    split(xt[:, HI, k], xt[:, LO, k], ps_x[k][:, 0:RW], xt_high, n * KT + k + 1, xt_split)

            def two_experts(it, last):
                for j, n, expert, e, i in tiles(it):
                    final = last and j == 2 * RT - 1
                    for f in range(FT):
                        dve.wait_ge(relu_done, 4 + n * FT + f + 1)
                        split(hid[:, HI, f], hid[:, LO, f], relu[:, f % 2], hid_high, n * FT + f + 1, hid_split)
                    if not final:
                        split_xt(n + 1)
                        if j % RT == RT - 1:
                            split_w1(expert + 1)
                    dve.wait_ge(b_in[e], (it + 1) * 2 * 16)
                    dve.wait_ge(stored[i], 1 + (it * RT + j // 2) * 16)
                    st = Steps(dve, nought_step, n * S * 2)
                    for s in range(S):
                        dve.wait_ge(y_mm, 1 + n * S + s + 1)
                        nc.vector.tensor_tensor(y[:, i, s], ps_y[s % 2][0:R, 0:CH], b2_sb[0:R, e], ALU.add).then_inc(y_done, 1)
                        if s == S - 1 and not final and j % RT == RT - 1:
                            split_w2(expert + 1)
                        dve.wait_ge(y_done, 3 + n * S + s + 1)
                        st.then(nc.vector.tensor_scalar(nought[:], y[:, i, s], 0.0, None, ALU.mult))
                        st.then(nc.vector.reduce_sum(noughts[:, bass.ds(n * S + s, 1)], nought[:], AX.X))

            split_xt(0)
            split_w1(0)
            split_w2(0)
            each_pair(dve, two_experts)
            st = Steps(dve, nought_step, TILES * S * 2)
            st.then(nc.vector.reduce_sum(total[:], noughts[:], AX.X))
            nc.vector.tensor_scalar(finite[:], total[:], 0.0, None, ALU.is_equal).then_inc(finite_done, 1)
            st.then(nc.vector.tensor_scalar(weight_noughts[:], weight[:], 0.0, None, ALU.mult))
            st.then(nc.vector.reduce_sum(weight_total[:], weight_noughts[:], AX.X))
            nc.vector.tensor_scalar(weight_finite[:], weight_total[:], 0.0, None, ALU.is_equal).then_inc(finite_done, 1)
            dve.wait_ge(finite_mm, 1)
            st.then(nc.vector.tensor_reduce(fewest[:], ps_x[0][0:1, 0:R + P], AX.X, ALU.min))
            st.then(nc.vector.tensor_copy(all_finite[:], fewest[:]))

        @block.tensor
        def _(pe):
            pe.sem_inc(y_mm, 1)
            pe.wait_ge(consts_in, 16)

            def transposes(n, i, uses):
                pe.wait_ge(x_in[i], uses * 16)
                for k in range(KT):
                    for s in range(S):
                        last = nc.tensor.transpose(ps_x[k][:, s * R:(s + 1) * R], x[:, i, s, k * P:(k + 1) * P], ident[0:R, 0:R])
                last.then_inc(xt_mm, 1)

            def two_experts(it, last):
                for j, n, expert, e, i in tiles(it):
                    pe.wait_ge(xt_split, (n + 1) * KT)
                    pe.wait_ge(w1_split, expert + 1)
                    for f in range(FT):
                        pe.wait_ge(relu_done, n * FT + f + 1)
                        for k in range(KT):
                            for a, b in PARTS:
                                step = nc.tensor.matmul(ps_h[f % 4][:, 0:RW], w1_sb[:, a, k, f * P:(f + 1) * P], xt[:, b, k],
                                                        start=(k == 0 and (a, b) == PARTS[0]),
                                                        stop=(k == KT - 1 and (a, b) == PARTS[-1]))
                        step.then_inc(hid_mm, 1)
                    if not (last and j == 2 * RT - 1):
                        transposes(n + 1, 1 - i, it * RT + (j + 1) // 2 + 1)
                    pe.wait_ge(w2_split, expert + 1)
                    for s in range(S):
                        pe.wait_ge(y_done, 3 + n * S + s - 1)
                        for f in range(FT):
                            if s == 0:
                                pe.wait_ge(hid_split, 2 + n * FT + f + 1)
                            for a, b in PARTS:
                                step = nc.tensor.matmul(ps_y[s % 2][0:R, 0:CH], hid[:, a, f, s * R:(s + 1) * R], w2_sb[:, b, f],
                                                        start=(f == 0 and (a, b) == PARTS[0]),
                                                        stop=(f == FT - 1 and (a, b) == PARTS[-1]))
                        step.then_inc(y_mm, 1)

            transposes(0, 0, 1)
            each_pair(pe, two_experts)
            pe.wait_ge(finite_done, 2)
            nc.tensor.transpose(ps_x[0][0:1, 0:R], finite[:], ident[0:R, 0:R])
            nc.tensor.transpose(ps_x[0][0:1, R:R + P], weight_finite[:], ident[:]).then_inc(finite_mm, 1)


def combine(nc, results, from_slot, weight, t2, eye, all_finite, out):
    with ExitStack() as ctx:
        def sb(name, shape, dt=F32):
            return ctx.enter_context(nc.sbuf_tensor(name, shape, dt))

        def sem(name):
            return ctx.enter_context(nc.semaphore(name))

        FLT_MAX = 3.4028234e38
        NAN_TO_NUM = 10000.0
        SLOTS = 4
        rows = sb("orows", [P, SLOTS, SUB, CH])
        pos = sb("opos", [P, SUB, CH])
        neg = sb("oneg", [P, SUB, CH])
        cap = sb("ocap", [P, 2, SUB, CH])
        tok = sb("otok", [P, 2, SUB, CH])
        img = sb("oimg", [P, 2, KT, W])
        ident = sb("oident", [P, P])
        ps = [[ctx.enter_context(nc.psum_tensor(f"op{i}{k}", [P, 512], F32)) for k in range(KT)] for i in range(2)]
        CHUNKS = B * NC

        consts_in = sem("o_consts_in")
        rows_in = [sem(f"o_rows_in{i}") for i in range(SLOTS)]
        rows_used = sem("o_rows_used")
        dve_step = sem("o_dve_step")
        tok_done = sem("o_tok_done")
        tok_mm = sem("o_tok_mm")
        img_done = sem("o_img_done")
        stored = [sem(f"o_stored{i}") for i in range(2)]
        block = ctx.enter_context(nc.Block())

        @block.sync
        def _(sp):
            sp.dma_start(ident[:], eye[:]).then_inc(consts_in, 16)
            for counter in stored:
                sp.sem_inc(counter, 1)
            with sp.Fori(0, B) as b:
                for c in range(NC):
                    sp.wait_ge(img_done, 1 + KT + (b * NC + c + 1) * KT)
                    sp.dma_start(out[bass.ds(b, 1), :, c * W:(c + 1) * W].rearrange("a (k p) n -> p (a k) n", p=P), img[:, c % 2]
                                 ).then_inc(stored[c % 2], 16)
            for i in range(2):
                sp.wait_ge(stored[i], 1 + CHUNKS // 2 * 16)

        @block.gpsimd
        def _(pool):
            for n in range(CHUNKS):
                if n >= SLOTS:
                    pool.wait_ge(rows_used, n - SLOTS + 1)
                for j in range(SUB):
                    at = n * SUB + j
                    pool.indirect_dma_start(rows[:, n % SLOTS, j], None, results[:],
                                            bass.IndirectOffsetOnAxis(ap=from_slot[:, at:at + 1], axis=0)
                                            ).then_inc(rows_in[n % SLOTS], 16)

        @block.vector
        def _(dve):
            STEPS = 4

            def add_rows(n, turn, slot, i):
                dve.wait_ge(rows_in[slot], (turn + 1) * SUB * 16)
                dve.wait_ge(tok_mm, 1 + n * KT)
                for j in range(SUB):
                    at = bass.ds(n * SUB + j, 1)
                    nc.vector.scalar_tensor_tensor(out=tok[:, i, j], in0=rows[:, slot, j], scalar=weight[:, at],
                                                   in1=t2[:, at].rearrange("p a n -> p (a n)"), op0=ALU.mult, op1=ALU.add
                                                   ).then_inc(tok_done, 1)
                dve.wait_ge(tok_done, (n + 1) * SUB)
                dve.sem_inc(rows_used, 1)

            def add_mended_rows(n, turn, slot, i):
                st = Steps(dve, dve_step, n * STEPS)
                dve.wait_ge(rows_in[slot], (turn + 1) * SUB * 16)
                for j in range(SUB):
                    w = weight[:, bass.ds(n * SUB + j, 1)]
                    nc.vector.tensor_scalar(pos[:, j], rows[:, slot, j], w, 0.0, ALU.mult, ALU.max)
                    last = nc.vector.tensor_scalar(neg[:, j], rows[:, slot, j], w, 0.0, ALU.mult, ALU.min)
                st.then(last)
                dve.sem_inc(rows_used, 1)
                nc.vector.tensor_scalar(cap[:, 0], pos[:], FLT_MAX, FLT_MAX, ALU.is_le, ALU.mult)
                st.then(nc.vector.tensor_scalar(cap[:, 1], neg[:], -FLT_MAX, -FLT_MAX, ALU.is_ge, ALU.mult))
                nc.vector.scalar_tensor_tensor(out=pos[:], in0=cap[:, 0], scalar=NAN_TO_NUM, in1=pos[:],
                                               op0=ALU.max, op1=ALU.min)
                st.then(nc.vector.scalar_tensor_tensor(out=neg[:], in0=cap[:, 1], scalar=-NAN_TO_NUM, in1=neg[:],
                                                       op0=ALU.min, op1=ALU.max))
                st.then(nc.vector.tensor_tensor(pos[:], pos[:], neg[:], ALU.add))
                dve.wait_ge(tok_mm, 1 + n * KT)
                for j in range(SUB):
                    nc.vector.tensor_tensor(tok[:, i, j], pos[:, j], t2[:, bass.ds(n * SUB + j, 1)].rearrange("p a n -> p (a n)"),
                                            ALU.add).then_inc(tok_done, 1)
                dve.wait_ge(tok_done, (n + 1) * SUB)

            def each_chunk(add):
                with dve.Fori(0, CHUNKS // SLOTS) as turn:
                    for slot in range(SLOTS):
                        add(turn * SLOTS + slot, turn, slot, slot % 2)

            fast = dve.value_load(all_finite[0:1, 0:1], min_val=0, max_val=1)
            with dve.If(fast):
                each_chunk(add_rows)
            with dve.Else():
                each_chunk(add_mended_rows)

        @block.scalar
        def _(act):
            act.sem_inc(img_done, 1 + KT)
            with act.Fori(0, CHUNKS // 2) as pair:
                for i in range(2):
                    n = pair * 2 + i
                    act.wait_ge(stored[i], 1 + pair * 16)
                    for k in range(KT):
                        act.wait_ge(tok_mm, 1 + KT + n * KT + k + 1)
                        nc.scalar.activation(img[:, i, k], ps[i][k][:, 0:W], ACT.Identity).then_inc(img_done, 1)

        @block.tensor
        def _(pe):
            pe.sem_inc(tok_mm, 1 + KT)
            pe.wait_ge(consts_in, 16)
            with pe.Fori(0, CHUNKS // 2) as pair:
                for i in range(2):
                    n = pair * 2 + i
                    pe.wait_ge(tok_done, (n + 1) * SUB)
                    for k in range(KT):
                        pe.wait_ge(img_done, 1 + n * KT)
                        for j in range(SUB):
                            last = nc.tensor.transpose(ps[i][k][:, j * P:(j + 1) * P], tok[:, i, j, k * P:(k + 1) * P], ident[:])
                        last.then_inc(tok_mm, 1)


_INS = []


def kernel(**inputs):
    import numpy as _np
    import concourse.bacc as _bacc
    from concourse.bass_utils import run_bass_kernel_spmd as _run

    g = inputs
    w_qk = _np.asarray(g["L0_conv_w_qk"]).reshape(HEADS, 2, HD, CH)
    w_q, w_k = w_qk[:, 0].reshape(CH, CH), w_qk[:, 1].reshape(CH, CH)
    b_qk = _np.asarray(g["L0_conv_b_qk"]).reshape(HEADS, 2, HD)
    b_all = _np.stack([b_qk[:, 0].reshape(CH), b_qk[:, 1].reshape(CH), _np.asarray(g["L0_conv_b_v"])])
    eye = _np.eye(P, dtype=_np.float32)
    arrays = {
        "x": _np.asarray(g["x"]).reshape(B, CH, N),
        "w_qkv": _np.concatenate([w_q.T, w_k.T, _np.asarray(g["L0_conv_w_v"])[:, :, 0, 0].T], axis=1),
        "b_qkv": b_all.reshape(3 * KT, P).T,
        "bv_row": _np.asarray(g["L0_conv_b_v"]),
        "group_mean": _np.kron(_np.eye(P // GN_GROUP, dtype=_np.float32), _np.full((GN_GROUP, GN_GROUP), 1 / GN_GROUP, _np.float32)),
    }
    arrays["w_pe"] = _np.asarray(g["L0_conv_w_pe"]).reshape(CH, 9)
    arrays["b_pe"] = _np.asarray(g["L0_conv_b_pe"]).reshape(KT, P).T
    arrays["w_proj"] = _np.asarray(g["L0_conv_w_proj"])[:, :, 0, 0].T
    arrays["bp_row"] = _np.asarray(g["L0_conv_b_proj"])
    arrays["eye"] = eye
    arrays["head_sum"] = _np.kron(_np.eye(HG, dtype=_np.float32), _np.ones((HD, HD), _np.float32))
    arrays["w_key"] = _np.asarray(g["L1_attn_K"])
    arrays["temperature"] = _np.asarray(g["L1_attn_temperature"])
    arrays["bias"] = _np.asarray(g["L1_attn_bias"])
    ahead = _np.arange(-(NT - 1) * P, NT * P)[None, :] - _np.arange(P)[:, None]
    outside = (ahead < -(WINDOW // 2)) | (ahead >= WINDOW - WINDOW // 2)
    arrays["wide_mask"] = _np.where(outside, _np.float32(-OUTSIDE), _np.float32(0))
    at = (NT - 1) * P - WINDOW // 2
    inner = arrays["wide_mask"][:, at:at + P + WINDOW]
    near_masks = _np.repeat(_np.stack([inner] * SUB, axis=1)[None], 3, axis=0)
    near_masks[0, :, 0, :WINDOW // 2] = near_masks[2, :, SUB - 1, P + WINDOW // 2:] = GONE
    near_masks = near_masks.reshape(3, P, -1)
    arrays["near_masks"] = near_masks
    capacity = -(-T * 5 // (4 * EXPERTS))
    arrays["gate_w"] = _np.asarray(g["L1_ffn_gate_w"])
    arrays["gate_b"] = _np.asarray(g["L1_ffn_gate_b"])
    arrays["w1"] = _np.asarray(g["L1_ffn_w1"])
    arrays["w2"] = _np.asarray(g["L1_ffn_w2"])
    arrays["b1_cols"] = _np.asarray(g["L1_ffn_b1"]).reshape(EXPERTS, -1, P).transpose(0, 2, 1)
    arrays["b2"] = _np.asarray(g["L1_ffn_b2"])
    table = _np.zeros((P, EXPERTS, TT), _np.float32)
    expert = _np.arange(EXPERTS, dtype=_np.float32)[None, :, None]
    arrays["rank"] = table + (EXPERTS - expert)
    arrays["base"] = table + expert * capacity
    arrays["trash_place"] = _np.float32(EXPERTS * capacity) + _np.arange(T, dtype=_np.float32).reshape(TT, P).T
    arrays["prefix"] = _np.triu(_np.ones((P, P), _np.float32))
    nc = _bacc.Bacc("TRN2", target_bir_lowering=False, num_devices=1)
    arrays = {k: _np.ascontiguousarray(v) for k, v in arrays.items()}
    ap = {k: nc.dram_tensor(k, v.shape, mybir.dt.from_np(v.dtype), kind="ExternalInput").ap() for k, v in arrays.items()}
    def scratch(name, shape, dt=F32):
        return nc.dram_tensor(name, shape, dt).ap()
    small_scores = nc.alloc_sbuf_tensor("small_scores", [1, 1], I32)
    qh, ql = (scratch(n, (BG * NC, P, W)) for n in ("qh", "ql"))
    kh, kl, v_img, pe_img, xn_ch, key_ch = (scratch(n, (BG, P, N)) for n in ("kh", "kl", "v_img", "pe_img", "xn_ch", "key_ch"))
    v_tok, xn_tok = (scratch(n, (B, N, CH)) for n in ("v_tok", "xn_tok"))
    attn = scratch("attn", (BG * NC, P, W))
    with nc.sbuf_tensor("k_first", [P, HG, N], F32R) as k_first, nc.sbuf_tensor("v_first", [P, NT, P], F32) as v_first, \
            nc.sbuf_tensor("q_first", [P, HG, W], F32R) as q_first:
        conv_inputs(nc, ap["x"], ap["w_qkv"], ap["b_qkv"], ap["bv_row"], ap["group_mean"], ap["head_sum"], ap["eye"], qh, ql, kh, kl, v_img, v_tok, small_scores,
                    k_first, v_first, q_first)
        conv_attention(nc, k_first, v_first, q_first, qh, ql, kh, kl, v_img, v_tok, ap["w_pe"], ap["b_pe"], ap["eye"], small_scores, attn, pe_img)
    out = nc.dram_tensor("out_0", (B, CH, N), F32, kind="ExternalOutput").ap()
    near_only = nc.alloc_sbuf_tensor("near_only", [1, 1], I32)
    all_finite = nc.alloc_sbuf_tensor("all_finite", [1, 1], I32)
    t2_stats = nc.alloc_sbuf_tensor("t2_stats", [P, TT, BN6], F32)
    t2 = nc.alloc_sbuf_tensor("t2", [P, TT, CH], F32)
    project_and_norm(nc, attn, pe_img, ap["x"], ap["w_proj"], ap["bp_row"], ap["eye"], ap["w_key"], ap["temperature"],
                     ap["bias"], near_only, t2, xn_tok, xn_ch, key_ch)
    near_attention(nc, xn_tok, xn_ch, key_ch, ap["near_masks"], ap["temperature"], ap["bias"], ap["eye"], near_only, t2, t2_stats)
    dense_attention(nc, xn_tok, xn_ch, key_ch, ap["wide_mask"], ap["temperature"], ap["bias"], ap["eye"], near_only, t2, t2_stats)
    gate_logits = nc.alloc_sbuf_tensor("gate_logits", [P, EXPERTS, TT], F32)
    to_slot = nc.alloc_sbuf_tensor("to_slot", [P, TT], U32)
    from_slot = nc.alloc_sbuf_tensor("from_slot", [P, TT], U32)
    weight = nc.alloc_sbuf_tensor("weight", [P, TT], F32)
    slots = scratch("slots", (EXPERTS * capacity + T, CH))
    results = scratch("results", (EXPERTS * capacity, CH))
    with nc.sbuf_tensor("xn2", [P, TT, CH], F32) as xn2:
        norm_and_gate(nc, t2, t2_stats, ap["gate_w"], ap["gate_b"], ap["eye"], xn2, gate_logits, EXPERTS * capacity, slots)
        route(nc, gate_logits, capacity, ap["rank"], ap["base"], ap["trash_place"], ap["prefix"], to_slot, from_slot, weight)
        scatter_tokens(nc, xn2, to_slot, slots)
    experts(nc, slots, ap["w1"], ap["b1_cols"], ap["w2"], ap["b2"], ap["eye"], capacity, results, weight, all_finite)
    combine(nc, results, from_slot, weight, t2, ap["eye"], all_finite, out)
    r = _run(nc, [arrays], core_ids=[0])
    return r.results[0]["out_0"].reshape(B, CH, IMG, IMG)
```
